# Optimizing a Trainium2 kernel written in Bass

```python
import numpy as np
import jax
import jax.numpy as jnp

def _softmax(x, axis=-1):
    return jax.nn.softmax(x, axis=axis)

def _gelu(x):
    return jax.nn.gelu(x, approximate=True)

def _silu(x):
    return jax.nn.silu(x)

def _sigmoid(x):
    return jax.nn.sigmoid(x)

def _layernorm(x, axis=-1, eps=1e-05):
    m = jnp.mean(x, axis=axis, keepdims=True)
    v = jnp.var(x, axis=axis, keepdims=True)
    return (x - m) / jnp.sqrt(v + eps)

def _scatter_add(tgt, idx, src, axis=0):
    return tgt.at[idx].add(src)

def _segment_sum(src, seg, n):
    return jax.ops.segment_sum(src, seg, n)
kernel_name = 'mk_sandwich_d2_jaxref_r4_246f1c'

def setup_inputs(seed: int=0):
    np.random.seed(seed)
    _w = jnp.asarray

    def _L0_attn_setup():
        import math
        import jax, jax.numpy as jnp
        import numpy as np
        D_MODEL = 256
        N_HEADS = 16
        D_K = D_MODEL // N_HEADS
        D_C = 64
        B, S = (2, 512)
        key = jax.random.key(seed)
        ks = jax.random.split(key, 7)
        sd = lambda fan_in: 1.0 / math.sqrt(fan_in)
        return {'x': jax.random.normal(ks[0], (B, S, D_MODEL), dtype=jnp.float32), 'W_dq': jax.random.uniform(ks[1], (D_MODEL, D_C), minval=-sd(D_MODEL), maxval=sd(D_MODEL), dtype=jnp.float32), 'W_uq': jax.random.uniform(ks[2], (D_C, N_HEADS * D_K), minval=-sd(D_C), maxval=sd(D_C), dtype=jnp.float32), 'W_dkv': jax.random.uniform(ks[3], (D_MODEL, D_C), minval=-sd(D_MODEL), maxval=sd(D_MODEL), dtype=jnp.float32), 'W_uk': jax.random.uniform(ks[4], (D_C, N_HEADS * D_K), minval=-sd(D_C), maxval=sd(D_C), dtype=jnp.float32), 'W_uv': jax.random.uniform(ks[5], (D_C, N_HEADS * D_K), minval=-sd(D_C), maxval=sd(D_C), dtype=jnp.float32), 'W_o': jax.random.uniform(ks[6], (N_HEADS * D_K, D_MODEL), minval=-sd(N_HEADS * D_K), maxval=sd(N_HEADS * D_K), dtype=jnp.float32)}
    _L0_attn_in = _L0_attn_setup()

    def _L0_ffn_setup():
        import jax, jax.numpy as jnp
        import numpy as np

        def _bitlinear(x, w_latent):
            scale = jax.lax.stop_gradient(jnp.clip(jnp.mean(jnp.abs(w_latent), axis=1, keepdims=True), 1e-05, None))
            tern = jnp.clip(jnp.round(w_latent / scale), -1.0, 1.0)
            w = w_latent + jax.lax.stop_gradient(tern - w_latent)
            return x @ (w * scale).T
        key = jax.random.key(seed)
        ks = jax.random.split(key, 6)
        dim, hidden, rank = (256, 1024, 16)
        B, S = (4, 1024)
        x = jax.random.normal(ks[0], (B, S, dim), dtype=jnp.float32)
        w_fc = 0.02 * jax.random.normal(ks[1], (hidden, dim), dtype=jnp.float32)
        w_proj = 0.02 * jax.random.normal(ks[2], (dim, hidden), dtype=jnp.float32)
        u = 0.02 * jax.random.normal(ks[3], (hidden, rank), dtype=jnp.float32)
        v = 0.02 * jax.random.normal(ks[4], (rank, dim), dtype=jnp.float32)
        fast_b = jax.random.normal(ks[5], (rank, rank), dtype=jnp.float32)
        gate = jnp.float32(0.05)
        return {'x': x, 'fast_b': fast_b, 'w_fc': w_fc, 'w_proj': w_proj, 'u': u, 'v': v, 'gate': gate}
    _L0_ffn_in = _L0_ffn_setup()

    def _L1_attn_setup():
        import jax, jax.numpy as jnp
        import numpy as np
        HID = 256
        HEADS = 16
        FEAT = 16
        HD = HID // HEADS
        EPS = 1e-05
        LN_EPS = 1e-05
        B, T = (1, 256)
        IU, JU = np.triu_indices(FEAT, 1)

        def _feature_map(x, gamma, beta):
            mu = x.mean(axis=-1, keepdims=True)
            var = ((x - mu) ** 2).mean(axis=-1, keepdims=True)
            xn = (x - mu) / jnp.sqrt(var + LN_EPS) * gamma + beta
            diag = xn * xn
            off = xn[..., IU] * xn[..., JU]
            return jnp.concatenate([diag * FEAT ** (-0.5), off * (2.0 / FEAT) ** 0.5], axis=-1)
        key = jax.random.key(seed)
        ks = jax.random.split(key, 5)
        s = 0.02
        return {'hidden_states': jax.random.normal(ks[0], (B, T, HID), dtype=jnp.float32), 'Wq': jax.random.normal(ks[1], (FEAT * HEADS, HID), dtype=jnp.float32) * s, 'Wk': jax.random.normal(ks[2], (FEAT * HEADS, HID), dtype=jnp.float32) * s, 'Wv': jax.random.normal(ks[3], (HEADS * HD, HID), dtype=jnp.float32) * s, 'Wo': jax.random.normal(ks[4], (HID, HEADS * HD), dtype=jnp.float32) * s, 'gamma': jnp.ones((FEAT,), dtype=jnp.float32), 'beta': jnp.zeros((FEAT,), dtype=jnp.float32)}
    _L1_attn_in = _L1_attn_setup()

    def _L1_ffn_setup():
        import jax, jax.numpy as jnp
        import numpy as np
        LN_EPS = 0.001
        EPS = 1e-05
        QB = 128.0

        def ste_round(x):
            return x + jax.lax.stop_gradient(jnp.round(x) - x)
        key = jax.random.key(seed)
        k1, k2 = jax.random.split(key)
        x = jax.random.normal(k1, (4, 2048, 256), dtype=jnp.float32)
        weight = jax.random.normal(k2, (256, 256), dtype=jnp.float32) * 0.02
        ln_gamma = jnp.ones((256,), dtype=jnp.float32)
        ln_beta = jnp.zeros((256,), dtype=jnp.float32)
        return {'x': x, 'weight': weight, 'ln_gamma': ln_gamma, 'ln_beta': ln_beta}
    _L1_ffn_in = _L1_ffn_setup()
    _d = {'L0_attn_x': _L0_attn_in['x'], 'L0_attn_W_dq': _L0_attn_in['W_dq'], 'L0_attn_W_uq': _L0_attn_in['W_uq'], 'L0_attn_W_dkv': _L0_attn_in['W_dkv'], 'L0_attn_W_uk': _L0_attn_in['W_uk'], 'L0_attn_W_uv': _L0_attn_in['W_uv'], 'L0_attn_W_o': _L0_attn_in['W_o'], 'L0_ffn_fast_b': _L0_ffn_in['fast_b'], 'L0_ffn_w_fc': _L0_ffn_in['w_fc'], 'L0_ffn_w_proj': _L0_ffn_in['w_proj'], 'L0_ffn_u': _L0_ffn_in['u'], 'L0_ffn_v': _L0_ffn_in['v'], 'L0_ffn_gate': _L0_ffn_in['gate'], 'L1_attn_Wq': _L1_attn_in['Wq'], 'L1_attn_Wk': _L1_attn_in['Wk'], 'L1_attn_Wv': _L1_attn_in['Wv'], 'L1_attn_Wo': _L1_attn_in['Wo'], 'L1_attn_gamma': _L1_attn_in['gamma'], 'L1_attn_beta': _L1_attn_in['beta'], 'L1_ffn_weight': _L1_ffn_in['weight'], 'L1_ffn_ln_gamma': _L1_ffn_in['ln_gamma'], 'L1_ffn_ln_beta': _L1_ffn_in['ln_beta']}
    _x0 = _d['L0_attn_x']
    _d['L0_attn_x'] = jax.random.normal(jax.random.fold_in(jax.random.key(seed), 1), (8, 1024, 256), dtype=_x0.dtype)
    del _x0
    return _d

def reference(L0_attn_x, L0_attn_W_dq, L0_attn_W_uq, L0_attn_W_dkv, L0_attn_W_uk, L0_attn_W_uv, L0_attn_W_o, L0_ffn_fast_b, L0_ffn_w_fc, L0_ffn_w_proj, L0_ffn_u, L0_ffn_v, L0_ffn_gate, L1_attn_Wq, L1_attn_Wk, L1_attn_Wv, L1_attn_Wo, L1_attn_gamma, L1_attn_beta, L1_ffn_weight, L1_ffn_ln_gamma, L1_ffn_ln_beta):

    def _L0_attn_ref(x, W_dq, W_uq, W_dkv, W_uk, W_uv, W_o):
        import math
        import jax, jax.numpy as jnp
        import numpy as np
        D_MODEL = 256
        N_HEADS = 16
        D_K = D_MODEL // N_HEADS
        D_C = 64
        B, S = (2, 512)
        Bx, Sx, _ = x.shape
        c_q = x @ W_dq
        Q = (c_q @ W_uq).reshape(Bx, Sx, N_HEADS, D_K)
        c_kv = x @ W_dkv
        K = (c_kv @ W_uk).reshape(Bx, Sx, N_HEADS, D_K)
        V = (c_kv @ W_uv).reshape(Bx, Sx, N_HEADS, D_K)
        scores = jnp.einsum('bqhd,bkhd->bhqk', Q, K) / math.sqrt(D_K)
        causal = jnp.tril(jnp.ones((Sx, Sx), dtype=bool))
        scores = jnp.where(causal, scores, -jnp.inf)
        attn = jax.nn.softmax(scores, axis=-1)
        out = jnp.einsum('bhqk,bkhd->bqhd', attn, V).reshape(Bx, Sx, N_HEADS * D_K)
        return out @ W_o

    def _L0_ffn_ref(x, fast_b, w_fc, w_proj, u, v, gate):
        import jax, jax.numpy as jnp
        import numpy as np

        def _bitlinear(x, w_latent):
            scale = jax.lax.stop_gradient(jnp.clip(jnp.mean(jnp.abs(w_latent), axis=1, keepdims=True), 1e-05, None))
            tern = jnp.clip(jnp.round(w_latent / scale), -1.0, 1.0)
            w = w_latent + jax.lax.stop_gradient(tern - w_latent)
            return x @ (w * scale).T
        h = _bitlinear(x, w_fc) + gate * (x @ v.T @ fast_b.T @ u.T)
        r = jnp.maximum(h, 0.0)
        return _bitlinear(r * r, w_proj)

    def _L1_attn_ref(hidden_states, Wq, Wk, Wv, Wo, gamma, beta):
        import jax, jax.numpy as jnp
        import numpy as np
        HID = 256
        HEADS = 16
        FEAT = 16
        HD = HID // HEADS
        EPS = 1e-05
        LN_EPS = 1e-05
        B, T = (1, 256)
        IU, JU = np.triu_indices(FEAT, 1)

        def _feature_map(x, gamma, beta):
            mu = x.mean(axis=-1, keepdims=True)
            var = ((x - mu) ** 2).mean(axis=-1, keepdims=True)
            xn = (x - mu) / jnp.sqrt(var + LN_EPS) * gamma + beta
            diag = xn * xn
            off = xn[..., IU] * xn[..., JU]
            return jnp.concatenate([diag * FEAT ** (-0.5), off * (2.0 / FEAT) ** 0.5], axis=-1)
        b, t, _ = hidden_states.shape
        q = (hidden_states @ Wq.T).reshape(b, t, HEADS, FEAT).transpose(0, 2, 1, 3)
        k = (hidden_states @ Wk.T).reshape(b, t, HEADS, FEAT).transpose(0, 2, 1, 3)
        v = (hidden_states @ Wv.T).reshape(b, t, HEADS, HD).transpose(0, 2, 1, 3)
        phi_q = _feature_map(q, gamma, beta)
        phi_k = _feature_map(k, gamma, beta)
        kv_cum = jnp.cumsum(phi_k[..., :, None] * v[..., None, :], axis=2)
        num = jnp.einsum('bhtf,bhtfd->bhtd', phi_q, kv_cum)
        den = jnp.einsum('bhtf,bhtf->bht', phi_q, jnp.cumsum(phi_k, axis=2))[..., None] + EPS
        y = (num / den).transpose(0, 2, 1, 3).reshape(b, t, HEADS * HD)
        return y @ Wo.T

    def _L1_ffn_ref(x, weight, ln_gamma, ln_beta):
        import jax, jax.numpy as jnp
        import numpy as np
        LN_EPS = 0.001
        EPS = 1e-05
        QB = 128.0

        def ste_round(x):
            return x + jax.lax.stop_gradient(jnp.round(x) - x)
        mu = jnp.mean(x, axis=-1, keepdims=True)
        var = jnp.var(x, axis=-1, keepdims=True)
        xn = (x - mu) * jax.lax.rsqrt(var + LN_EPS) * ln_gamma + ln_beta
        beta = jnp.mean(jnp.abs(weight))
        w_q = jnp.clip(ste_round(weight / (beta + EPS)), -1.0, 1.0)
        gamma = jnp.max(jnp.abs(xn))
        xq = jnp.clip(xn * QB / gamma, -QB + EPS, QB - EPS)
        y = jnp.einsum('bsd,du->bsu', xq, w_q)
        return y * (gamma * beta / QB)
    x = L0_attn_x
    x = x + _layernorm(_L0_attn_ref(_layernorm(x, axis=-1), L0_attn_W_dq, L0_attn_W_uq, L0_attn_W_dkv, L0_attn_W_uk, L0_attn_W_uv, L0_attn_W_o), axis=-1)
    x = x + _layernorm(_L0_ffn_ref(_layernorm(x, axis=-1), L0_ffn_fast_b, L0_ffn_w_fc, L0_ffn_w_proj, L0_ffn_u, L0_ffn_v, L0_ffn_gate), axis=-1)
    x = x + _layernorm(_L1_attn_ref(_layernorm(x, axis=-1), L1_attn_Wq, L1_attn_Wk, L1_attn_Wv, L1_attn_Wo, L1_attn_gamma, L1_attn_beta), axis=-1)
    x = x + _layernorm(_L1_ffn_ref(_layernorm(x, axis=-1), L1_ffn_weight, L1_ffn_ln_gamma, L1_ffn_ln_beta), axis=-1)
    return x

_drawn_inputs = setup_inputs


def setup_inputs(seed=0):
    import zlib

    import numpy as np

    out = dict(_drawn_inputs(seed))
    spreads = {'L1_attn_gamma': (1.0, 0.2),
     'L1_attn_beta': (0.0, 0.373),
     'L1_ffn_ln_gamma': (1.0, 0.2),
     'L1_ffn_ln_beta': (0.0, 0.1)}
    factors = {'L0_ffn_fast_b': 3.569, 'L0_ffn_u': 3.621, 'L0_ffn_v': 3.528}
    for name, (base, spread) in spreads.items():
        noise = np.random.default_rng([zlib.crc32(name.encode()), seed]).standard_normal(out[name].shape)
        drawn = base * np.exp(spread * noise) if base else spread * noise
        out[name] = jnp.asarray(drawn.astype(out[name].dtype))
    for name, factor in factors.items():
        out[name] = (out[name] * factor).astype(out[name].dtype)
    return out
```

```python
from contextlib import ExitStack

import concourse.bass as bass
from concourse import mybir

F32 = mybir.dt.float32
BF16 = mybir.dt.bfloat16
ALU = mybir.AluOpType
ACT = mybir.ActivationFunctionType
AX = mybir.AxisListType

P = 128
NEG = -3.0e38
PARTS = 3
Q_STACK = (0, 0, 1, 0, 1, 2)
K_STACK = (0, 1, 0, 2, 1, 0)
STACK = 16 * len(Q_STACK)


class Sizes:
    def __init__(self, x, w_dq, w_fc):
        self.B, self.S, self.D = x.shape
        self.C = w_dq.shape[1]
        self.HID = w_fc.shape[0]
        self.DK = 16
        self.H = self.D // self.DK
        self.DC = self.D // P
        self.HC = self.HID // P
        self.TILES = self.B * self.S // P
        self.G = 4
        self.GT = self.G * P
        self.HPU = 4
        self.UPB = self.H // self.HPU
        self.UNITS = self.B * self.UPB
        self.ST = self.S // P
        assert self.S == 2 * self.GT and 2 * self.C == P and self.DC == 2 and self.H * self.DK == self.D


def build(nc, a, out):
    z = Sizes(a["L0_attn_x"], a["L0_attn_W_dq"], a["L0_ffn_w_fc"])
    with ExitStack() as ctx:
        m = Resident(nc, ctx, z)

        def run(one_pass, *args, **settings):
            with nc.cleanup_on_exit():
                one_pass(nc, z, m, *args, **settings)

        run(weights_pass, a)
        run(latent_pass, a)
        run(attend_pass, softmax=True)
        run(mix_pass, m.wo0, None)
        run(mlp_pass)
        run(features_pass)
        run(attend_pass, softmax=False)
        run(mix_pass, m.wo1, 1e-5)
        with nc.sbuf_tensor("normed", [P, z.TILES, z.D], F32) as normed:
            run(scale_pass, normed)
            run(ternary_pass, normed, out)


class Resident:

    def __init__(self, nc, ctx, z):
        def sb(name, shape, dt=F32):
            return ctx.enter_context(nc.sbuf_tensor(name, shape, dt))

        self.x = sb("x", [P, z.TILES, z.D])
        self.ident = sb("ident", [P, P])
        self.ident16 = sb("ident16", [P, P], BF16)
        self.eps = sb("eps", [P, 1])
        self.eps_in = sb("eps_in", [P, 1])
        self.w_down = sb("w_down", [P, z.DC, P])
        self.w_uq = sb("w_uq", [P, z.D])
        self.w_uk = sb("w_uk", [P, z.D])
        self.w_uv = sb("w_uv", [P, z.D])
        self.wo0 = sb("wo0", [P, z.DC, z.D])
        self.wo1 = sb("wo1", [P, z.DC, z.D])
        self.w_fc = sb("w_fc", [P, z.DC, z.HID])
        self.w_proj = sb("w_proj", [P, z.HC, z.D])
        self.w_qkv = sb("w_qkv", [P, z.DC, 3 * z.D])
        self.w_ter = sb("w_ter", [P, z.DC, z.D])
        self.gamma_col = sb("gamma_col", [P, 1])
        self.beta_col = sb("beta_col", [P, 1])
        self.ln_gamma = sb("ln_gamma", [P, z.D])
        self.ln_beta = sb("ln_beta", [P, z.D])
        self.peaks = sb("peaks", [P, z.TILES // z.G])
        self.w_mean = sb("w_mean", [P, 1])
        self.psum = ctx.enter_context(nc.psum_tensor("psum", [P, 8, 512], F32))
        self.bank = [self.psum[:, i, :] for i in range(8)]
        self.alone = ctx.enter_context(nc.semaphore("alone"))
        self.qk_dram = nc.dram_tensor("qk_parts", [PARTS, 2, z.B * z.D, z.S], BF16, kind="Internal").ap()
        self.v_dram = nc.dram_tensor("values", [z.UNITS, z.S, P], F32, kind="Internal").ap()
        self.o_dram = nc.dram_tensor("sums", [2, z.B * z.D, z.S], F32, kind="Internal").ap()


def sems(nc, *names):
    return [nc.alloc_semaphore(n) for n in names]



def wait_alone(eng, sem, value, alone):
    eng.wait_ge(sem, value)
    eng.sem_inc(alone, 1)


def statistics(m, dve, tiles, raw, mv, raw_done, mv_ready, n):
    for t, tile in enumerate(tiles):
        last = dve.bn_stats(raw[:, t, :], tile)
    last.then_inc(raw_done, 1)
    wait_alone(dve, raw_done, n + 1, m.alone)
    for t in range(len(tiles)):
        last = dve.bn_aggr(mv[:, t, :], raw[:, t, :])
    last.then_inc(mv_ready, 1)


def deviation(act, mv, sd, eps, mv_ready, sd_ready, n, credit=0, scale=1.0):
    act.wait_ge(mv_ready, n + 1 + credit)
    act.activation(sd[:, :], mv[:, :, 1], ACT.Sqrt, bias=eps[:, 0:1], scale=scale).then_inc(sd_ready, 1)


def inverse(dve, sd, rs, sd_ready, rs_ready, n):
    dve.wait_ge(sd_ready, n + 1)
    dve.reciprocal(rs[:, :], sd[:, :]).then_inc(rs_ready, 1)
    dve.wait_ge(rs_ready, n + 1)


def normalise(dve, out, tiles, mv, rs):
    for t, tile in enumerate(tiles):
        last = dve.tensor_scalar(out[:, t, :], tile, mv[:, t, 0:1], rs[:, t:t + 1], ALU.subtract, ALU.mult)
    return last


def turn_group(pe, z, banks, src, ident):
    for c in range(z.DC):
        for t in range(z.G):
            last = pe.transpose(banks[c][:, t * P:(t + 1) * P], src[:, t, c * P:(c + 1) * P], ident[:, :])
    return last


def staggered(eng, groups, ahead, behind, behind_first=False):
    for u in range(2):
        ahead(0, u)
    with eng.Fori(0, groups // 2 - 1) as i:
        for u in range(2):
            if behind_first:
                behind(i, u)
            ahead(i + 1, u)
            if not behind_first:
                behind(i, u)
    for u in range(2):
        behind(groups // 2 - 1, u)


def of_group(z, x, n):
    return [x[:, bass.ds(n * z.G + t, 1), :] for t in range(z.G)]



def weights_pass(nc, z, m, a):
    with ExitStack() as ctx:
        def sb(name, shape, dt=F32):
            return ctx.enter_context(nc.sbuf_tensor(name, shape, dt))

        rank = a["L0_ffn_u"].shape[1]
        fc = sb("fc", [P, z.HC, z.D])
        proj = sb("proj", [P, z.DC, z.HID])
        qkv = sb("qkv", [P, 3, z.DC, z.D])
        wo = sb("wo", [P, z.DC, z.D])
        ter = sb("ter", [P, z.DC, z.D])
        u = sb("u", [P, z.HC, rank])
        fast = sb("fast", [rank, rank])
        v = sb("v", [rank, z.D])
        gate = sb("gate", [rank, 1])
        fast_t = sb("fast_t", [rank, rank])
        fv = sb("fv", [rank, z.D])
        u_t = sb("u_t", [rank, z.HID])
        sums = sb("sums_w", [P, z.HC + z.DC + 1])
        scale = sb("scale", [P, z.HC + z.DC])
        half = sb("half", [P, z.HC + z.DC + 1])
        nhalf = sb("nhalf", [P, z.HC + z.DC + 1])
        fc_w = sb("fc_w", [P, z.HC, z.D])
        proj_w = sb("proj_w", [P, z.DC, z.HID])
        neg = sb("neg", [P, z.HC * z.D])
        means = sb("means", [P, z.DC * 2 * z.H])
        total = sb("total", [P, 1])
        (loaded, ident_zero, ident_ready, zeros_ready, step, pe_step, drained, total_ready, total_in) = sems(
            nc, "w_loaded", "w_ident_zero", "w_ident_ready", "w_zeros_ready", "w_dve_step", "w_pe_step",
            "w_drained", "w_total_ready", "w_total_in")
        block = ctx.enter_context(nc.Block())
        chunks = lambda w: w.rearrange("(c p) n -> p c n", p=P)
        loads = [
            (fc[:, :, :], chunks(a["L0_ffn_w_fc"])), (proj[:, :, :], chunks(a["L0_ffn_w_proj"])),
            (qkv[:, 0, :, :], chunks(a["L1_attn_Wq"])), (qkv[:, 1, :, :], chunks(a["L1_attn_Wk"])),
            (qkv[:, 2, :, :], chunks(a["L1_attn_Wv"])), (wo[:, :, :], chunks(a["L1_attn_Wo"])),
            (ter[:, :, :], chunks(a["L1_ffn_weight"])), (u[:, :, :], chunks(a["L0_ffn_u"])),
            (fast[:, :], a["L0_ffn_fast_b"]), (v[:, :], a["L0_ffn_v"]),
            (gate[:, :], a["L0_ffn_gate"].partition_broadcast(rank)),
            (m.w_down[:, :, 0:z.C], chunks(a["L0_attn_W_dq"])), (m.w_down[:, :, z.C:P], chunks(a["L0_attn_W_dkv"])),
            (m.w_uq[0:z.C, :], a["L0_attn_W_uq"]), (m.w_uk[z.C:P, :], a["L0_attn_W_uk"]),
            (m.w_uv[z.C:P, :], a["L0_attn_W_uv"]), (m.wo0[:, :, :], chunks(a["L0_attn_W_o"])),
            (m.ln_gamma[:, :], a["L1_ffn_ln_gamma"].partition_broadcast(P)),
            (m.ln_beta[:, :], a["L1_ffn_ln_beta"].partition_broadcast(P)),
        ]
        for h in range(P // z.DK):
            rows = slice(h * z.DK, (h + 1) * z.DK)
            loads.append((m.gamma_col[rows, :], a["L1_attn_gamma"].unsqueeze(1)))
            loads.append((m.beta_col[rows, :], a["L1_attn_beta"].unsqueeze(1)))

        @block.sync
        def _(sp):
            for dst, src in loads:
                sp.dma_start(dst, src).then_inc(loaded, 16)

        @block.gpsimd
        def _(pool):
            pool.memset(m.ident[:, :], 0.0).then_inc(ident_zero, 1)
            pool.memset(m.ident16[:, :], 0.0).then_inc(ident_zero, 1)
            pool.wait_ge(ident_zero, 2)
            for t in (m.ident, m.ident16):
                pool.affine_select(out=t[:, :], in_=t[:, :], compare_op=ALU.not_equal, fill=1.0, base=0,
                                   pattern=[[-1, P]], channel_multiplier=1).then_inc(ident_ready, 1)
            pool.wait_ge(total_in, 1)
            pool.partition_all_reduce(total[:, :], sums[:, z.HC + z.DC:], P,
                                      bass.bass_isa.ReduceOp.add).then_inc(total_ready, 1)

        T_FC, T_PROJ, T_FAST = "fc", "proj", "fast"
        dve_done, pe_done = {}, {}

        @block.vector
        def _(dve):
            count = [0]

            def did(ins, name=None):
                count[0] += 1
                ins.then_inc(step, 1)
                dve.wait_ge(step, count[0])
                if name:
                    dve_done[name] = count[0]

            did(dve.memset(m.w_uq[z.C:P, :], 0.0))
            did(dve.memset(m.w_uk[0:z.C, :], 0.0))
            did(dve.memset(m.w_uv[0:z.C, :], 0.0))
            did(dve.memset(m.eps[:, :], 1e-5))
            did(dve.memset(m.eps_in[:, :], 1e-3))
            dve.wait_ge(loaded, 16 * len(loads))
            did(dve.tensor_reduce(sums[:, 0:z.HC], fc[:, :, :], AX.X, ALU.add, apply_absolute_value=True))
            did(dve.tensor_reduce(sums[:, z.HC:z.HC + z.DC], proj[:, :, :], AX.X, ALU.add, apply_absolute_value=True))
            did(dve.tensor_reduce(sums[:, z.HC + z.DC:], ter[:, :, :], AX.XY, ALU.add, apply_absolute_value=True))
            dve.sem_inc(total_in, 1)
            did(dve.tensor_scalar(scale[:, 0:z.HC], sums[:, 0:z.HC], 1.0 / z.D, 1e-5, ALU.mult, ALU.max))
            did(dve.tensor_scalar(scale[:, z.HC:], sums[:, z.HC:z.HC + z.DC], 1.0 / z.HID, 1e-5, ALU.mult, ALU.max))
            did(dve.tensor_scalar(half[:, 0:z.HC + z.DC], scale[:, :], 0.5, None, ALU.mult))
            did(dve.tensor_scalar(nhalf[:, 0:z.HC + z.DC], scale[:, :], -0.5, None, ALU.mult))
            for name, w, dst, rows, width, at in ((T_FC, fc, fc_w, z.HC, z.D, 0),
                                                  (T_PROJ, proj, proj_w, z.DC, z.HID, z.HC)):
                view = neg[:, :].rearrange("p (r w) -> p r w", r=rows)
                for r in range(rows):
                    k = at + r
                    dve.tensor_scalar(dst[:, r, :], w[:, r, :], half[:, k:k + 1], scale[:, k:k + 1], ALU.is_gt, ALU.mult)
                    last = dve.tensor_scalar(view[:, r, :], w[:, r, :], nhalf[:, k:k + 1], scale[:, k:k + 1],
                                             ALU.is_lt, ALU.mult)
                did(last)
                did(dve.tensor_tensor(dst[:, :, :], dst[:, :, :], view, ALU.subtract), name)
            dve.wait_ge(total_ready, 1)
            k = z.HC + z.DC
            did(dve.tensor_scalar(m.w_mean[:, :], total[:, :], 1.0 / (z.D * z.D), None, ALU.mult))
            did(dve.tensor_scalar(half[:, k:k + 1], m.w_mean[:, :], 1e-5, 0.5, ALU.add, ALU.mult))
            did(dve.tensor_scalar(nhalf[:, k:k + 1], half[:, k:k + 1], -1.0, None, ALU.mult))
            did(dve.tensor_scalar(neg[:, 0:z.DC * z.D], ter[:, :, :].rearrange("p c n -> p (c n)"),
                                  nhalf[:, k:k + 1], None, ALU.is_lt))
            did(dve.scalar_tensor_tensor(out=m.w_ter[:, :, :].rearrange("p c n -> p (c n)"),
                                         in0=ter[:, :, :].rearrange("p c n -> p (c n)"), scalar=half[:, k:k + 1],
                                         in1=neg[:, 0:z.DC * z.D], op0=ALU.is_gt, op1=ALU.subtract))

            got = [0]

            def take(name=None, fn=None):
                got[0] += 1
                dve.wait_ge(pe_step, got[0])
                fn().then_inc(drained, 1)
                dve.wait_ge(drained, got[0])
                if name:
                    pe_done[name] = got[0]

            take("fast_t", lambda: dve.tensor_copy(fast_t[:, :], m.bank[0][0:rank, 0:rank]))
            take("fv", lambda: dve.tensor_scalar(fv[:, :], m.bank[1][0:rank, 0:z.D], gate[:, 0:1], None, ALU.mult))
            for k in range(2):
                take("u_t", lambda: dve.tensor_copy(u_t[:, k * 512:(k + 1) * 512], m.bank[2 + k][0:rank, :]))
            for n, (c, k) in enumerate((c, k) for c in range(z.DC) for k in range(z.HID // 512)):
                dst = m.w_fc[:, c, k * 512:(k + 1) * 512]
                take(None, lambda: dve.tensor_copy(dst, m.bank[4][:, :]))
                take("fc", lambda: dve.tensor_tensor(dst, dst, m.bank[5][:, :], ALU.add))
            for g in range(z.HC // 2):
                take("proj", lambda: dve.tensor_copy(m.w_proj[:, 2 * g:2 * g + 2, :],
                                                     m.bank[6 + g % 2][:, :].rearrange("p (j n) -> p j n", j=2)))
            for w in range(4):
                dst = m.w_qkv[:, :, w * z.D:(w + 1) * z.D] if w < 3 else m.wo1[:, :, :]
                take("qkv", lambda: dve.tensor_copy(dst, m.bank[w][:, :].rearrange("p (c n) -> p c n", c=z.DC)))
            for c in range(z.DC):
                view = m.w_qkv[:, c, 0:2 * z.D].rearrange("p (h f) -> p h f", f=z.DK)
                mean = means[:, c * 2 * z.H:(c + 1) * 2 * z.H]
                did(dve.tensor_reduce(mean, view, AX.X, ALU.add))
                did(dve.tensor_scalar(mean, mean, 1.0 / z.DK, None, ALU.mult))
                did(dve.tensor_tensor(view, view, mean.unsqueeze(2).to_broadcast([P, 2 * z.H, z.DK]), ALU.subtract))

        @block.tensor
        def _(pe):
            pe.wait_ge(loaded, 16 * len(loads))
            pe.wait_ge(ident_ready, 2)
            pe.transpose(m.bank[0][0:rank, 0:rank], fast[:, :], m.ident[0:rank, 0:rank]).then_inc(pe_step, 1)
            pe.wait_ge(drained, pe_done["fast_t"])
            pe.matmul(m.bank[1][0:rank, 0:z.D], fast_t[:, :], v[:, :], start=True, stop=True).then_inc(pe_step, 1)
            for k in range(2):
                for t in range(4):
                    last = pe.transpose(m.bank[2 + k][0:rank, t * P:(t + 1) * P], u[:, 4 * k + t, :], m.ident[:, :])
                last.then_inc(pe_step, 1)
            pe.wait_ge(drained, pe_done["u_t"])
            pe.wait_ge(step, dve_done[T_PROJ])
            done = pe_done["u_t"]
            for c in range(z.DC):
                for k in range(z.HID // 512):
                    for t in range(4):
                        last = pe.transpose(m.bank[4][:, t * P:(t + 1) * P],
                                            fc_w[:, 4 * k + t, c * P:(c + 1) * P], m.ident[:, :])
                    last.then_inc(pe_step, 1)
                    pe.matmul(m.bank[5][:, :], fv[:, c * P:(c + 1) * P], u_t[:, k * 512:(k + 1) * 512],
                              start=True, stop=True).then_inc(pe_step, 1)
                    done += 2
                    pe.wait_ge(drained, done)
            for g in range(z.HC // 2):
                if g >= 2:
                    pe.wait_ge(drained, done + g - 1)
                for j in range(2):
                    for c in range(z.DC):
                        col = j * z.D + c * P
                        last = pe.transpose(m.bank[6 + g % 2][:, col:col + P],
                                            proj_w[:, c, (2 * g + j) * P:(2 * g + j + 1) * P], m.ident[:, :])
                last.then_inc(pe_step, 1)
            for w in range(4):
                src = qkv[:, w, :, :] if w < 3 else wo[:, :, :]
                for c in range(z.DC):
                    for o in range(z.DC):
                        col = c * z.D + o * P
                        last = pe.transpose(m.bank[w][:, col:col + P], src[:, o, c * P:(c + 1) * P], m.ident[:, :])
                last.then_inc(pe_step, 1)



def latent_pass(nc, z, m, a):
    G, DC, GROUPS = z.G, z.DC, z.TILES // z.G
    xg = a["L0_attn_x"].rearrange("b s d -> (b s) d").rearrange("(n p) d -> p n d", p=P)
    with ExitStack() as ctx:
        def sb(name, shape, dt=F32):
            return [ctx.enter_context(nc.sbuf_tensor(f"l_{name}{u}", shape, dt)) for u in range(2)]

        raw, mv, sd, rs = sb("raw", [P, G, 6]), sb("mv", [P, G, 2]), sb("sd", [P, G]), sb("rs", [P, G])
        xn, xt, ct = sb("xn", [P, G, z.D]), sb("xt", [P, DC, z.GT]), sb("ct", [P, z.GT])
        parts, rest = sb("parts", [P, PARTS, 4, z.GT], BF16), sb("rest", [P, 4, z.GT])
        vx = sb("vx", [P, G, z.H, 32])
        x_loaded = sems(nc, "l_x_loaded0", "l_x_loaded1")
        stored = sems(nc, "l_stored0", "l_stored1")
        (raw_done, mv_ready, sd_ready, rs_ready, xn_ready, turned, xt_ready, c_ready, ct_ready, qk_ready,
         high_done, rest_done, mid_done, low_done, v_ready, vx_ready, ones_ready) = sems(
            nc, "l_raw_done", "l_mv_ready", "l_sd_ready", "l_rs_ready", "l_xn_ready", "l_turned", "l_xt_ready",
            "l_c_ready", "l_ct_ready", "l_qk_ready", "l_high_done", "l_rest_done", "l_mid_done", "l_low_done",
            "l_v_ready", "l_vx_ready", "l_ones_ready")
        block = ctx.enter_context(nc.Block())
        T0, CB, QK0, VB = 0, 2, 3, 7
        STORED = 16 * (PARTS * 4 + G)

        @block.sync
        def _(sp):
            for u in range(2):
                sp.sem_inc(stored[u], STORED)

            def load(i, u):
                n = 2 * i + u
                sp.wait_ge(mv_ready, n + 1)
                sp.dma_start(m.x[:, bass.ts(n, G), :], xg[:, bass.ts(n, G), :]).then_inc(x_loaded[u], 16)

            def store(i, u):
                n = 2 * i + u
                sp.wait_ge(vx_ready, 2 * n + 3)
                for t in range(G):
                    at = u * z.GT + t * P
                    sp.dma_start(m.v_dram[bass.ts(i, z.UPB), at:at + P, :].rearrange("g p k -> p g k"),
                                 vx[u][:, t, :, :].rearrange("p (g h) k -> p g (h k)", g=z.UPB)).then_inc(stored[u], 16)
                sp.wait_ge(low_done, n + 3)
                store_parts(sp, z, m, parts[u], stored[u], i, u)

            staggered(sp, GROUPS, load, store)
            for u in range(2):
                sp.wait_ge(stored[u], STORED * (GROUPS // 2 + 1))

        @block.vector
        def _(dve):
            for u in range(2):
                last = dve.memset(vx[u][:, :, :, 16:32], 1.0)
            last.then_inc(ones_ready, 1)
            dve.sem_inc(mv_ready, 2)
            dve.sem_inc(rest_done, 4)

            def norm(i, u):
                n = 2 * i + u
                dve.wait_ge(x_loaded[u], 16 * i + 16)
                tiles = of_group(z, m.x, n)
                statistics(m, dve, tiles, raw[u], mv[u], raw_done, mv_ready, n)
                inverse(dve, sd[u], rs[u], sd_ready, rs_ready, n)
                dve.wait_ge(turned, n + 1)
                normalise(dve, xn[u], tiles, mv[u], rs[u]).then_inc(xn_ready, 1)

            def split(i, u):
                n = 2 * i + u
                dve.wait_ge(low_done, n + 1)
                for j in range(4):
                    dve.wait_ge(high_done, 4 * n + j + 1)
                    dve.tensor_tensor(rest[u][:, j, :], m.bank[QK0 + j][:, :], parts[u][:, 0, j, :],
                                      ALU.subtract).then_inc(rest_done, 1)

            staggered(dve, GROUPS, norm, split)

        @block.gpsimd
        def _(pool):
            pool.sem_inc(low_done, 2)
            with pool.Fori(0, GROUPS // 2) as i:
                for u in range(2):
                    n = 2 * i + u
                    wait_alone(pool, rest_done, 4 * n + 8, m.alone)
                    split_rest(pool, parts[u], rest[u], mid_done, low_done, n)

        @block.scalar
        def _(act):
            act.sem_inc(xt_ready, 1)
            act.sem_inc(ct_ready, 1)
            act.sem_inc(vx_ready, 1)

            def root(i, u):
                deviation(act, mv[u], sd[u], m.eps, mv_ready, sd_ready, 2 * i + u, credit=2)

            def take_turned(i, u):
                n = 2 * i + u
                act.wait_ge(turned, n + 3)
                act.wait_ge(c_ready, n + 1)
                for c in range(DC):
                    last = act.activation(xt[u][:, c, :], m.bank[T0 + c][:, :], ACT.Copy)
                last.then_inc(xt_ready, 1)

            def rest_of_group(i, u):
                n = 2 * i + u
                act.wait_ge(c_ready, n + 3)
                act.wait_ge(v_ready, 2 * n + 2)
                act.activation(ct[u][:, :], m.bank[CB][:, :], ACT.Copy).then_inc(ct_ready, 1)
                act.wait_ge(stored[u], STORED * i + STORED)
                for j in range(4):
                    act.wait_ge(qk_ready, 4 * n + j + 1)
                    act.activation(parts[u][:, 0, j, :], m.bank[QK0 + j][:, :], ACT.Copy).then_inc(high_done, 1)
                act.wait_ge(ones_ready, 1)
                for k in range(2):
                    act.wait_ge(v_ready, 2 * n + k + 5)
                    act.activation(vx[u][:, 2 * k:2 * k + 2, :, 0:16],
                                   m.bank[VB][:, :].rearrange("p (t h d) -> p t h d", t=2, d=16),
                                   ACT.Copy).then_inc(vx_ready, 1)

            for u in range(2):
                root(0, u)
                take_turned(0, u)
            with act.Fori(0, GROUPS // 2 - 1) as i:
                for u in range(2):
                    root(i + 1, u)
                    rest_of_group(i, u)
                    take_turned(i + 1, u)
            for u in range(2):
                rest_of_group(GROUPS // 2 - 1, u)

        @block.tensor
        def _(pe):
            pe.sem_inc(turned, 2)
            pe.sem_inc(c_ready, 2)
            pe.sem_inc(v_ready, 4)

            def turn(i, u):
                n = 2 * i + u
                pe.wait_ge(xn_ready, n + 1)
                pe.wait_ge(xt_ready, n + 1)
                turn_group(pe, z, m.bank[T0:T0 + DC], xn[u], m.ident).then_inc(turned, 1)

            def project(i, u):
                n = 2 * i + u
                pe.wait_ge(xt_ready, n + 2)
                pe.wait_ge(ct_ready, n + 1)
                for c in range(DC):
                    last = pe.matmul(m.bank[CB][:, :], m.w_down[:, c, :], xt[u][:, c, :], start=(c == 0), stop=(c == DC - 1))
                last.then_inc(c_ready, 1)
                pe.wait_ge(ct_ready, n + 2)
                for j in range(4):
                    w = (m.w_uq, m.w_uk)[j // 2]
                    pe.wait_ge(rest_done, 4 * n + j + 1)
                    pe.matmul(m.bank[QK0 + j][:, :], w[:, (j % 2) * P:(j % 2 + 1) * P], ct[u][:, :],
                              start=True, stop=True).then_inc(qk_ready, 1)
                for k in range(2):
                    pe.wait_ge(vx_ready, 2 * n + k + 1)
                    for t in range(2):
                        cols = slice((2 * k + t) * P, (2 * k + t + 1) * P)
                        last = pe.matmul(m.bank[VB][:, t * z.D:(t + 1) * z.D], ct[u][:, cols], m.w_uv[:, :],
                                         start=True, stop=True)
                    last.then_inc(v_ready, 1)

            staggered(pe, GROUPS, turn, project, behind_first=True)


def store_parts(eng, z, m, parts, stored, i, u):
    for part in range(PARTS):
        for j in range(4):
            eng.dma_start(m.qk_dram[part, j // 2, bass.ds(i * z.D + (j % 2) * P, P), u * z.GT:(u + 1) * z.GT],
                          parts[:, part, j, :]).then_inc(stored, 16)


def split_rest(pool, parts, rest, mid_done, low_done, n):
    pool.tensor_copy(parts[:, 1, :, :], rest[:, :, :]).then_inc(mid_done, 1)
    pool.wait_ge(mid_done, n + 1)
    pool.tensor_tensor(parts[:, 2, :, :], rest[:, :, :], parts[:, 1, :, :], ALU.subtract).then_inc(low_done, 1)



def attend_pass(nc, z, m, softmax):
    tag = "a" if softmax else "b"
    RING = 3
    HPU, ST, UNITS = z.HPU, z.ST, z.UNITS
    ROUNDS = (UNITS - 2) // RING
    assert UNITS == RING * ROUNDS + 2
    ROWS = STACK + 2 if softmax else STACK
    steps = [(h, kt) for h in range(2) for kt in range(4 * (h + 1))]
    STEPS = len(steps)
    DIAG = [s for s, (h, kt) in enumerate(steps) if kt >= 4 * h]
    chunks = [(hd, qt, h) for hd in range(HPU) for qt in range(ST) for h in range(1 + qt // 4)]
    CH = len(chunks)
    BY = [min(CH, CH * s // 10) for s in range(STEPS + 1)]
    with ExitStack() as ctx:
        def sb(name, shape, dt=F32, n=1):
            return [ctx.enter_context(nc.sbuf_tensor(f"{tag}_{name}{u}", shape, dt)) for u in range(n)]

        def sm(*names):
            return sems(nc, *[f"{tag}_{x}" for x in names])

        qs, ks = sb("qs", [P, HPU, z.S], BF16, RING), sb("ks", [P, HPU, z.S], BF16, RING)
        vs = sb("vs", [P, ST, P], F32, RING)
        p = sb("p", [P, HPU, 512], F32, 3)
        osb = sb("osb", [P, 512], F32, 2)
        loaded = sm(*[f"loaded{r}" for r in range(RING)])
        stored = sm("stored0", "stored1")
        st_ready, p_ready, masked, pv_done, o_taken = sm("st_ready", "p_ready", "masked", "pv_done", "o_taken")
        LOADED = 16 * (2 * len(Q_STACK) + 1)
        STORED = 16 * 2 * HPU
        PV, PR, OT, STK, RT, RR = 3, 2, 1, 2, 1, 1
        if softmax:
            bias, = sb("bias", [P, 512])
            dump = sb("dump", [P, 512], BF16, 2)
            peak, = sb("peak", [P, HPU * ST, 2])
            npeak, = sb("npeak", [P, HPU * ST])
            split, = sb("split", [P, 2, HPU * ST], BF16)
            rows, = sb("rows", [2 * HPU * ST, P], BF16)
            rows_loaded = sm(*[f"rows_loaded{r}" for r in range(RING)])
            (bias_zero, bias_ready, peak_set, s_ready, s_taken, npeak_ready, high_ready, split_ready, rows_turned,
             rows_ready, ones_ready) = sm("bias_zero", "bias_ready", "peak_set", "s_ready", "s_taken", "npeak_ready",
                                          "high_ready", "split_ready", "rows_turned", "rows_ready", "ones_ready")
        block = ctx.enter_context(nc.Block())
        SB, OB, RB = 4, 6, 7

        def q0(s):
            h, kt = steps[s]
            return max(0, kt * P - h * 512)

        def all_units(eng, unit):
            with eng.Fori(0, ROUNDS) as i:
                for r in range(RING):
                    unit(RING * i + r, r, i, True, True)
            unit(UNITS - 2, 0, ROUNDS, True, False)
            unit(UNITS - 1, 1, ROUNDS, False, False)

        @block.sync
        def _(sp):
            for u in range(2):
                sp.sem_inc(stored[u], STORED)

            def load(n, r):
                for tile, which, stack in ((qs[r], 0, Q_STACK), (ks[r], 1, K_STACK)):
                    for g, part in enumerate(stack):
                        src = m.qk_dram[part, which, bass.ts(n, HPU * z.DK), :]
                        sp.dma_start(tile[16 * g:16 * g + 16, :, :], src.rearrange("(h d) t -> d h t", d=z.DK)
                                     ).then_inc(loaded[r], 16)
                sp.dma_start(vs[r][:, :, :], m.v_dram[bass.ts(n, 1), :, :].rearrange("n (k p) c -> p (n k) c", p=P)
                             ).then_inc(loaded[r], 16)

            def load_rows(n, r):
                sp.wait_ge(rows_ready, n + 1 + RR)
                for k in range(2):
                    sp.dma_start(qs[r][STACK + k:STACK + k + 1, :, :],
                                 rows[k * HPU * ST:(k + 1) * HPU * ST, :]).then_inc(rows_loaded[r], 16)

            def store(n, h):
                sp.wait_ge(o_taken, 2 * n + h + 1 + OT)
                for hd in range(HPU):
                    for k in range(2):
                        row = 32 * hd + 16 * k
                        sp.dma_start(m.o_dram[k, bass.ds(z.DK * (HPU * n + hd), z.DK), h * 512:(h + 1) * 512],
                                     osb[h][row:row + 16, :]).then_inc(stored[h], 16)

            def unit(n, r, rnd, ahead, far):
                if far:
                    sp.wait_ge(pv_done, STEPS * n + PV)
                    load(n + 2, (r + 2) % RING)
                store(n, 0)
                if softmax and ahead:
                    load_rows(n + 1, (r + 1) % RING)
                store(n, 1)

            load(0, 0)
            load(1, 1)
            if softmax:
                load_rows(0, 0)
            all_units(sp, unit)
            for h in range(2):
                sp.wait_ge(stored[h], STORED * (UNITS + 1))

        @block.gpsimd
        def _(pool):
            if softmax:
                pool.memset(bias[:, :], 0.0).then_inc(bias_zero, 1)
                pool.wait_ge(bias_zero, 1)
                pool.affine_select(out=bias[:, 512 - P:], in_=bias[:, 512 - P:], compare_op=ALU.is_ge, fill=NEG,
                                   base=0, pattern=[[-1, P]], channel_multiplier=1).then_inc(bias_ready, 1)

            def unit(n, r, rnd, ahead, far):
                for d, s in enumerate(DIAG):
                    wait_alone(pool, p_ready, 2 * STEPS * n + 2 * s + 2 + PR, m.alone)
                    diag = p[s % 3][:, :, q0(s):q0(s) + P]
                    pool.affine_select(out=diag, in_=diag, compare_op=ALU.is_ge, fill=0.0, base=0,
                                       pattern=[[0, HPU], [1, P]], channel_multiplier=-1).then_inc(masked, 1)

            all_units(pool, unit)

        @block.scalar
        def _(act):
            act.sem_inc(p_ready, PR)
            act.sem_inc(o_taken, OT)
            if softmax:
                act.sem_inc(rows_ready, RR)

            def take_rows(n, before):
                act.wait_ge(rows_turned, n + 1 + RT)
                if before:
                    act.wait_ge(*before)
                act.activation(rows[:, :], m.bank[RB].bitcast(BF16)[0:2 * HPU * ST, 0:P], ACT.Copy).then_inc(rows_ready, 1)

            def take_sums(n, h):
                act.wait_ge(pv_done, STEPS * n + (4, STEPS)[h] + PV)
                act.wait_ge(stored[h], STORED * n + STORED)
                act.activation(osb[h][:, :], m.bank[OB], ACT.Copy).then_inc(o_taken, 1)

            def unit(n, r, rnd, ahead, far):
                for s in range(STEPS):
                    act.wait_ge(pv_done, STEPS * n + s + 1)
                    for k in range(2):
                        act.wait_ge(st_ready, 2 * STEPS * n + 2 * s + k + 1)
                        src = m.psum[:, 2 * k:2 * k + 2, q0(s):512]
                        act.activation(p[s % 3][:, 2 * k:2 * k + 2, q0(s):512], src, ACT.Exp if softmax else ACT.Square,
                                       scale=z.DK ** -0.5).then_inc(p_ready, 1)
                    if s == 4:
                        take_sums(n, 0)
                if softmax and ahead:
                    take_rows(n + 1, (rows_loaded[r], 32 * rnd + 32))
                take_sums(n, 1)

            if softmax:
                take_rows(0, None)
            all_units(act, unit)

        @block.vector
        def _(dve):
            if not softmax:
                return
            for r in range(RING):
                last = dve.memset(ks[r][STACK:STACK + 2, :, :], 1.0)
            last.then_inc(ones_ready, 1)
            dve.memset(peak[:, :, :], NEG).then_inc(peak_set, 1)
            dve.sem_inc(s_taken, STK)
            dve.wait_ge(peak_set, 1)
            dve.wait_ge(bias_ready, 1)

            def maxima(n):
                for c, (hd, qt, h) in enumerate(chunks):
                    wait_alone(dve, s_ready, CH * n + c + 1, m.alone)
                    bank, dst = m.bank[SB + c % 2], peak[:, hd * ST + qt, h:h + 1]
                    if h < qt // 4:
                        last = dve.tensor_reduce(dst, bank, AX.X, ALU.max)
                    else:
                        w = (qt % 4 + 1) * P
                        last = dve.tensor_tensor_reduce(dump[c % 2][:, 0:w], bank[:, 0:w], bias[:, 512 - w:], 1.0, NEG,
                                                        ALU.add, ALU.max, dst)
                    last.then_inc(s_taken, 1)
                dve.wait_ge(s_taken, CH * n + CH + STK)
                dve.tensor_reduce(npeak[:, :], peak[:, :, :], AX.X, ALU.max, negate=True).then_inc(npeak_ready, 1)
                dve.wait_ge(npeak_ready, n + 1)
                dve.wait_ge(rows_turned, n + 1)
                dve.tensor_copy(split[:, 0, :], npeak[:, :]).then_inc(high_ready, 1)
                dve.wait_ge(high_ready, n + 1)
                dve.tensor_tensor(split[:, 1, :], npeak[:, :], split[:, 0, :], ALU.subtract).then_inc(split_ready, 1)

            maxima(0)
            all_units(dve, lambda n, r, rnd, ahead, far: maxima(n + 1) if ahead else None)

        @block.tensor
        def _(pe):
            pe.sem_inc(pv_done, PV)
            if softmax:
                pe.sem_inc(rows_turned, RT)
                pe.wait_ge(ones_ready, 1)

            def maximum_scores(n, r, a, b):
                for c in range(a, b):
                    hd, qt, h = chunks[c]
                    pe.wait_ge(s_taken, CH * n + c + 1)
                    w = 512 if h < qt // 4 else (qt % 4 + 1) * P
                    pe.matmul(m.bank[SB + c % 2][:, 0:w], qs[r][0:STACK, hd, qt * P:(qt + 1) * P],
                              ks[r][0:STACK, hd, h * 512:h * 512 + w], start=True, stop=True).then_inc(s_ready, 1)

            def turn_rows(n):
                pe.wait_ge(split_ready, n + 1)
                wait_alone(pe, rows_ready, n + 1, m.alone)
                pe.transpose(m.bank[RB].bitcast(BF16)[0:2 * HPU * ST, 0:P], split[:, :, :].rearrange("p k c -> p (k c)"),
                             m.ident16[:, :]).then_inc(rows_turned, 1)

            def scores(n, r, s):
                h, kt = steps[s]
                for k in range(2):
                    pe.wait_ge(p_ready, 2 * STEPS * n + 2 * s + k + 1)
                    for hd in (2 * k, 2 * k + 1):
                        last = pe.matmul(m.bank[hd][:, q0(s):512], ks[r][0:ROWS, hd, kt * P:(kt + 1) * P],
                                         qs[r][0:ROWS, hd, h * 512 + q0(s):(h + 1) * 512], start=True, stop=True)
                    last.then_inc(st_ready, 1)

            def weigh(n, r, s):
                h, kt = steps[s]
                pe.wait_ge(p_ready, 2 * STEPS * n + 2 * s + 2 + PR)
                if s in DIAG:
                    pe.wait_ge(masked, len(DIAG) * n + DIAG.index(s) + 1)
                if kt == 0:
                    pe.wait_ge(o_taken, 2 * n + h + 1)
                for hd in range(HPU):
                    last = pe.matmul(m.bank[OB][32 * hd:32 * hd + 32, q0(s):512], vs[r][:, kt, 32 * hd:32 * hd + 32],
                                     p[s % 3][:, hd, q0(s):512], start=(kt == 0), stop=(kt == 4 * h + 3),
                                     skip_group_check=True)
                last.then_inc(pv_done, 1)

            def unit(n, r, rnd, ahead, far):
                pe.wait_ge(loaded[r], LOADED * rnd + LOADED)
                if softmax:
                    pe.wait_ge(rows_loaded[r], 32 * rnd + 32)
                    if ahead:
                        rn = (r + 1) % RING
                        pe.wait_ge(loaded[rn], LOADED * (rnd + (r + 1) // RING) + LOADED)
                for s in range(STEPS):
                    scores(n, r, s)
                    if s:
                        weigh(n, r, s - 1)
                    if softmax and ahead:
                        maximum_scores(n + 1, (r + 1) % RING, BY[s], BY[s + 1])
                        if s == STEPS - 1:
                            turn_rows(n + 1)
                weigh(n, r, STEPS - 1)

            if softmax:
                pe.wait_ge(loaded[0], LOADED)
                maximum_scores(0, 0, 0, CH)
                turn_rows(0)
            all_units(pe, unit)



def mix_pass(nc, z, m, wo, den_eps):
    tag = "m0" if den_eps is None else "m1"
    G, DC, GROUPS = z.G, z.DC, z.TILES // z.G
    with ExitStack() as ctx:
        def sb(name, shape, dt=F32):
            return [ctx.enter_context(nc.sbuf_tensor(f"{tag}_{name}{u}", shape, dt)) for u in range(2)]

        num, den, att = sb("num", [P, DC, z.GT]), sb("den", [P, DC, z.GT]), sb("att", [P, DC, z.GT])
        raw, mv, sd, rs = sb("raw", [P, G, 6]), sb("mv", [P, G, 2]), sb("sd", [P, G]), sb("rs", [P, G])
        zt = sb("zt", [P, G, z.D])
        loaded = sems(nc, f"{tag}_loaded0", f"{tag}_loaded1")
        (padded, inverted, att_ready, y_ready, raw_done, mv_ready, sd_ready, rs_ready, zt_ready, added) = sems(
            nc, *[f"{tag}_{x}" for x in ("padded", "inverted", "att_ready", "y_ready", "raw_done", "mv_ready",
                                              "sd_ready", "rs_ready", "zt_ready", "added")])
        block = ctx.enter_context(nc.Block())
        LOADED = 16 * 2 * DC

        def banks(u):
            return [m.psum[:, 2 * u + t // 2, (t % 2) * z.D:(t % 2 + 1) * z.D] for t in range(G)]

        @block.sync
        def _(sp):
            with sp.Fori(0, GROUPS // 2) as i:
                for u in range(2):
                    n = 2 * i + u
                    sp.wait_ge(att_ready, n + 1)
                    for c in range(DC):
                        for k, dst in enumerate((num, den)):
                            sp.dma_start(dst[u][:, c, :], m.o_dram[k, bass.ds(z.D * i + P * c, P), u * z.GT:(u + 1) * z.GT]
                                         ).then_inc(loaded[u], 16)

        @block.vector
        def _(dve):
            dve.sem_inc(att_ready, 2)
            dve.sem_inc(zt_ready, 2)

            def divide(i, u):
                n = 2 * i + u
                dve.wait_ge(loaded[u], LOADED * i + LOADED)
                if den_eps is not None:
                    dve.tensor_scalar(den[u][:, :, :], den[u][:, :, :], den_eps, None, ALU.add).then_inc(padded, 1)
                    dve.wait_ge(padded, n + 1)
                dve.reciprocal(den[u][:, :, :], den[u][:, :, :]).then_inc(inverted, 1)
                dve.wait_ge(inverted, n + 1)
                dve.wait_ge(y_ready, n + 1)
                dve.tensor_tensor(att[u][:, :, :], num[u][:, :, :], den[u][:, :, :], ALU.mult).then_inc(att_ready, 1)

            staggered(dve, GROUPS, divide, lambda i, u: norm_sums(m, dve, banks(u), raw[u], mv[u], sd[u], rs[u], zt[u], y_ready,
                      raw_done, mv_ready, sd_ready, rs_ready, added, zt_ready, 2 * i + u, 2))

        @block.gpsimd
        def _(pool):
            add_to_x(pool, z, m, zt, zt_ready, added, GROUPS)

        @block.scalar
        def _(act):
            with act.Fori(0, GROUPS // 2) as i:
                for u in range(2):
                    deviation(act, mv[u], sd[u], m.eps, mv_ready, sd_ready, 2 * i + u)

        @block.tensor
        def _(pe):
            pe.sem_inc(y_ready, 2)
            with pe.Fori(0, GROUPS // 2) as i:
                for u in range(2):
                    n = 2 * i + u
                    pe.wait_ge(att_ready, n + 3)
                    pe.wait_ge(zt_ready, n + 1)
                    for t, bank in enumerate(banks(u)):
                        for c in range(DC):
                            last = pe.matmul(bank, att[u][:, c, t * P:(t + 1) * P], wo[:, c, :], start=(c == 0),
                                             stop=(c == DC - 1))
                    last.then_inc(y_ready, 1)


def norm_sums(m, dve, banks, raw, mv, sd, rs, zt, y_ready, raw_done, mv_ready, sd_ready, rs_ready, added, zt_ready, n,
              credit, gain=None):
    dve.wait_ge(y_ready, n + 1 + credit)
    statistics(m, dve, banks, raw, mv, raw_done, mv_ready, n)
    inverse(dve, sd, rs, sd_ready, rs_ready, n)
    if gain:
        factor, gained, ready = gain
        dve.tensor_scalar(gained[:, :], rs[:, :], factor, None, ALU.mult).then_inc(ready, 1)
        dve.wait_ge(ready, n + 1)
        rs = gained
    dve.wait_ge(added, n + 1)
    normalise(dve, zt, banks, mv, rs).then_inc(zt_ready, 1)


def add_to_x(pool, z, m, zt, zt_ready, added, groups, credit=2):
    pool.sem_inc(added, 2)
    with pool.Fori(0, groups // 2) as i:
        for u in range(2):
            n = 2 * i + u
            wait_alone(pool, zt_ready, n + 1 + credit, m.alone)
            x = m.x[:, bass.ts(n, z.G), :]
            pool.tensor_tensor(x, x, zt[u][:, :, :], ALU.add).then_inc(added, 1)



def mlp_pass(nc, z, m):
    G, DC, HC, GROUPS = z.G, z.DC, z.HC, z.TILES // z.G
    with ExitStack() as ctx:
        def sb(name, shape, dt=F32, n=2):
            return [ctx.enter_context(nc.sbuf_tensor(f"f_{name}{u}", shape, dt)) for u in range(n)]

        raw, mv, sd, rs = sb("raw", [P, G, 6]), sb("mv", [P, G, 2]), sb("sd", [P, G]), sb("rs", [P, G])
        raw2, mv2, sd2, rs2 = sb("raw2", [P, G, 6]), sb("mv2", [P, G, 2]), sb("sd2", [P, G]), sb("rs2", [P, G])
        xn, xt, zt = sb("xn", [P, G, z.D]), sb("xt", [P, DC, z.GT]), sb("zt", [P, G, z.D])
        relu, hid = sb("relu", [P, z.GT], n=4), sb("hid", [P, HC, z.GT])
        (raw_done, mv_ready, sd_ready, rs_ready, xn_ready, turned, xt_ready, fc_ready, relu_ready, hid_ready, y_ready,
         raw2_done, mv2_ready, sd2_ready, rs2_ready, zt_ready, added) = sems(nc, *["f_" + x for x in (
             "raw_done", "mv_ready", "sd_ready", "rs_ready", "xn_ready", "turned", "xt_ready", "fc_ready", "relu_ready",
             "hid_ready", "y_ready", "raw2_done", "mv2_ready", "sd2_ready", "rs2_ready", "zt_ready", "added")])
        block = ctx.enter_context(nc.Block())
        T0, F0, Y0 = 0, 2, 6
        banks = [m.psum[:, Y0 + t // 2, (t % 2) * z.D:(t % 2 + 1) * z.D] for t in range(G)]

        @block.vector
        def _(dve):
            dve.sem_inc(hid_ready, 4)
            dve.sem_inc(zt_ready, 1)

            def norm(i, u):
                n = 2 * i + u
                tiles = of_group(z, m.x, n)
                statistics(m, dve, tiles, raw[u], mv[u], raw_done, mv_ready, n)
                inverse(dve, sd[u], rs[u], sd_ready, rs_ready, n)
                dve.wait_ge(turned, n + 1)
                normalise(dve, xn[u], tiles, mv[u], rs[u]).then_inc(xn_ready, 1)

            def square(i, u):
                n = 2 * i + u
                dve.wait_ge(y_ready, n + 1)
                for j in range(HC):
                    dve.wait_ge(relu_ready, HC * n + j + 5)
                    dve.tensor_tensor(hid[u][:, j, :], relu[j % 4][:, :], relu[j % 4][:, :], ALU.mult).then_inc(hid_ready, 1)

            def out(i, u):
                norm_sums(m, dve, banks, raw2[u], mv2[u], sd2[u], rs2[u], zt[u], y_ready, raw2_done, mv2_ready, sd2_ready,
                          rs2_ready, added, zt_ready, 2 * i + u, 2)

            for u in range(2):
                norm(0, u)
            with dve.Fori(0, GROUPS // 2 - 1) as i:
                for u in range(2):
                    square(i, u)
                    norm(i + 1, u)
                    out(i, u)
            for u in range(2):
                square(GROUPS // 2 - 1, u)
                out(GROUPS // 2 - 1, u)

        @block.gpsimd
        def _(pool):
            add_to_x(pool, z, m, zt, zt_ready, added, GROUPS, credit=1)

        @block.scalar
        def _(act):
            act.sem_inc(xt_ready, 1)
            act.sem_inc(relu_ready, 4)

            def root(i, u):
                deviation(act, mv[u], sd[u], m.eps, mv_ready, sd_ready, 2 * i + u)

            def take_turned(i, u):
                n = 2 * i + u
                act.wait_ge(turned, n + 3)
                act.wait_ge(fc_ready, HC * n + HC)
                for c in range(DC):
                    last = act.activation(xt[u][:, c, :], m.bank[T0 + c], ACT.Copy)
                last.then_inc(xt_ready, 1)

            def rectify(i, u):
                n = 2 * i + u
                for j in range(HC):
                    act.wait_ge(fc_ready, HC * n + j + 1 + 2 * HC)
                    act.wait_ge(hid_ready, HC * n + j + 1)
                    act.activation(relu[j % 4][:, :], m.bank[F0 + j % 4], ACT.Relu).then_inc(relu_ready, 1)

            def root2(i, u):
                deviation(act, mv2[u], sd2[u], m.eps, mv2_ready, sd2_ready, 2 * i + u)

            for u in range(2):
                root(0, u)
                take_turned(0, u)
            with act.Fori(0, GROUPS // 2 - 1) as i:
                for u in range(2):
                    rectify(i, u)
                    root(i + 1, u)
                    take_turned(i + 1, u)
                    root2(i, u)
            for u in range(2):
                rectify(GROUPS // 2 - 1, u)
                root2(GROUPS // 2 - 1, u)

        @block.tensor
        def _(pe):
            pe.sem_inc(turned, 2)
            pe.sem_inc(fc_ready, 2 * HC)
            pe.sem_inc(y_ready, 2)

            def turn(i, u):
                n = 2 * i + u
                pe.wait_ge(xn_ready, n + 1)
                pe.wait_ge(xt_ready, n + 1)
                turn_group(pe, z, m.bank[T0:T0 + DC], xn[u], m.ident).then_inc(turned, 1)

            def hidden(i, u):
                n = 2 * i + u
                pe.wait_ge(xt_ready, n + 2)
                for j in range(HC):
                    pe.wait_ge(relu_ready, HC * n + j + 1)
                    for c in range(DC):
                        last = pe.matmul(m.bank[F0 + j % 4], m.w_fc[:, c, j * P:(j + 1) * P], xt[u][:, c, :],
                                         start=(c == 0), stop=(c == DC - 1))
                    last.then_inc(fc_ready, 1)

            def project(i, u):
                n = 2 * i + u
                pe.wait_ge(zt_ready, n + 1)
                pe.wait_ge(hid_ready, HC * n + HC + 4)
                for t, bank in enumerate(banks):
                    for j in range(HC):
                        last = pe.matmul(bank, hid[u][:, j, t * P:(t + 1) * P], m.w_proj[:, j, :], start=(j == 0),
                                         stop=(j == HC - 1))
                last.then_inc(y_ready, 1)

            for u in range(2):
                turn(0, u)
            with pe.Fori(0, GROUPS // 2 - 1) as i:
                for u in range(2):
                    hidden(i, u)
                    turn(i + 1, u)
                    project(i, u)
            for u in range(2):
                hidden(GROUPS // 2 - 1, u)
                project(GROUPS // 2 - 1, u)



def features_pass(nc, z, m):
    G, DC, GROUPS, H2 = z.G, z.DC, z.TILES // z.G, 2 * z.H
    W = 2 * z.D
    with ExitStack() as ctx:
        def sb(name, shape, dt=F32):
            return [ctx.enter_context(nc.sbuf_tensor(f"g_{name}{u}", shape, dt)) for u in range(2)]

        raw, mv, sd, rs = sb("raw", [P, G, 6]), sb("mv", [P, G, 2]), sb("sd", [P, G]), sb("rs", [P, G])
        xn, xt = sb("xn", [P, G, z.D]), sb("xt", [P, DC, z.GT])
        qk, sq = sb("qk", [P, G, W]), sb("sq", [P, W])
        var, hsd, hrs = sb("var", [P, G, H2]), sb("hsd", [P, G, H2]), sb("hrs", [P, G, H2])
        feat = sb("feat", [P, 4, z.GT])
        parts = sb("parts", [P, PARTS, 4, z.GT], BF16)
        rest = ctx.enter_context(nc.sbuf_tensor("g_rest", [P, 4, z.GT], F32))
        vx = sb("vx", [P, G, z.H, 32])
        stored = sems(nc, "g_stored0", "g_stored1")
        (raw_done, mv_ready, sd_ready, rs_ready, xn_ready, turned, xt_ready, qk_ready, qk_taken, sq_ready, var_ready,
         hsd_ready, hrs_ready, qn_ready, ft_ready, feat_ready, high_done, rest_done, mid_done, low_done, v_ready,
         vx_ready, ones_ready) = sems(nc, *["g_" + x for x in (
             "raw_done", "mv_ready", "sd_ready", "rs_ready", "xn_ready", "turned", "xt_ready", "qk_ready", "qk_taken",
             "sq_ready", "var_ready", "hsd_ready", "hrs_ready", "qn_ready", "ft_ready", "feat_ready", "high_done",
             "rest_done", "mid_done", "low_done", "v_ready", "vx_ready", "ones_ready")])
        block = ctx.enter_context(nc.Block())
        T0, Q0, VB, F0 = 0, 2, 4, 5
        STORED = 16 * (PARTS * 4 + G)

        @block.sync
        def _(sp):
            for u in range(2):
                sp.sem_inc(stored[u], STORED)
            with sp.Fori(0, GROUPS // 2) as i:
                for u in range(2):
                    n = 2 * i + u
                    sp.wait_ge(vx_ready, 2 * n + 3)
                    for t in range(G):
                        at = u * z.GT + t * P
                        sp.dma_start(m.v_dram[bass.ts(i, z.UPB), at:at + P, :].rearrange("g p k -> p g k"),
                                     vx[u][:, t, :, :].rearrange("p (g h) k -> p g (h k)", g=z.UPB)).then_inc(stored[u], 16)
                    sp.wait_ge(low_done, n + 2)
                    store_parts(sp, z, m, parts[u], stored[u], i, u)
            for u in range(2):
                sp.wait_ge(stored[u], STORED * (GROUPS // 2 + 1))

        @block.vector
        def _(dve):
            for u in range(2):
                last = dve.memset(vx[u][:, :, :, 16:32], 1.0)
            last.then_inc(ones_ready, 1)
            dve.sem_inc(var_ready, 2)
            dve.sem_inc(rest_done, 2)

            def norm(i, u):
                n = 2 * i + u
                tiles = of_group(z, m.x, n)
                statistics(m, dve, tiles, raw[u], mv[u], raw_done, mv_ready, n)
                inverse(dve, sd[u], rs[u], sd_ready, rs_ready, n)
                dve.wait_ge(turned, n + 1)
                normalise(dve, xn[u], tiles, mv[u], rs[u]).then_inc(xn_ready, 1)

            def scale_heads(i, u):
                n = 2 * i + u
                for t in range(G):
                    dve.wait_ge(sq_ready, G * n + t + 1)
                    dve.tensor_reduce(var[u][:, t, :], sq[t % 2][:, :].rearrange("p (h f) -> p h f", f=z.DK), AX.X,
                                      ALU.add).then_inc(var_ready, 1)
                dve.wait_ge(hsd_ready, n + 1)
                dve.reciprocal(hrs[u][:, :, :], hsd[u][:, :, :]).then_inc(hrs_ready, 1)
                dve.wait_ge(hrs_ready, n + 1)
                for t in range(G):
                    view = qk[u][:, t, :].rearrange("p (h f) -> p h f", f=z.DK)
                    last = dve.tensor_tensor(view, view, hrs[u][:, t, :].unsqueeze(2).to_broadcast([P, H2, z.DK]), ALU.mult)
                last.then_inc(qn_ready, 1)

            def split(i, u):
                n = 2 * i + u
                dve.wait_ge(feat_ready, 4 * n + 6)
                dve.wait_ge(stored[u], STORED * i + STORED)
                dve.tensor_copy(parts[u][:, 0, :, :], feat[u][:, :, :]).then_inc(high_done, 1)
                dve.wait_ge(high_done, n + 1)
                dve.wait_ge(low_done, n + 1)
                dve.tensor_tensor(rest[:, :, :], feat[u][:, :, :], parts[u][:, 0, :, :], ALU.subtract).then_inc(rest_done, 1)

            for u in range(2):
                norm(0, u)
            with dve.Fori(0, GROUPS // 2 - 1) as i:
                for u in range(2):
                    scale_heads(i, u)
                    norm(i + 1, u)
                    split(i, u)
            for u in range(2):
                scale_heads(GROUPS // 2 - 1, u)
                split(GROUPS // 2 - 1, u)

        @block.gpsimd
        def _(pool):
            pool.sem_inc(low_done, 1)
            with pool.Fori(0, GROUPS // 2) as i:
                for u in range(2):
                    n = 2 * i + u
                    wait_alone(pool, rest_done, n + 3, m.alone)
                    split_rest(pool, parts[u], rest, mid_done, low_done, n)

        @block.scalar
        def _(act):
            act.sem_inc(xt_ready, 1)
            act.sem_inc(qk_taken, 2)
            act.sem_inc(feat_ready, 2)
            act.sem_inc(vx_ready, 1)

            def root(i, u):
                deviation(act, mv[u], sd[u], m.eps, mv_ready, sd_ready, 2 * i + u)

            def take_turned(i, u):
                n = 2 * i + u
                act.wait_ge(turned, n + 3)
                act.wait_ge(v_ready, 2 * n + 2)
                for c in range(DC):
                    last = act.activation(xt[u][:, c, :], m.bank[T0 + c], ACT.Copy)
                last.then_inc(xt_ready, 1)

            def take_heads(i, u):
                n = 2 * i + u
                act.wait_ge(ft_ready, 4 * n + 4)
                for t in range(G):
                    act.wait_ge(qk_ready, G * n + t + 1)
                    act.wait_ge(var_ready, G * n + t + 1)
                    act.activation(sq[t % 2][:, :], m.bank[Q0 + t % 2], ACT.Square).then_inc(sq_ready, 1)
                    act.activation(qk[u][:, t, :], m.bank[Q0 + t % 2], ACT.Copy).then_inc(qk_taken, 1)
                act.wait_ge(ones_ready, 1)
                act.wait_ge(stored[u], STORED * i + STORED)
                for k in range(2):
                    act.wait_ge(v_ready, 2 * n + k + 5)
                    act.activation(vx[u][:, 2 * k:2 * k + 2, :, 0:16],
                                   m.bank[VB].rearrange("p (t h d) -> p t h d", t=2, d=16), ACT.Copy).then_inc(vx_ready, 1)
                act.wait_ge(var_ready, G * n + G + 2)
                act.activation(hsd[u][:, :, :], var[u][:, :, :], ACT.Sqrt, bias=m.eps[:, 0:1], scale=1.0 / z.DK
                               ).then_inc(hsd_ready, 1)

            def take_features(i, u):
                n = 2 * i + u
                act.wait_ge(rest_done, n + 1)
                for j in range(4):
                    act.wait_ge(ft_ready, 4 * n + j + 9)
                    act.activation(feat[u][:, j, :], m.bank[F0 + j % 2], ACT.Identity, bias=m.beta_col[:, 0:1],
                                   scale=m.gamma_col[:, 0:1]).then_inc(feat_ready, 1)

            for u in range(2):
                root(0, u)
                take_turned(0, u)
            with act.Fori(0, GROUPS // 2 - 1) as i:
                for u in range(2):
                    take_heads(i, u)
                    root(i + 1, u)
                    take_turned(i + 1, u)
                    take_features(i, u)
            for u in range(2):
                take_heads(GROUPS // 2 - 1, u)
                take_features(GROUPS // 2 - 1, u)

        @block.tensor
        def _(pe):
            pe.sem_inc(turned, 2)
            pe.sem_inc(v_ready, 4)
            pe.sem_inc(ft_ready, 8)

            def turn(i, u):
                n = 2 * i + u
                pe.wait_ge(xn_ready, n + 1)
                pe.wait_ge(xt_ready, n + 1)
                turn_group(pe, z, m.bank[T0:T0 + DC], xn[u], m.ident).then_inc(turned, 1)

            def project(i, u):
                n = 2 * i + u
                pe.wait_ge(xt_ready, n + 2)
                for t in range(G):
                    pe.wait_ge(qk_taken, G * n + t + 1)
                    for c in range(DC):
                        last = pe.matmul(m.bank[Q0 + t % 2], xt[u][:, c, t * P:(t + 1) * P], m.w_qkv[:, c, 0:W],
                                         start=(c == 0), stop=(c == DC - 1))
                    last.then_inc(qk_ready, 1)
                for k in range(2):
                    pe.wait_ge(vx_ready, 2 * n + k + 1)
                    for t in range(2):
                        for c in range(DC):
                            cols = slice((2 * k + t) * P, (2 * k + t + 1) * P)
                            last = pe.matmul(m.bank[VB][:, t * z.D:(t + 1) * z.D], xt[u][:, c, cols],
                                             m.w_qkv[:, c, W:W + z.D], start=(c == 0), stop=(c == DC - 1))
                    last.then_inc(v_ready, 1)

            def turn_features(i, u):
                n = 2 * i + u
                pe.wait_ge(qn_ready, n + 1)
                for j in range(4):
                    pe.wait_ge(feat_ready, 4 * n + j + 1)
                    for t in range(G):
                        last = pe.transpose(m.bank[F0 + j % 2][:, t * P:(t + 1) * P], qk[u][:, t, j * P:(j + 1) * P],
                                            m.ident[:, :])
                    last.then_inc(ft_ready, 1)

            for u in range(2):
                turn(0, u)
            with pe.Fori(0, GROUPS // 2 - 1) as i:
                for u in range(2):
                    project(i, u)
                    turn(i + 1, u)
                    turn_features(i, u)
            for u in range(2):
                project(GROUPS // 2 - 1, u)
                turn_features(GROUPS // 2 - 1, u)



def scale_pass(nc, z, m, normed):
    G, GROUPS = z.G, z.TILES // z.G
    with ExitStack() as ctx:
        def sb(name, shape, dt=F32):
            return [ctx.enter_context(nc.sbuf_tensor(f"s_{name}{u}", shape, dt)) for u in range(2)]

        raw, mv, sd, rs = sb("raw", [P, G, 6]), sb("mv", [P, G, 2]), sb("sd", [P, G]), sb("rs", [P, G])
        raw2, mv2, sd2, rs2 = sb("raw2", [P, G, 6]), sb("mv2", [P, G, 2]), sb("sd2", [P, G]), sb("rs2", [P, G])
        xn = sb("xn", [P, G, z.D])
        (raw_done, mv_ready, sd_ready, rs_ready, xn_ready, raw2_done, mv2_ready, sd2_ready, rs2_ready, inner_ready,
         gained, normed_ready, peaked) = sems(nc, *["s_" + x for x in (
             "raw_done", "mv_ready", "sd_ready", "rs_ready", "xn_ready", "raw2_done", "mv2_ready", "sd2_ready",
             "rs2_ready", "inner_ready", "gained", "normed_ready", "peaked")])
        block = ctx.enter_context(nc.Block())

        @block.vector
        def _(dve):
            def outer(i, u):
                n = 2 * i + u
                tiles = of_group(z, m.x, n)
                statistics(m, dve, tiles, raw[u], mv[u], raw_done, mv_ready, n)
                inverse(dve, sd[u], rs[u], sd_ready, rs_ready, n)
                normalise(dve, xn[u], tiles, mv[u], rs[u]).then_inc(xn_ready, 1)
                dve.wait_ge(xn_ready, n + 1)
                tiles = [xn[u][:, t, :] for t in range(G)]
                statistics(m, dve, tiles, raw2[u], mv2[u], raw2_done, mv2_ready, n)

            def inner(i, u):
                n = 2 * i + u
                inverse(dve, sd2[u], rs2[u], sd2_ready, rs2_ready, n)
                for t, dst in enumerate(of_group(z, normed, n)):
                    last = dve.tensor_scalar(dst, xn[u][:, t:t + 1, :], mv2[u][:, t, 0:1], rs2[u][:, t:t + 1],
                                             ALU.subtract, ALU.mult)
                last.then_inc(inner_ready, 1)

            def largest(n):
                dve.wait_ge(normed_ready, n + 1)
                dve.tensor_reduce(m.peaks[:, bass.ds(n, 1)], normed[:, bass.ts(n, G), :], AX.XY, ALU.max,
                                  apply_absolute_value=True).then_inc(peaked, 1)

            for u in range(2):
                outer(0, u)
            with dve.Fori(0, GROUPS // 2 - 1) as i:
                for u in range(2):
                    inner(i, u)
                    outer(i + 1, u)
                for u in range(2):
                    largest(2 * i + u)
            for u in range(2):
                inner(GROUPS // 2 - 1, u)
            for u in range(2):
                largest(GROUPS - 2 + u)

        @block.gpsimd
        def _(pool):
            with pool.Fori(0, GROUPS // 2) as i:
                for u in range(2):
                    n = 2 * i + u
                    wait_alone(pool, inner_ready, n + 1, m.alone)
                    view = normed[:, bass.ts(n, G), :]
                    pool.tensor_tensor(view, view, m.ln_gamma[:, :].unsqueeze(1).to_broadcast([P, G, z.D]),
                                       ALU.mult).then_inc(gained, 1)
                    wait_alone(pool, gained, n + 1, m.alone)
                    pool.tensor_tensor(view, view, m.ln_beta[:, :].unsqueeze(1).to_broadcast([P, G, z.D]),
                                       ALU.add).then_inc(normed_ready, 1)

        @block.scalar
        def _(act):
            def root(i, u):
                deviation(act, mv[u], sd[u], m.eps, mv_ready, sd_ready, 2 * i + u)

            def root2(i, u):
                deviation(act, mv2[u], sd2[u], m.eps_in, mv2_ready, sd2_ready, 2 * i + u)

            with act.Fori(0, GROUPS // 2) as i:
                for u in range(2):
                    root(i, u)
                    root2(i, u)



def ternary_pass(nc, z, m, normed, out):
    G, DC, GROUPS = z.G, z.DC, z.TILES // z.G
    QB, EPS = 128.0, 1e-5
    og = out.rearrange("b s d -> (b s) d").rearrange("(n p) d -> p n d", p=P)
    with ExitStack() as ctx:
        def sb(name, shape, dt=F32):
            return [ctx.enter_context(nc.sbuf_tensor(f"t_{name}{u}", shape, dt)) for u in range(2)]

        raw, mv, sd, rs = sb("raw", [P, G, 6]), sb("mv", [P, G, 2]), sb("sd", [P, G]), sb("rs", [P, G])
        grs, xt, zt = sb("grs", [P, G]), sb("xt", [P, DC, z.GT]), sb("zt", [P, G, z.D])
        cap_in = sb("cap_in", [P, G, z.D])
        one = lambda name: ctx.enter_context(nc.sbuf_tensor("t_" + name, [P, 1], F32))
        peak, gamma, inv, factor, gain, gain2 = (one(x) for x in ("peak", "gamma", "inv", "factor", "gain", "gain2"))
        stored = sems(nc, "t_stored0", "t_stored1")
        (peak_ready, gamma_ready, setup, capped, turned, xt_ready, y_ready, raw_done, mv_ready, sd_ready, rs_ready,
         grs_ready, zt_ready, added) = sems(nc, *["t_" + x for x in (
             "peak_ready", "gamma_ready", "setup", "capped", "turned", "xt_ready", "y_ready", "raw_done", "mv_ready",
             "sd_ready", "rs_ready", "grs_ready", "zt_ready", "added")])
        block = ctx.enter_context(nc.Block())
        T0 = 0
        SETUP = 6

        def banks(u):
            return [m.psum[:, 4 + 2 * u + t // 2, (t % 2) * z.D:(t % 2 + 1) * z.D] for t in range(G)]

        @block.sync
        def _(sp):
            with sp.Fori(0, GROUPS // 2) as i:
                for u in range(2):
                    n = 2 * i + u
                    sp.wait_ge(added, n + 3)
                    sp.dma_start(og[:, bass.ts(n, G), :], m.x[:, bass.ts(n, G), :]).then_inc(stored[u], 16)
            for u in range(2):
                sp.wait_ge(stored[u], 16 * (GROUPS // 2))

        @block.vector
        def _(dve):
            count = [0]

            def did(ins):
                count[0] += 1
                ins.then_inc(setup, 1)
                dve.wait_ge(setup, count[0])

            dve.tensor_reduce(peak[:, :], m.peaks[:, :], AX.X, ALU.max).then_inc(peak_ready, 1)
            dve.wait_ge(gamma_ready, 1)
            did(dve.reciprocal(inv[:, :], gamma[:, :]))
            did(dve.tensor_scalar(factor[:, :], inv[:, :], QB, None, ALU.mult))
            did(dve.tensor_scalar(gain[:, :], gamma[:, :], m.w_mean[:, 0:1], None, ALU.mult))
            did(dve.tensor_scalar(gain[:, :], gain[:, :], 1.0 / QB, None, ALU.mult))
            did(dve.tensor_tensor(gain2[:, :], gain[:, :], gain[:, :], ALU.mult))
            dve.sem_inc(setup, 1)
            dve.sem_inc(xt_ready, 2)
            dve.sem_inc(zt_ready, 2)

            def cap(i, u):
                n = 2 * i + u
                dve.wait_ge(turned, n + 1)
                dve.tensor_scalar(cap_in[u][:, :, :], normed[:, bass.ts(n, G), :], factor[:, 0:1], QB - EPS, ALU.mult,
                                  ALU.min).then_inc(capped, 1)

            def floor(i, u):
                n = 2 * i + u
                dve.wait_ge(turned, n + 3)
                dve.wait_ge(y_ready, n + 1)
                for c in range(DC):
                    last = dve.tensor_scalar(xt[u][:, c, :], m.bank[T0 + 2 * u + c], EPS - QB, None, ALU.max)
                last.then_inc(xt_ready, 1)

            def back(i, u):
                floor(i, u)
                norm_sums(m, dve, banks(u), raw[u], mv[u], sd[u], rs[u], zt[u], y_ready, raw_done, mv_ready, sd_ready,
                          rs_ready, added, zt_ready, 2 * i + u, 2, gain=(gain[:, 0:1], grs[u], grs_ready))

            staggered(dve, GROUPS, cap, back)

        @block.gpsimd
        def _(pool):
            pool.wait_ge(peak_ready, 1)
            pool.partition_all_reduce(gamma[:, :], peak[:, :], P, bass.bass_isa.ReduceOp.max).then_inc(gamma_ready, 1)
            add_to_x(pool, z, m, zt, zt_ready, added, GROUPS)

        @block.scalar
        def _(act):
            act.wait_ge(setup, SETUP)
            with act.Fori(0, GROUPS // 2) as i:
                for u in range(2):
                    deviation(act, mv[u], sd[u], m.eps, mv_ready, sd_ready, 2 * i + u, scale=gain2[:, 0:1])

        @block.tensor
        def _(pe):
            pe.sem_inc(y_ready, 2)
            pe.sem_inc(turned, 2)

            def turn(i, u):
                n = 2 * i + u
                pe.wait_ge(capped, n + 1)
                pe.wait_ge(xt_ready, n + 1)
                for c in range(DC):
                    for t in range(G):
                        src = cap_in[u][:, t, c * P:(c + 1) * P]
                        last = pe.transpose(m.bank[T0 + 2 * u + c][:, t * P:(t + 1) * P], src, m.ident[:, :])
                last.then_inc(turned, 1)

            def project(i, u):
                n = 2 * i + u
                pe.wait_ge(xt_ready, n + 3)
                pe.wait_ge(zt_ready, n + 1)
                for t, bank in enumerate(banks(u)):
                    for c in range(DC):
                        last = pe.matmul(bank, xt[u][:, c, t * P:(t + 1) * P], m.w_ter[:, c, :], start=(c == 0),
                                         stop=(c == DC - 1))
                last.then_inc(y_ready, 1)

            staggered(pe, GROUPS, turn, project, behind_first=True)


_INS = ['L0_attn_x', 'L0_attn_W_dq', 'L0_attn_W_uq', 'L0_attn_W_dkv', 'L0_attn_W_uk', 'L0_attn_W_uv', 'L0_attn_W_o',
        'L0_ffn_fast_b', 'L0_ffn_w_fc', 'L0_ffn_w_proj', 'L0_ffn_u', 'L0_ffn_v', 'L0_ffn_gate', 'L1_attn_Wq',
        'L1_attn_Wk', 'L1_attn_Wv', 'L1_attn_Wo', 'L1_attn_gamma', 'L1_attn_beta', 'L1_ffn_weight',
        'L1_ffn_ln_gamma', 'L1_ffn_ln_beta']


def kernel(**inputs):
    import numpy as _np
    import concourse.bacc as _bacc
    from concourse.bass_utils import run_bass_kernel_spmd as _run

    nc = _bacc.Bacc("TRN2", target_bir_lowering=False, num_devices=1)
    arrays, aps = {}, {}
    for name in _INS:
        a = _np.ascontiguousarray(inputs[name]).reshape(_np.shape(inputs[name]) or (1,))
        arrays[f"in_{name}"] = a
        aps[name] = nc.dram_tensor(f"in_{name}", a.shape, mybir.dt.from_np(a.dtype), kind="ExternalInput").ap()
    out = nc.dram_tensor("out_0", arrays["in_L0_attn_x"].shape, F32, kind="ExternalOutput").ap()
    build(nc, aps, out)
    r = _run(nc, [arrays], core_ids=[0])
    return r.results[0]["out_0"]
```

```python
from contextlib import ExitStack

import concourse.bass as bass
from concourse import mybir

F32 = mybir.dt.float32
BF16 = mybir.dt.bfloat16
ALU = mybir.AluOpType
ACT = mybir.ActivationFunctionType
AX = mybir.AxisListType

P = 128
EPS = 1e-5
EPS_IN = 1e-3
NEG = -3.0e38
PARTS = 3
Q_STACK = ((0, 0, 3), (1, 0, 2), (2, 0, 1))
K_STACK = ((0, 1, 3), (0, 1, 2), (0, 1, 1))
STACK = 16 * 6


class Sizes:
    def __init__(self, x, w_dq, w_fc):
        self.B, self.S, self.D = x.shape
        self.C = w_dq.shape[1]
        self.HID = w_fc.shape[0]
        self.DK = 16
        self.H = self.D // self.DK
        self.DC = self.D // P
        self.HC = self.HID // P
        self.TILES = self.B * self.S // P
        self.G = 4
        self.GT = self.G * P
        self.HPU = 4
        self.UPB = self.H // self.HPU
        self.UNITS = self.B * self.UPB
        self.ST = self.S // P
        assert self.S == 2 * self.GT and 2 * self.C == P and self.DC == 2 and self.H * self.DK == self.D


def build(nc, a, out):
    z = Sizes(a["L0_attn_x"], a["L0_attn_W_dq"], a["L0_ffn_w_fc"])
    with ExitStack() as ctx:
        m = Resident(nc, ctx, z)

        def run(one_pass, *args, **settings):
            with nc.cleanup_on_exit():
                one_pass(nc, z, m, *args, **settings)

        run(weights_pass, a)
        run(latent_pass)
        run(attend_pass, softmax=True)
        run(mix_pass, m.wo0, None)
        run(mlp_pass)
        run(features_pass)
        run(attend_pass, softmax=False)
        run(mix_pass, m.wo1, 1e-5)
        with nc.sbuf_tensor("normed", [P, z.TILES, z.D], F32) as normed:
            run(scale_pass, normed)
            run(ternary_pass, normed, out)


class Resident:

    def __init__(self, nc, ctx, z):
        def sb(name, shape, dt=F32):
            return ctx.enter_context(nc.sbuf_tensor(name, shape, dt))

        self.x = sb("x", [P, z.TILES, z.D])
        self.ident = sb("ident", [P, P])
        self.ident16 = sb("ident16", [P, P], BF16)
        self.eps = sb("eps", [P, 1])
        self.eps_both = sb("eps_both", [P, 1])
        self.w_down = sb("w_down", [P, z.DC, P])
        self.w_uq = sb("w_uq", [P, z.D])
        self.w_uk = sb("w_uk", [P, z.D])
        self.w_uv = sb("w_uv", [P, z.D])
        self.wo0 = sb("wo0", [P, z.DC, z.D])
        self.wo1 = sb("wo1", [P, z.DC, z.D])
        self.w_fc = sb("w_fc", [P, z.DC, z.HID])
        self.w_proj = sb("w_proj", [P, z.HC, z.D])
        self.w_qkv = sb("w_qkv", [P, z.DC, 3 * z.D])
        self.w_ter = sb("w_ter", [P, z.DC, z.D])
        self.gamma_col = sb("gamma_col", [P, 1])
        self.beta_col = sb("beta_col", [P, 1])
        self.ln_gamma = sb("ln_gamma", [P, z.D])
        self.ln_beta = sb("ln_beta", [P, z.D])
        self.peaks = sb("peaks", [P, z.TILES // z.G])
        self.w_mean = sb("w_mean", [P, 1])
        self.psum = ctx.enter_context(nc.psum_tensor("psum", [P, 8, 512], F32))
        self.bank = [self.psum[:, i, :] for i in range(8)]
        self.alone = ctx.enter_context(nc.semaphore("alone"))
        self.qk_dram = nc.dram_tensor("qk_parts", [PARTS, 2, z.B * z.D, z.S], BF16, kind="Internal").ap()
        self.v_dram = nc.dram_tensor("values", [z.UNITS, z.S, P], F32, kind="Internal").ap()
        self.sums_dram = nc.dram_tensor("sums", [z.B * z.H * 32, z.S], F32, kind="Internal").ap()
        self.inv_dram = nc.dram_tensor("reciprocals", [z.B * z.H, z.S], F32, kind="Internal").ap()


def sems(nc, *names):
    return [nc.alloc_semaphore(n) for n in names]



def wait_alone(eng, sem, value, alone):
    eng.wait_ge(sem, value)
    eng.sem_inc(alone, 1)


def statistics(m, dve, tiles, raw, mv, raw_done, mv_ready, n):
    for t, tile in enumerate(tiles):
        last = dve.bn_stats(raw[:, t, :], tile)
    last.then_inc(raw_done, 1)
    wait_alone(dve, raw_done, n + 1, m.alone)
    for t in range(len(tiles)):
        last = dve.bn_aggr(mv[:, t, :], raw[:, t, :])
    last.then_inc(mv_ready, 1)


def deviation(act, mv, sd, eps, mv_ready, sd_ready, n, scale=1.0):
    act.wait_ge(mv_ready, n + 1)
    act.activation(sd[:, :], mv[:, :, 1], ACT.Sqrt, bias=eps[:, 0:1], scale=scale).then_inc(sd_ready, 1)


def inverse(dve, sd, rs, sd_ready, rs_ready, n):
    dve.wait_ge(sd_ready, n + 1)
    dve.reciprocal(rs[:, :], sd[:, :]).then_inc(rs_ready, 1)
    dve.wait_ge(rs_ready, n + 1)


def normalise(dve, out, tiles, mv, rs):
    for t, tile in enumerate(tiles):
        last = dve.tensor_scalar(out[:, t, :], tile, mv[:, t, 0:1], rs[:, t:t + 1], ALU.subtract, ALU.mult)
    return last


def turn_group(pe, z, banks, src, ident):
    for c in range(z.DC):
        for t in range(z.G):
            last = pe.transpose(banks[c][:, t * P:(t + 1) * P], src[:, t, c * P:(c + 1) * P], ident[:, :])
    return last


def staggered(eng, groups, ahead, behind, behind_first=False):
    for u in range(2):
        ahead(0, u)
    with eng.Fori(0, groups // 2 - 1) as i:
        for u in range(2):
            if behind_first:
                behind(i, u)
            ahead(i + 1, u)
            if not behind_first:
                behind(i, u)
    for u in range(2):
        behind(groups // 2 - 1, u)


def three_stages(eng, groups, order):
    rounds = groups // 2

    def round_of(i, has_last, has_now, has_next):
        for u in range(2):
            order(lambda fn: fn(i - 1, u) if has_last else None, lambda fn: fn(i, u) if has_now else None,
                  lambda fn: fn(i + 1, u) if has_next else None)

    round_of(-1, False, False, True)
    round_of(0, False, True, True)
    with eng.Fori(1, rounds - 1) as i:
        round_of(i, True, True, True)
    round_of(rounds - 1, True, True, False)
    round_of(rounds, True, False, False)


def of_group(z, x, n):
    return [x[:, bass.ds(n * z.G + t, 1), :] for t in range(z.G)]



def weights_pass(nc, z, m, a):
    with ExitStack() as ctx:
        def sb(name, shape, dt=F32):
            return ctx.enter_context(nc.sbuf_tensor(name, shape, dt))

        rank = a["L0_ffn_u"].shape[1]
        fc = sb("fc", [P, z.HC, z.D])
        proj = sb("proj", [P, z.DC, z.HID])
        qkv = sb("qkv", [P, 3, z.DC, z.D])
        wo = sb("wo", [P, z.DC, z.D])
        ter = sb("ter", [P, z.DC, z.D])
        u = sb("u", [P, z.HC, rank])
        fast = sb("fast", [rank, rank])
        v = sb("v", [rank, z.D])
        gate = sb("gate", [rank, 1])
        uq = sb("uq", [P, z.D])
        fast_t = sb("fast_t", [rank, rank])
        fv = sb("fv", [rank, z.D])
        u_t = sb("u_t", [rank, z.HID])
        sums = sb("sums_w", [P, z.HC + z.DC + 1])
        scale = sb("scale", [P, z.HC + z.DC])
        half = sb("half", [P, z.HC + z.DC + 1])
        nhalf = sb("nhalf", [P, z.HC + z.DC + 1])
        fc_w = sb("fc_w", [P, z.HC, z.D])
        proj_w = sb("proj_w", [P, z.DC, z.HID])
        neg = sb("neg", [P, z.HC * z.D])
        means = sb("means", [P, z.DC * 2 * z.H])
        total = sb("total", [P, 1])
        (loaded, x_loaded, ident_zero, ident_ready, zeros_ready, step, pe_step, drained, total_ready, total_in) = sems(
            nc, "w_loaded", "w_x_loaded", "w_ident_zero", "w_ident_ready", "w_zeros_ready", "w_dve_step", "w_pe_step",
            "w_drained", "w_total_ready", "w_total_in")
        block = ctx.enter_context(nc.Block())
        chunks = lambda w: w.rearrange("(c p) n -> p c n", p=P)
        loads = [
            (fc[:, :, :], chunks(a["L0_ffn_w_fc"])), (proj[:, :, :], chunks(a["L0_ffn_w_proj"])),
            (qkv[:, 0, :, :], chunks(a["L1_attn_Wq"])), (qkv[:, 1, :, :], chunks(a["L1_attn_Wk"])),
            (qkv[:, 2, :, :], chunks(a["L1_attn_Wv"])), (wo[:, :, :], chunks(a["L1_attn_Wo"])),
            (ter[:, :, :], chunks(a["L1_ffn_weight"])), (u[:, :, :], chunks(a["L0_ffn_u"])),
            (fast[:, :], a["L0_ffn_fast_b"]), (v[:, :], a["L0_ffn_v"]),
            (gate[:, :], a["L0_ffn_gate"].partition_broadcast(rank)),
            (m.w_down[:, :, 0:z.C], chunks(a["L0_attn_W_dq"])), (m.w_down[:, :, z.C:P], chunks(a["L0_attn_W_dkv"])),
            (uq[0:z.C, :], a["L0_attn_W_uq"]), (uq[z.C:P, :], a["L0_attn_W_uk"]),
            (m.w_uv[z.C:P, :], a["L0_attn_W_uv"]), (m.wo0[:, :, :], chunks(a["L0_attn_W_o"])),
            (m.ln_gamma[:, :], a["L1_ffn_ln_gamma"].partition_broadcast(P)),
            (m.ln_beta[:, :], a["L1_ffn_ln_beta"].partition_broadcast(P)),
        ]
        for row in range(0, P, z.HPU * z.DK):
            for column, name in ((m.gamma_col, "L1_attn_gamma"), (m.beta_col, "L1_attn_beta")):
                src = a[name].unsqueeze(1).unsqueeze(2).to_broadcast([z.DK, z.HPU, 1])
                loads.append((column[row:row + z.HPU * z.DK, :], src))

        @block.sync
        def _(sp):
            for dst, src in loads:
                sp.dma_start(dst, src).then_inc(loaded, 16)
            for b in range(z.B):
                sp.dma_start(m.x[:, b * z.ST:(b + 1) * z.ST, :], a["L0_attn_x"][b].rearrange("(n p) d -> p n d", p=P)
                             ).then_inc(x_loaded, 16)
            sp.wait_ge(x_loaded, 16 * z.B)

        @block.gpsimd
        def _(pool):
            pool.memset(m.ident[:, :], 0.0).then_inc(ident_zero, 1)
            pool.memset(m.ident16[:, :], 0.0).then_inc(ident_zero, 1)
            pool.wait_ge(ident_zero, 2)
            for t in (m.ident, m.ident16):
                pool.affine_select(out=t[:, :], in_=t[:, :], compare_op=ALU.not_equal, fill=1.0, base=0,
                                   pattern=[[-1, P]], channel_multiplier=1).then_inc(ident_ready, 1)
            pool.wait_ge(total_in, 1)
            pool.partition_all_reduce(total[:, :], sums[:, z.HC + z.DC:], P,
                                      bass.bass_isa.ReduceOp.add).then_inc(total_ready, 1)

        T_FC, T_PROJ, T_FAST = "fc", "proj", "fast"
        dve_done, pe_done = {}, {}

        @block.vector
        def _(dve):
            count = [0]

            def did(ins, name=None):
                count[0] += 1
                ins.then_inc(step, 1)
                dve.wait_ge(step, count[0])
                if name:
                    dve_done[name] = count[0]

            did(dve.memset(m.w_uq[z.C:P, :], 0.0))
            did(dve.memset(m.w_uk[0:z.C, :], 0.0))
            did(dve.memset(m.w_uv[0:z.C, :], 0.0))
            did(dve.memset(m.eps[:, :], EPS))
            did(dve.memset(m.eps_both[:, :], EPS * EPS_IN))
            dve.wait_ge(loaded, 16 * len(loads))
            for dst, rows in ((m.w_uq, slice(0, z.C)), (m.w_uk, slice(z.C, P))):
                did(dve.tensor_copy(dst[rows, :].rearrange("p (n d h) -> p n h d", d=z.DK, h=z.HPU),
                                    uq[rows, :].rearrange("p (n h d) -> p n h d", d=z.DK, h=z.HPU)))
            did(dve.tensor_reduce(sums[:, 0:z.HC], fc[:, :, :], AX.X, ALU.add, apply_absolute_value=True))
            did(dve.tensor_reduce(sums[:, z.HC:z.HC + z.DC], proj[:, :, :], AX.X, ALU.add, apply_absolute_value=True))
            did(dve.tensor_reduce(sums[:, z.HC + z.DC:], ter[:, :, :], AX.XY, ALU.add, apply_absolute_value=True))
            dve.sem_inc(total_in, 1)
            did(dve.tensor_scalar(scale[:, 0:z.HC], sums[:, 0:z.HC], 1.0 / z.D, 1e-5, ALU.mult, ALU.max))
            did(dve.tensor_scalar(scale[:, z.HC:], sums[:, z.HC:z.HC + z.DC], 1.0 / z.HID, 1e-5, ALU.mult, ALU.max))
            did(dve.tensor_scalar(half[:, 0:z.HC + z.DC], scale[:, :], 0.5, None, ALU.mult))
            did(dve.tensor_scalar(nhalf[:, 0:z.HC + z.DC], scale[:, :], -0.5, None, ALU.mult))
            for name, w, dst, rows, width, at in ((T_FC, fc, fc_w, z.HC, z.D, 0),
                                                  (T_PROJ, proj, proj_w, z.DC, z.HID, z.HC)):
                view = neg[:, :].rearrange("p (r w) -> p r w", r=rows)
                for r in range(rows):
                    k = at + r
                    dve.tensor_scalar(dst[:, r, :], w[:, r, :], half[:, k:k + 1], scale[:, k:k + 1], ALU.is_gt, ALU.mult)
                    last = dve.tensor_scalar(view[:, r, :], w[:, r, :], nhalf[:, k:k + 1], scale[:, k:k + 1],
                                             ALU.is_lt, ALU.mult)
                did(last)
                did(dve.tensor_tensor(dst[:, :, :], dst[:, :, :], view, ALU.subtract), name)
            dve.wait_ge(total_ready, 1)
            k = z.HC + z.DC
            did(dve.tensor_scalar(m.w_mean[:, :], total[:, :], 1.0 / (z.D * z.D), None, ALU.mult))
            did(dve.tensor_scalar(half[:, k:k + 1], m.w_mean[:, :], 1e-5, 0.5, ALU.add, ALU.mult))
            did(dve.tensor_scalar(nhalf[:, k:k + 1], half[:, k:k + 1], -1.0, None, ALU.mult))
            did(dve.tensor_scalar(neg[:, 0:z.DC * z.D], ter[:, :, :].rearrange("p c n -> p (c n)"),
                                  nhalf[:, k:k + 1], None, ALU.is_lt))
            did(dve.scalar_tensor_tensor(out=m.w_ter[:, :, :].rearrange("p c n -> p (c n)"),
                                         in0=ter[:, :, :].rearrange("p c n -> p (c n)"), scalar=half[:, k:k + 1],
                                         in1=neg[:, 0:z.DC * z.D], op0=ALU.is_gt, op1=ALU.subtract))

            got = [0]

            def take(name=None, fn=None):
                got[0] += 1
                dve.wait_ge(pe_step, got[0])
                fn().then_inc(drained, 1)
                dve.wait_ge(drained, got[0])
                if name:
                    pe_done[name] = got[0]

            take("fast_t", lambda: dve.tensor_copy(fast_t[:, :], m.bank[0][0:rank, 0:rank]))
            take("fv", lambda: dve.tensor_scalar(fv[:, :], m.bank[1][0:rank, 0:z.D], gate[:, 0:1], None, ALU.mult))
            for k in range(2):
                take("u_t", lambda: dve.tensor_copy(u_t[:, k * 512:(k + 1) * 512], m.bank[2 + k][0:rank, :]))
            for n, (c, k) in enumerate((c, k) for c in range(z.DC) for k in range(z.HID // 512)):
                dst = m.w_fc[:, c, k * 512:(k + 1) * 512]
                take(None, lambda: dve.tensor_copy(dst, m.bank[4][:, :]))
                take("fc", lambda: dve.tensor_tensor(dst, dst, m.bank[5][:, :], ALU.add))
            for g in range(z.HC // 2):
                take("proj", lambda: dve.tensor_copy(m.w_proj[:, 2 * g:2 * g + 2, :],
                                                     m.bank[6 + g % 2][:, :].rearrange("p (j n) -> p j n", j=2)))
            for w in range(4):
                dst = m.w_qkv[:, :, w * z.D:(w + 1) * z.D] if w < 3 else m.wo1[:, :, :]
                take("qkv", lambda: dve.tensor_copy(dst, m.bank[w][:, :].rearrange("p (c n) -> p c n", c=z.DC)))
            for c in range(z.DC):
                view = m.w_qkv[:, c, 0:2 * z.D].rearrange("p (h f) -> p h f", f=z.DK)
                mean = means[:, c * 2 * z.H:(c + 1) * 2 * z.H]
                did(dve.tensor_reduce(mean, view, AX.X, ALU.add))
                did(dve.tensor_scalar(mean, mean, 1.0 / z.DK, None, ALU.mult))
                did(dve.tensor_tensor(view, view, mean.unsqueeze(2).to_broadcast([P, 2 * z.H, z.DK]), ALU.subtract))

        @block.tensor
        def _(pe):
            pe.wait_ge(loaded, 16 * len(loads))
            pe.wait_ge(ident_ready, 2)
            pe.transpose(m.bank[0][0:rank, 0:rank], fast[:, :], m.ident[0:rank, 0:rank]).then_inc(pe_step, 1)
            pe.wait_ge(drained, pe_done["fast_t"])
            pe.matmul(m.bank[1][0:rank, 0:z.D], fast_t[:, :], v[:, :], start=True, stop=True).then_inc(pe_step, 1)
            for k in range(2):
                for t in range(4):
                    last = pe.transpose(m.bank[2 + k][0:rank, t * P:(t + 1) * P], u[:, 4 * k + t, :], m.ident[:, :])
                last.then_inc(pe_step, 1)
            pe.wait_ge(drained, pe_done["u_t"])
            pe.wait_ge(step, dve_done[T_PROJ])
            done = pe_done["u_t"]
            for c in range(z.DC):
                for k in range(z.HID // 512):
                    for t in range(4):
                        last = pe.transpose(m.bank[4][:, t * P:(t + 1) * P],
                                            fc_w[:, 4 * k + t, c * P:(c + 1) * P], m.ident[:, :])
                    last.then_inc(pe_step, 1)
                    pe.matmul(m.bank[5][:, :], fv[:, c * P:(c + 1) * P], u_t[:, k * 512:(k + 1) * 512],
                              start=True, stop=True).then_inc(pe_step, 1)
                    done += 2
                    pe.wait_ge(drained, done)
            for g in range(z.HC // 2):
                if g >= 2:
                    pe.wait_ge(drained, done + g - 1)
                for j in range(2):
                    for c in range(z.DC):
                        col = j * z.D + c * P
                        last = pe.transpose(m.bank[6 + g % 2][:, col:col + P],
                                            proj_w[:, c, (2 * g + j) * P:(2 * g + j + 1) * P], m.ident[:, :])
                last.then_inc(pe_step, 1)
            for w in range(4):
                src = qkv[:, w, :, :] if w < 3 else wo[:, :, :]
                for c in range(z.DC):
                    for o in range(z.DC):
                        col = c * z.D + o * P
                        last = pe.transpose(m.bank[w][:, col:col + P], src[:, o, c * P:(c + 1) * P], m.ident[:, :])
                last.then_inc(pe_step, 1)



def latent_pass(nc, z, m):
    G, DC, GROUPS = z.G, z.DC, z.TILES // z.G
    with ExitStack() as ctx:
        def sb(name, shape, dt=F32):
            return [ctx.enter_context(nc.sbuf_tensor(f"l_{name}{u}", shape, dt)) for u in range(2)]

        raw, mv, sd, rs = sb("raw", [P, G, 6]), sb("mv", [P, G, 2]), sb("sd", [P, G]), sb("rs", [P, G])
        xn, xt, ct = sb("xn", [P, G, z.D]), sb("xt", [P, DC, z.GT]), sb("ct", [P, z.GT])
        parts, rest = sb("parts", [P, PARTS, 4, z.GT], BF16), sb("rest", [P, 4, z.GT])
        vx = sb("vx", [P, G, z.H, 32])
        stored = sems(nc, "l_stored0", "l_stored1")
        (raw_done, mv_ready, sd_ready, rs_ready, xn_ready, turned, xt_ready, c_ready, ct_ready, qk_ready,
         high_done, rest_done, mid_done, low_done, v_ready, vx_ready, ones_ready) = sems(
            nc, "l_raw_done", "l_mv_ready", "l_sd_ready", "l_rs_ready", "l_xn_ready", "l_turned", "l_xt_ready",
            "l_c_ready", "l_ct_ready", "l_qk_ready", "l_high_done", "l_rest_done", "l_mid_done", "l_low_done",
            "l_v_ready", "l_vx_ready", "l_ones_ready")
        block = ctx.enter_context(nc.Block())
        T0, CB, QK0, VB = 0, 2, 3, 7
        STORED = 16 * (PARTS * 4 + G)

        @block.sync
        def _(sp):
            for u in range(2):
                sp.sem_inc(stored[u], STORED)

            def store(i, u):
                n = 2 * i + u
                sp.wait_ge(vx_ready, 2 * n + 3)
                for t in range(G):
                    at = u * z.GT + t * P
                    sp.dma_start(m.v_dram[bass.ts(i, z.UPB), at:at + P, :].rearrange("g p k -> p g k"),
                                 vx[u][:, t, :, :].rearrange("p (g h) k -> p g (h k)", g=z.UPB)).then_inc(stored[u], 16)
                sp.wait_ge(low_done, n + 3)
                store_parts(sp, z, m, parts[u], stored[u], i, u)

            with sp.Fori(0, GROUPS // 2) as i:
                for u in range(2):
                    store(i, u)
            for u in range(2):
                sp.wait_ge(stored[u], STORED * (GROUPS // 2 + 1))

        @block.vector
        def _(dve):
            for u in range(2):
                last = dve.memset(vx[u][:, :, :, 16:32], 1.0)
            last.then_inc(ones_ready, 1)
            dve.sem_inc(rest_done, 4)

            def norm(i, u):
                n = 2 * i + u
                tiles = of_group(z, m.x, n)
                statistics(m, dve, tiles, raw[u], mv[u], raw_done, mv_ready, n)
                inverse(dve, sd[u], rs[u], sd_ready, rs_ready, n)
                dve.wait_ge(turned, n + 1)
                normalise(dve, xn[u], tiles, mv[u], rs[u]).then_inc(xn_ready, 1)

            def split(i, u):
                n = 2 * i + u
                dve.wait_ge(low_done, n + 1)
                for j in range(4):
                    dve.wait_ge(high_done, 4 * n + j + 1)
                    dve.tensor_tensor(rest[u][:, j, :], m.bank[QK0 + j][:, :], parts[u][:, 0, j, :],
                                      ALU.subtract).then_inc(rest_done, 1)
                    dve.wait_ge(rest_done, 4 * n + j + 5)
                    dve.tensor_copy(parts[u][:, 1, j, :], rest[u][:, j, :]).then_inc(mid_done, 1)

            staggered(dve, GROUPS, norm, split)

        @block.gpsimd
        def _(pool):
            pool.sem_inc(low_done, 2)
            with pool.Fori(0, GROUPS // 2) as i:
                for u in range(2):
                    n = 2 * i + u
                    for j in range(4):
                        wait_alone(pool, mid_done, 4 * n + j + 1, m.alone)
                        last = pool.tensor_tensor(parts[u][:, 2, j, :], rest[u][:, j, :], parts[u][:, 1, j, :],
                                                  ALU.subtract)
                    last.then_inc(low_done, 1)

        @block.scalar
        def _(act):
            act.sem_inc(xt_ready, 1)
            act.sem_inc(ct_ready, 1)
            act.sem_inc(vx_ready, 1)

            def root(i, u):
                deviation(act, mv[u], sd[u], m.eps, mv_ready, sd_ready, 2 * i + u)

            def take_turned(i, u):
                n = 2 * i + u
                act.wait_ge(turned, n + 3)
                act.wait_ge(c_ready, n + 1)
                for c in range(DC):
                    last = act.activation(xt[u][:, c, :], m.bank[T0 + c][:, :], ACT.Copy)
                last.then_inc(xt_ready, 1)

            def take_down(i, u):
                n = 2 * i + u
                act.wait_ge(c_ready, n + 3)
                act.wait_ge(v_ready, 2 * n + 2)
                act.activation(ct[u][:, :], m.bank[CB][:, :], ACT.Copy).then_inc(ct_ready, 1)

            def take_heads(i, u):
                n = 2 * i + u
                act.wait_ge(stored[u], STORED * i + STORED)
                for j in range(4):
                    act.wait_ge(qk_ready, 4 * n + j + 1)
                    act.activation(parts[u][:, 0, j, :], m.bank[QK0 + j][:, :], ACT.Copy).then_inc(high_done, 1)
                act.wait_ge(ones_ready, 1)
                for k in range(2):
                    act.wait_ge(v_ready, 2 * n + k + 5)
                    act.activation(vx[u][:, 2 * k:2 * k + 2, :, 0:16],
                                   m.bank[VB][:, :].rearrange("p (t h d) -> p t h d", t=2, d=16),
                                   ACT.Copy).then_inc(vx_ready, 1)

            for u in range(2):
                root(0, u)
                take_turned(0, u)
            with act.Fori(0, GROUPS // 2 - 1) as i:
                for u in range(2):
                    take_down(i, u)
                    root(i + 1, u)
                    take_heads(i, u)
                    take_turned(i + 1, u)
            for u in range(2):
                take_down(GROUPS // 2 - 1, u)
                take_heads(GROUPS // 2 - 1, u)

        @block.tensor
        def _(pe):
            pe.sem_inc(turned, 2)
            pe.sem_inc(c_ready, 2)
            pe.sem_inc(v_ready, 4)

            def turn(i, u):
                n = 2 * i + u
                pe.wait_ge(xn_ready, n + 1)
                pe.wait_ge(xt_ready, n + 1)
                turn_group(pe, z, m.bank[T0:T0 + DC], xn[u], m.ident).then_inc(turned, 1)

            def down(i, u):
                n = 2 * i + u
                pe.wait_ge(xt_ready, n + 2)
                pe.wait_ge(ct_ready, n + 1)
                for c in range(DC):
                    last = pe.matmul(m.bank[CB][:, :], m.w_down[:, c, :], xt[u][:, c, :], start=(c == 0), stop=(c == DC - 1))
                last.then_inc(c_ready, 1)

            def heads(i, u):
                n = 2 * i + u
                pe.wait_ge(ct_ready, n + 2)
                for j in range(4):
                    w = (m.w_uq, m.w_uk)[j // 2]
                    pe.wait_ge(rest_done, 4 * n + j + 1)
                    pe.matmul(m.bank[QK0 + j][:, :], w[:, (j % 2) * P:(j % 2 + 1) * P], ct[u][:, :],
                              start=True, stop=True).then_inc(qk_ready, 1)

            def values(i, u, k):
                n = 2 * i + u
                pe.wait_ge(vx_ready, 2 * n + k + 1)
                for t in range(2):
                    cols = slice((2 * k + t) * P, (2 * k + t + 1) * P)
                    last = pe.matmul(m.bank[VB][:, t * z.D:(t + 1) * z.D], ct[u][:, cols], m.w_uv[:, :],
                                     start=True, stop=True)
                last.then_inc(v_ready, 1)

            for u in range(2):
                turn(0, u)
            with pe.Fori(0, GROUPS // 2 - 1) as i:
                for u in range(2):
                    down(i, u)
                    heads(i, u)
                    values(i, u, 0)
                    turn(i + 1, u)
                    values(i, u, 1)
            for u in range(2):
                down(GROUPS // 2 - 1, u)
                heads(GROUPS // 2 - 1, u)
                for k in range(2):
                    values(GROUPS // 2 - 1, u, k)


def store_parts(eng, z, m, parts, stored, i, u):
    for part in range(PARTS):
        for j in range(4):
            eng.dma_start(m.qk_dram[part, j // 2, bass.ds(i * z.D + (j % 2) * P, P), u * z.GT:(u + 1) * z.GT],
                          parts[:, part, j, :]).then_inc(stored, 16)



def attend_pass(nc, z, m, softmax):
    tag = "a" if softmax else "b"
    RING = 3
    HPU, ST, UNITS = z.HPU, z.ST, z.UNITS
    ROUNDS = (UNITS - 2) // RING
    assert UNITS == RING * ROUNDS + 2
    ROWS = STACK + 2 if softmax else STACK
    steps = [(h, kt) for h in range(2) for kt in range(4 * (h + 1))]
    STEPS = len(steps)
    DIAG = [s for s, (h, kt) in enumerate(steps) if kt >= 4 * h]
    AHEAD = 2
    PAIRS = 2 if softmax else 3
    SLOTS = 4
    chunks = [(hd, pieces) for hd in range(HPU) for pieces in (
        ((0, 0, 0, 128), (2, 0, 128, 384)), ((3, 0, 0, 512),), ((1, 0, 0, 256), (5, 1, 256, 256)),
        ((4, 0, 0, 512),), ((4, 1, 0, 128), (6, 1, 128, 384)), ((5, 0, 0, 512),), ((6, 0, 0, 512),),
        ((7, 0, 0, 512),), ((7, 1, 0, 512),))]
    CH = len(chunks)
    assert CH == 3 * STEPS
    SRING = 3
    with ExitStack() as ctx:
        def sb(name, shape, dt=F32, n=1):
            return [ctx.enter_context(nc.sbuf_tensor(f"{tag}_{name}{u}", shape, dt)) for u in range(n)]

        def sm(*names):
            return sems(nc, *[f"{tag}_{x}" for x in names])

        qs, ks = sb("qs", [P, HPU, z.S], BF16, RING), sb("ks", [P, HPU, z.S], BF16, RING)
        vs = sb("vs", [P, ST, P], F32, RING)
        p = sb("p", [P, HPU, 512], F32, SLOTS)
        osb = sb("osb", [P, 512], F32, 2)
        loaded = sm(*[f"loaded{r}" for r in range(RING)])
        stored = sm("stored0", "stored1")
        st_ready, p_ready, masked, pv_done, o_taken = sm("st_ready", "p_ready", "masked", "pv_done", "o_taken")
        LOADED = 16 * (2 * len(Q_STACK) + 1)
        STORED = 16
        PV, PR, OT, STK, DR = SLOTS, PAIRS, 1, SRING, 2
        if softmax:
            bias, = sb("bias", [P, 512])
            dump = sb("dump", [P, 512], BF16, SRING)
            peak, = sb("peak", [P, HPU * ST, 2])
            npeak, = sb("npeak", [P, HPU * ST])
            split, = sb("split", [P, 2, HPU * ST], BF16)
            rows, = sb("rows", [P, 2, HPU * ST], BF16)
            rows_loaded = sm(*[f"rows_loaded{r}" for r in range(RING)])
            (bias_zero, bias_ready, peak_set, s_ready, s_taken, npeak_ready, high_ready, split_ready,
             rows_ready, ones_ready) = sm("bias_zero", "bias_ready", "peak_set", "s_ready", "s_taken", "npeak_ready",
                                          "high_ready", "split_ready", "rows_ready", "ones_ready")
            ROWS_LOADED = 16 * 8
        else:
            twin = sb("twin", [P, 512], F32, 2)
            twin_ready, d_ready = sm("twin_ready", "d_ready")
        block = ctx.enter_context(nc.Block())
        SB, OB = 4, 7

        def q0(s):
            h, kt = steps[s]
            return max(0, kt * P - h * 512)

        def score_bank(s, hd):
            return 2 * ((2 * s + hd // 2) % PAIRS) + hd % 2

        def all_units(eng, unit):
            with eng.Fori(0, ROUNDS) as i:
                for r in range(RING):
                    unit(RING * i + r, r, i, True, True)
            unit(UNITS - 2, 0, ROUNDS, True, False)
            unit(UNITS - 1, 1, ROUNDS, False, False)

        @block.sync
        def _(sp):
            for u in range(2):
                sp.sem_inc(stored[u], STORED)

            def load(n, r):
                for tile, which, stack in ((qs[r], 0, Q_STACK), (ks[r], 1, K_STACK)):
                    row = 0
                    for first, step, groups in stack:
                        last = first + step * (groups - 1) + 1
                        src = m.qk_dram[first:last, which, bass.ts(n, HPU * z.DK), :]
                        src = src.rearrange("g (d h) t -> g d (h t)", h=HPU)
                        if not step:
                            src = src.to_broadcast([groups, z.DK, HPU * z.S])
                        sp.dma_start(tile[row:row + 16 * groups, :, :].rearrange("p h t -> p (h t)"), src
                                     ).then_inc(loaded[r], 16)
                        row += 16 * groups
                sp.dma_start(vs[r][:, :, :], m.v_dram[bass.ts(n, 1), :, :].rearrange("n (k p) c -> p (n k) c", p=P)
                             ).then_inc(loaded[r], 16)

            def load_rows(n, r):
                sp.wait_ge(rows_ready, n + 1)
                for k in range(2):
                    at = qs[r][STACK + k:STACK + k + 1, :, :].rearrange("o h (q b i) -> o (h q) b i", b=4, i=32)
                    for b in range(4):
                        sp.dma_start(at[:, :, b, :], rows[32 * b:32 * b + 32, k, :]).then_inc(rows_loaded[r], 16)

            def store(n, h):
                sp.wait_ge(o_taken, 2 * n + h + 1 + OT)
                sp.dma_start(m.sums_dram[bass.ts(n, P), h * 512:(h + 1) * 512], osb[h][:, :]).then_inc(stored[h], 16)

            def unit(n, r, rnd, ahead, far):
                if far:
                    sp.wait_ge(pv_done, STEPS * n + PV)
                    load(n + 2, (r + 2) % RING)
                store(n, 0)
                if softmax and ahead:
                    load_rows(n + 1, (r + 1) % RING)
                store(n, 1)

            load(0, 0)
            load(1, 1)
            if softmax:
                load_rows(0, 0)
            all_units(sp, unit)
            for h in range(2):
                sp.wait_ge(stored[h], STORED * (UNITS + 1))

        @block.gpsimd
        def _(pool):
            if softmax:
                pool.memset(bias[:, :], 0.0).then_inc(bias_zero, 1)
                pool.wait_ge(bias_zero, 1)
                pool.affine_select(out=bias[:, 512 - P:], in_=bias[:, 512 - P:], compare_op=ALU.is_ge, fill=NEG,
                                   base=0, pattern=[[-1, P]], channel_multiplier=1).then_inc(bias_ready, 1)

            def unit(n, r, rnd, ahead, far):
                for d, s in enumerate(DIAG):
                    if not softmax:
                        pool.wait_ge(d_ready, STEPS * n + s + 1 + DR)
                    wait_alone(pool, p_ready, 2 * STEPS * n + 2 * s + 2 + PR, m.alone)
                    diag = p[s % SLOTS][:, :, q0(s):q0(s) + P]
                    pool.affine_select(out=diag, in_=diag, compare_op=ALU.is_ge, fill=0.0, base=0,
                                       pattern=[[0, HPU], [1, P]], channel_multiplier=-1).then_inc(masked, 1)

            all_units(pool, unit)

        @block.scalar
        def _(act):
            act.sem_inc(p_ready, PR)
            act.sem_inc(o_taken, OT)

            def take_sums(n, h):
                act.wait_ge(pv_done, STEPS * n + (4, STEPS)[h] + PV)
                act.wait_ge(stored[h], STORED * n + STORED)
                act.activation(osb[h][:, :], m.bank[OB], ACT.Copy).then_inc(o_taken, 1)

            def weights(n, s):
                act.wait_ge(pv_done, STEPS * n + s + 1)
                for k in range(2):
                    act.wait_ge(st_ready, 2 * STEPS * n + 2 * s + k + 1)
                    heads = 2 if softmax or k == 0 else 1
                    at = score_bank(s, 2 * k)
                    act.activation(p[s % SLOTS][:, 2 * k:2 * k + heads, q0(s):512], m.psum[:, at:at + heads, q0(s):512],
                                   ACT.Exp if softmax else ACT.Square, scale=z.DK ** -0.5).then_inc(p_ready, 1)

            def unit(n, r, rnd, ahead, far):
                for s in range(STEPS):
                    if s + AHEAD < STEPS:
                        weights(n, s + AHEAD)
                    elif ahead:
                        weights(n + 1, s + AHEAD - STEPS)
                    if s == 3:
                        take_sums(n, 0)
                take_sums(n, 1)

            for s in range(AHEAD):
                weights(0, s)
            all_units(act, unit)

        @block.vector
        def _(dve):
            if not softmax:
                dve.sem_inc(d_ready, DR)

                def unit(n, r, rnd, ahead, far):
                    for s in range(STEPS):
                        dve.wait_ge(st_ready, 2 * STEPS * n + 2 * s + 2)
                        bank = m.bank[score_bank(s, 3)][:, q0(s):512]
                        dve.tensor_copy(twin[s % 2][:, q0(s):512], bank).then_inc(twin_ready, 1)
                        dve.wait_ge(pv_done, STEPS * n + s + 1)
                        dve.wait_ge(twin_ready, STEPS * n + s + 1)
                        dve.scalar_tensor_tensor(out=p[s % SLOTS][:, 3, q0(s):512], in0=bank, scalar=1.0 / z.DK,
                                                 in1=twin[s % 2][:, q0(s):512], op0=ALU.mult, op1=ALU.mult
                                                 ).then_inc(d_ready, 1)

                all_units(dve, unit)
                return
            for r in range(RING):
                last = dve.memset(ks[r][STACK:STACK + 2, :, :], 1.0)
            last.then_inc(ones_ready, 1)
            dve.memset(peak[:, :, :], NEG).then_inc(peak_set, 1)
            dve.sem_inc(s_taken, STK)
            dve.wait_ge(peak_set, 1)
            dve.wait_ge(bias_ready, 1)

            def maxima(n, a, b):
                for c in range(a, b):
                    hd, pieces = chunks[c]
                    wait_alone(dve, s_ready, CH * n + c + 1, m.alone)
                    for qt, h, at, w in pieces:
                        piece, dst = m.bank[SB + c % SRING][:, at:at + w], peak[:, hd * ST + qt, h:h + 1]
                        if h < qt // 4:
                            last = dve.tensor_reduce(dst, piece, AX.X, ALU.max)
                        else:
                            last = dve.tensor_tensor_reduce(dump[c % SRING][:, at:at + w], piece, bias[:, 512 - w:], 1.0,
                                                            NEG, ALU.add, ALU.max, dst)
                    last.then_inc(s_taken, 1)

            def largest(n, before):
                dve.wait_ge(s_taken, CH * n + CH + STK)
                dve.tensor_reduce(npeak[:, :], peak[:, :, :], AX.X, ALU.max, negate=True).then_inc(npeak_ready, 1)
                dve.wait_ge(npeak_ready, n + 1)
                dve.tensor_copy(split[:, 0, :], npeak[:, :]).then_inc(high_ready, 1)
                dve.wait_ge(high_ready, n + 1)
                dve.tensor_tensor(split[:, 1, :], npeak[:, :], split[:, 0, :], ALU.subtract).then_inc(split_ready, 1)
                if before:
                    dve.wait_ge(*before)
                dve.wait_ge(split_ready, n + 1)
                dve.transpose(rows[:, :, :].rearrange("p k c -> p (k c)"), split[:, :, :].rearrange("p k c -> p (k c)")
                              ).then_inc(rows_ready, 1)

            def unit(n, r, rnd, ahead, far):
                if ahead:
                    maxima(n + 1, CH // 2, CH)
                    largest(n + 1, (rows_loaded[r], ROWS_LOADED * rnd + ROWS_LOADED))
                if far:
                    maxima(n + 2, 0, CH // 2)

            maxima(0, 0, CH)
            largest(0, None)
            maxima(1, 0, CH // 2)
            all_units(dve, unit)

        @block.tensor
        def _(pe):
            pe.sem_inc(pv_done, PV)
            if softmax:
                pe.wait_ge(ones_ready, 1)

            def maximum_scores(n, r, a, b):
                for c in range(a, b):
                    hd, pieces = chunks[c]
                    pe.wait_ge(s_taken, CH * n + c + 1)
                    for qt, h, at, w in pieces:
                        last = pe.matmul(m.bank[SB + c % SRING][:, at:at + w], qs[r][0:STACK, hd, qt * P:(qt + 1) * P],
                                         ks[r][0:STACK, hd, h * 512:h * 512 + w], start=True, stop=True)
                    last.then_inc(s_ready, 1)

            def scores(n, r, s, k):
                h, kt = steps[s]
                pe.wait_ge(p_ready, 2 * STEPS * n + 2 * s + k + 1)
                if not softmax and k == 0:
                    pe.wait_ge(d_ready, STEPS * n + s + 1)
                for hd in (2 * k, 2 * k + 1):
                    last = pe.matmul(m.bank[score_bank(s, hd)][:, q0(s):512], ks[r][0:ROWS, hd, kt * P:(kt + 1) * P],
                                     qs[r][0:ROWS, hd, h * 512 + q0(s):(h + 1) * 512], start=True, stop=True)
                last.then_inc(st_ready, 1)

            def weigh(n, r, s):
                h, kt = steps[s]
                pe.wait_ge(p_ready, 2 * STEPS * n + 2 * s + 2 + PR)
                if not softmax:
                    pe.wait_ge(d_ready, STEPS * n + s + 1 + DR)
                if s in DIAG:
                    pe.wait_ge(masked, len(DIAG) * n + DIAG.index(s) + 1)
                if kt == 0:
                    pe.wait_ge(o_taken, 2 * n + h + 1)
                for hd in range(HPU):
                    last = pe.matmul(m.bank[OB][32 * hd:32 * hd + 32, q0(s):512], vs[r][:, kt, 32 * hd:32 * hd + 32],
                                     p[s % SLOTS][:, hd, q0(s):512], start=(kt == 0), stop=(kt == 4 * h + 3),
                                     skip_group_check=True)
                last.then_inc(pv_done, 1)

            def operands(n, r, rnd):
                pe.wait_ge(loaded[r], LOADED * rnd + LOADED)
                if softmax:
                    pe.wait_ge(rows_loaded[r], ROWS_LOADED * rnd + ROWS_LOADED)

            def unit(n, r, rnd, ahead, far):
                def some_maxima(k):
                    if not softmax:
                        return
                    half = CH // 2
                    if k < half and ahead:
                        maximum_scores(n + 1, (r + 1) % RING, half + k, half + k + 1)
                    if k >= half and far:
                        if k == half:
                            pe.wait_ge(loaded[(r + 2) % RING], LOADED * (rnd + (r + 2) // RING) + LOADED)
                        maximum_scores(n + 2, (r + 2) % RING, k - half, k - half + 1)

                for s in range(STEPS):
                    t = s + AHEAD
                    there = t < STEPS or ahead
                    if t == STEPS and ahead:
                        operands(n + 1, (r + 1) % RING, rnd + (r + 1) // RING)
                    at = (n, r, t) if t < STEPS else (n + 1, (r + 1) % RING, t - STEPS)
                    if there:
                        scores(*at, 0)
                    some_maxima(3 * s)
                    if there:
                        scores(*at, 1)
                    some_maxima(3 * s + 1)
                    weigh(n, r, s)
                    some_maxima(3 * s + 2)

            if softmax:
                pe.wait_ge(loaded[0], LOADED)
                maximum_scores(0, 0, 0, CH)
                pe.wait_ge(loaded[1], LOADED)
                maximum_scores(1, 1, 0, CH // 2)
            operands(0, 0, 0)
            for s in range(AHEAD):
                for k in range(2):
                    scores(0, 0, s, k)
            all_units(pe, unit)



def mix_pass(nc, z, m, wo, den_eps):
    tag = "m0" if den_eps is None else "m1"
    G, DC, GROUPS = z.G, z.DC, z.TILES // z.G
    with ExitStack() as ctx:
        def sb(name, shape, dt=F32):
            return [ctx.enter_context(nc.sbuf_tensor(f"{tag}_{name}{u}", shape, dt)) for u in range(2)]

        num, inv, att = sb("num", [P, DC, z.GT]), sb("inv", [P, DC, z.GT]), sb("att", [P, DC, z.GT])
        dens = ctx.enter_context(nc.sbuf_tensor(f"{tag}_dens", [P, z.S], F32))
        raw, mv, sd, rs = sb("raw", [P, G, 6]), sb("mv", [P, G, 2]), sb("sd", [P, G]), sb("rs", [P, G])
        zt = sb("zt", [P, G, z.D])
        loaded = sems(nc, f"{tag}_loaded0", f"{tag}_loaded1")
        (dens_loaded, padded, inverted, inv_stored, att_ready, y_ready, raw_done, mv_ready, sd_ready, rs_ready,
         zt_ready, added) = sems(nc, *[f"{tag}_{x}" for x in (
             "dens_loaded", "padded", "inverted", "inv_stored", "att_ready", "y_ready", "raw_done", "mv_ready",
             "sd_ready", "rs_ready", "zt_ready", "added")])
        block = ctx.enter_context(nc.Block())
        HPC = P // z.DK
        LOADED = 16 * 2 * DC
        assert z.B * z.H == P

        def banks(u):
            return [m.psum[:, 2 * u + t // 2, (t % 2) * z.D:(t % 2 + 1) * z.D] for t in range(G)]

        @block.sync
        def _(sp):
            heads = m.sums_dram.rearrange("(h k) t -> h k t", k=32)
            sp.dma_start(dens[:, :], heads[:, z.DK, :]).then_inc(dens_loaded, 16)
            sp.wait_ge(inverted, 1)
            sp.dma_start(m.inv_dram, dens[:, :]).then_inc(inv_stored, 16)
            sp.wait_ge(inv_stored, 16)
            with sp.Fori(0, GROUPS // 2) as i:
                for u in range(2):
                    n = 2 * i + u
                    sp.wait_ge(att_ready, n + 1)
                    for c in range(DC):
                        src = heads[bass.ds(z.H * i + HPC * c, HPC), 0:z.DK, u * z.GT:(u + 1) * z.GT]
                        sp.dma_start(num[u][:, c, :], src).then_inc(loaded[u], 16)
                        rows = m.inv_dram[bass.ds(z.H * i + HPC * c, HPC), u * z.GT:(u + 1) * z.GT]
                        sp.dma_start(inv[u][:, c, :], rows.unsqueeze(1).to_broadcast([HPC, z.DK, z.GT])
                                     ).then_inc(loaded[u], 16)

        @block.vector
        def _(dve):
            dve.sem_inc(zt_ready, 2)
            dve.wait_ge(dens_loaded, 16)
            if den_eps is not None:
                dve.tensor_scalar(dens[:, :], dens[:, :], den_eps, None, ALU.add).then_inc(padded, 1)
                dve.wait_ge(padded, 1)
            dve.reciprocal(dens[:, :], dens[:, :]).then_inc(inverted, 1)
            with dve.Fori(0, GROUPS // 2) as i:
                for u in range(2):
                    norm_sums(m, dve, banks(u), raw[u], mv[u], sd[u], rs[u], zt[u], y_ready, raw_done, mv_ready,
                              sd_ready, rs_ready, added, zt_ready, 2 * i + u, 2)

        @block.gpsimd
        def _(pool):
            pool.sem_inc(added, 2)
            pool.sem_inc(att_ready, 2)

            def divide(i, u):
                n = 2 * i + u
                pool.wait_ge(y_ready, n + 1)
                pool.wait_ge(loaded[u], LOADED * i + LOADED)
                pool.sem_inc(m.alone, 1)
                pool.tensor_tensor(att[u][:, :, :], num[u][:, :, :], inv[u][:, :, :], ALU.mult).then_inc(att_ready, 1)

            staggered(pool, GROUPS, divide, lambda i, u: add_group(pool, z, m, zt, zt_ready, added, i, u, 2))

        @block.scalar
        def _(act):
            with act.Fori(0, GROUPS // 2) as i:
                for u in range(2):
                    deviation(act, mv[u], sd[u], m.eps, mv_ready, sd_ready, 2 * i + u)

        @block.tensor
        def _(pe):
            pe.sem_inc(y_ready, 2)
            with pe.Fori(0, GROUPS // 2) as i:
                for u in range(2):
                    n = 2 * i + u
                    pe.wait_ge(att_ready, n + 3)
                    pe.wait_ge(zt_ready, n + 1)
                    for t, bank in enumerate(banks(u)):
                        for c in range(DC):
                            last = pe.matmul(bank, att[u][:, c, t * P:(t + 1) * P], wo[:, c, :], start=(c == 0),
                                             stop=(c == DC - 1))
                    last.then_inc(y_ready, 1)


def norm_sums(m, dve, banks, raw, mv, sd, rs, zt, y_ready, raw_done, mv_ready, sd_ready, rs_ready, added, zt_ready, n,
              credit, gain=None):
    dve.wait_ge(y_ready, n + 1 + credit)
    statistics(m, dve, banks, raw, mv, raw_done, mv_ready, n)
    inverse(dve, sd, rs, sd_ready, rs_ready, n)
    if gain:
        factor, gained, ready = gain
        dve.tensor_scalar(gained[:, :], rs[:, :], factor, None, ALU.mult).then_inc(ready, 1)
        dve.wait_ge(ready, n + 1)
        rs = gained
    dve.wait_ge(added, n + 1)
    normalise(dve, zt, banks, mv, rs).then_inc(zt_ready, 1)


def add_group(pool, z, m, zt, zt_ready, added, i, u, credit):
    n = 2 * i + u
    wait_alone(pool, zt_ready, n + 1 + credit, m.alone)
    x = m.x[:, bass.ts(n, z.G), :]
    pool.tensor_tensor(x, x, zt[u][:, :, :], ALU.add).then_inc(added, 1)


def add_to_x(pool, z, m, zt, zt_ready, added, groups, credit=2):
    pool.sem_inc(added, 2)
    with pool.Fori(0, groups // 2) as i:
        for u in range(2):
            add_group(pool, z, m, zt, zt_ready, added, i, u, credit)



def mlp_pass(nc, z, m):
    G, DC, HC, GROUPS = z.G, z.DC, z.HC, z.TILES // z.G
    with ExitStack() as ctx:
        def sb(name, shape, dt=F32, n=2):
            return [ctx.enter_context(nc.sbuf_tensor(f"f_{name}{u}", shape, dt)) for u in range(n)]

        raw, mv, sd, rs = sb("raw", [P, G, 6]), sb("mv", [P, G, 2]), sb("sd", [P, G]), sb("rs", [P, G])
        raw2, mv2, sd2, rs2 = sb("raw2", [P, G, 6]), sb("mv2", [P, G, 2]), sb("sd2", [P, G]), sb("rs2", [P, G])
        xn, xt, zt = sb("xn", [P, G, z.D]), sb("xt", [P, DC, z.GT]), sb("zt", [P, G, z.D])
        relu, hid = sb("relu", [P, z.GT], n=4), sb("hid", [P, HC, z.GT])
        (raw_done, mv_ready, sd_ready, rs_ready, xn_ready, turned, xt_ready, fc_ready, relu_ready, hid_ready, y_ready,
         raw2_done, mv2_ready, sd2_ready, rs2_ready, zt_ready, added) = sems(nc, *["f_" + x for x in (
             "raw_done", "mv_ready", "sd_ready", "rs_ready", "xn_ready", "turned", "xt_ready", "fc_ready", "relu_ready",
             "hid_ready", "y_ready", "raw2_done", "mv2_ready", "sd2_ready", "rs2_ready", "zt_ready", "added")])
        block = ctx.enter_context(nc.Block())
        T0, F0, Y0 = 0, 2, 6
        banks = [m.psum[:, Y0 + t // 2, (t % 2) * z.D:(t % 2 + 1) * z.D] for t in range(G)]

        @block.vector
        def _(dve):
            dve.sem_inc(hid_ready, 4)
            dve.sem_inc(zt_ready, 1)

            def norm(i, u):
                n = 2 * i + u
                tiles = of_group(z, m.x, n)
                statistics(m, dve, tiles, raw[u], mv[u], raw_done, mv_ready, n)
                inverse(dve, sd[u], rs[u], sd_ready, rs_ready, n)
                dve.wait_ge(turned, n + 1)
                normalise(dve, xn[u], tiles, mv[u], rs[u]).then_inc(xn_ready, 1)

            def square(i, u):
                n = 2 * i + u
                dve.wait_ge(y_ready, n + 1)
                for j in range(HC):
                    dve.wait_ge(relu_ready, HC * n + j + 5)
                    dve.tensor_tensor(hid[u][:, j, :], relu[j % 4][:, :], relu[j % 4][:, :], ALU.mult).then_inc(hid_ready, 1)

            def out(i, u):
                norm_sums(m, dve, banks, raw2[u], mv2[u], sd2[u], rs2[u], zt[u], y_ready, raw2_done, mv2_ready, sd2_ready,
                          rs2_ready, added, zt_ready, 2 * i + u, 2)

            for u in range(2):
                norm(0, u)
            square(0, 0)
            with dve.Fori(0, GROUPS // 2 - 1) as i:
                norm(i + 1, 0)
                square(i, 1)
                out(i, 0)
                norm(i + 1, 1)
                square(i + 1, 0)
                out(i, 1)
            square(GROUPS // 2 - 1, 1)
            for u in range(2):
                out(GROUPS // 2 - 1, u)

        @block.gpsimd
        def _(pool):
            add_to_x(pool, z, m, zt, zt_ready, added, GROUPS, credit=1)

        @block.scalar
        def _(act):
            act.sem_inc(xt_ready, 1)
            act.sem_inc(relu_ready, 4)

            def root(i, u):
                deviation(act, mv[u], sd[u], m.eps, mv_ready, sd_ready, 2 * i + u)

            def take_turned(i, u):
                n = 2 * i + u
                act.wait_ge(turned, n + 3)
                act.wait_ge(fc_ready, HC * n + HC)
                for c in range(DC):
                    last = act.activation(xt[u][:, c, :], m.bank[T0 + c], ACT.Copy)
                last.then_inc(xt_ready, 1)

            def rectify(i, u):
                n = 2 * i + u
                for j in range(HC):
                    act.wait_ge(fc_ready, HC * n + j + 1 + 2 * HC)
                    act.wait_ge(hid_ready, HC * n + j + 1)
                    act.activation(relu[j % 4][:, :], m.bank[F0 + j % 4], ACT.Relu).then_inc(relu_ready, 1)

            def root2(i, u):
                deviation(act, mv2[u], sd2[u], m.eps, mv2_ready, sd2_ready, 2 * i + u)

            for u in range(2):
                root(0, u)
                take_turned(0, u)
            rectify(0, 0)
            with act.Fori(0, GROUPS // 2 - 1) as i:
                root(i + 1, 0)
                rectify(i, 1)
                take_turned(i + 1, 0)
                root2(i, 0)
                root(i + 1, 1)
                rectify(i + 1, 0)
                take_turned(i + 1, 1)
                root2(i, 1)
            rectify(GROUPS // 2 - 1, 1)
            for u in range(2):
                root2(GROUPS // 2 - 1, u)

        @block.tensor
        def _(pe):
            pe.sem_inc(turned, 2)
            pe.sem_inc(fc_ready, 2 * HC)
            pe.sem_inc(y_ready, 2)

            def turn(i, u):
                n = 2 * i + u
                pe.wait_ge(xn_ready, n + 1)
                pe.wait_ge(xt_ready, n + 1)
                turn_group(pe, z, m.bank[T0:T0 + DC], xn[u], m.ident).then_inc(turned, 1)

            def hidden(i, u):
                n = 2 * i + u
                pe.wait_ge(xt_ready, n + 2)
                for j in range(HC):
                    pe.wait_ge(relu_ready, HC * n + j + 1)
                    for c in range(DC):
                        last = pe.matmul(m.bank[F0 + j % 4], m.w_fc[:, c, j * P:(j + 1) * P], xt[u][:, c, :],
                                         start=(c == 0), stop=(c == DC - 1))
                    last.then_inc(fc_ready, 1)

            def project(i, u):
                n = 2 * i + u
                pe.wait_ge(zt_ready, n + 1)
                pe.wait_ge(hid_ready, HC * n + HC + 4)
                for t, bank in enumerate(banks):
                    for j in range(HC):
                        last = pe.matmul(bank, hid[u][:, j, t * P:(t + 1) * P], m.w_proj[:, j, :], start=(j == 0),
                                         stop=(j == HC - 1))
                last.then_inc(y_ready, 1)

            for u in range(2):
                turn(0, u)
            hidden(0, 0)
            with pe.Fori(0, GROUPS // 2 - 1) as i:
                hidden(i, 1)
                turn(i + 1, 0)
                project(i, 0)
                hidden(i + 1, 0)
                turn(i + 1, 1)
                project(i, 1)
            hidden(GROUPS // 2 - 1, 1)
            for u in range(2):
                project(GROUPS // 2 - 1, u)



def features_pass(nc, z, m):
    G, DC, GROUPS, H2 = z.G, z.DC, z.TILES // z.G, 2 * z.H
    W = 2 * z.D
    with ExitStack() as ctx:
        def sb(name, shape, dt=F32):
            return [ctx.enter_context(nc.sbuf_tensor(f"g_{name}{u}", shape, dt)) for u in range(2)]

        raw, mv, sd, rs = sb("raw", [P, G, 6]), sb("mv", [P, G, 2]), sb("sd", [P, G]), sb("rs", [P, G])
        xn, xt = sb("xn", [P, G, z.D]), sb("xt", [P, DC, z.GT])
        qk, sq = sb("qk", [P, G, W]), sb("sq", [P, W])
        var, hsd, hrs = sb("var", [P, G, H2]), sb("hsd", [P, G, H2]), sb("hrs", [P, G, H2])
        feat = sb("feat", [P, 4, z.GT])
        parts = sb("parts", [P, PARTS, 4, z.GT], BF16)
        rest = ctx.enter_context(nc.sbuf_tensor("g_rest", [P, 4, z.GT], F32))
        vx = sb("vx", [P, G, z.H, 32])
        v_stored, stored = sems(nc, "g_v_stored0", "g_v_stored1"), sems(nc, "g_stored0", "g_stored1")
        (raw_done, mv_ready, sd_ready, rs_ready, xn_ready, turned, xt_ready, qk_ready, qk_taken, sq_ready, var_ready,
         hsd_ready, hrs_ready, qn_ready, ft_ready, feat_ready, high_done, rest_done, mid_done, low_done, v_ready,
         vx_ready, ones_ready) = sems(nc, *["g_" + x for x in (
             "raw_done", "mv_ready", "sd_ready", "rs_ready", "xn_ready", "turned", "xt_ready", "qk_ready", "qk_taken",
             "sq_ready", "var_ready", "hsd_ready", "hrs_ready", "qn_ready", "ft_ready", "feat_ready", "high_done",
             "rest_done", "mid_done", "low_done", "v_ready", "vx_ready", "ones_ready")])
        block = ctx.enter_context(nc.Block())
        T0, Q0, VB, F0 = 0, 2, 4, 5
        V_STORED, STORED = 16 * G, 16 * PARTS * 4

        @block.sync
        def _(sp):
            for u in range(2):
                sp.sem_inc(v_stored[u], V_STORED)
                sp.sem_inc(stored[u], STORED)

            def store_values(i, u):
                sp.wait_ge(vx_ready, 2 * (2 * i + u) + 3)
                for t in range(G):
                    at = u * z.GT + t * P
                    sp.dma_start(m.v_dram[bass.ts(i, z.UPB), at:at + P, :].rearrange("g p k -> p g k"),
                                 vx[u][:, t, :, :].rearrange("p (g h) k -> p g (h k)", g=z.UPB)).then_inc(v_stored[u], 16)

            def store_features(i, u):
                sp.wait_ge(low_done, 2 * i + u + 2)
                store_parts(sp, z, m, parts[u], stored[u], i, u)

            staggered(sp, GROUPS, store_values, store_features)
            for u in range(2):
                sp.wait_ge(v_stored[u], V_STORED * (GROUPS // 2 + 1))
                sp.wait_ge(stored[u], STORED * (GROUPS // 2 + 1))

        @block.vector
        def _(dve):
            for u in range(2):
                last = dve.memset(vx[u][:, :, :, 16:32], 1.0)
            last.then_inc(ones_ready, 1)
            dve.sem_inc(var_ready, 2)
            dve.sem_inc(rest_done, 2)

            def measure(i, u):
                n = 2 * i + u
                statistics(m, dve, of_group(z, m.x, n), raw[u], mv[u], raw_done, mv_ready, n)

            def norm(i, u):
                n = 2 * i + u
                inverse(dve, sd[u], rs[u], sd_ready, rs_ready, n)
                dve.wait_ge(turned, n + 1)
                normalise(dve, xn[u], of_group(z, m.x, n), mv[u], rs[u]).then_inc(xn_ready, 1)

            def sum_squares(i, u):
                n = 2 * i + u
                for t in range(G):
                    dve.wait_ge(sq_ready, G * n + t + 1)
                    dve.tensor_reduce(var[u][:, t, :], sq[t % 2][:, :].rearrange("p (h f) -> p h f", f=z.DK), AX.X,
                                      ALU.add).then_inc(var_ready, 1)

            def scale_heads(i, u):
                n = 2 * i + u
                dve.wait_ge(hsd_ready, n + 1)
                dve.reciprocal(hrs[u][:, :, :], hsd[u][:, :, :]).then_inc(hrs_ready, 1)
                dve.wait_ge(hrs_ready, n + 1)
                for t in range(G):
                    view = qk[u][:, t, :].rearrange("p (n d h) -> p n d h", d=z.DK, h=z.HPU)
                    inverses = hrs[u][:, t, :].rearrange("p (n h) -> p n h", h=z.HPU).unsqueeze(2)
                    last = dve.tensor_tensor(view, view, inverses.to_broadcast([P, H2 // z.HPU, z.DK, z.HPU]), ALU.mult)
                last.then_inc(qn_ready, 1)

            def split(i, u):
                n = 2 * i + u
                dve.wait_ge(feat_ready, 4 * n + 6)
                dve.wait_ge(stored[u], STORED * i + STORED)
                dve.tensor_copy(parts[u][:, 0, :, :], feat[u][:, :, :]).then_inc(high_done, 1)
                dve.wait_ge(high_done, n + 1)
                dve.wait_ge(low_done, n + 1)
                dve.tensor_tensor(rest[:, :, :], feat[u][:, :, :], parts[u][:, 0, :, :], ALU.subtract).then_inc(rest_done, 1)
                dve.wait_ge(rest_done, n + 3)
                dve.tensor_copy(parts[u][:, 1, :, :], rest[:, :, :]).then_inc(mid_done, 1)

            three_stages(dve, GROUPS, lambda last, now, next: (next(measure), now(sum_squares), next(norm), last(split),
                                                               now(scale_heads)))

        @block.gpsimd
        def _(pool):
            pool.sem_inc(low_done, 1)
            with pool.Fori(0, GROUPS // 2) as i:
                for u in range(2):
                    n = 2 * i + u
                    wait_alone(pool, mid_done, n + 1, m.alone)
                    pool.tensor_tensor(parts[u][:, 2, :, :], rest[:, :, :], parts[u][:, 1, :, :], ALU.subtract
                                       ).then_inc(low_done, 1)

        @block.scalar
        def _(act):
            act.sem_inc(xt_ready, 1)
            act.sem_inc(qk_taken, 2)
            act.sem_inc(feat_ready, 2)
            act.sem_inc(vx_ready, 1)

            def root(i, u):
                deviation(act, mv[u], sd[u], m.eps, mv_ready, sd_ready, 2 * i + u)

            def take_turned(i, u):
                n = 2 * i + u
                act.wait_ge(turned, n + 3)
                act.wait_ge(v_ready, 2 * n + 2)
                for c in range(DC):
                    last = act.activation(xt[u][:, c, :], m.bank[T0 + c], ACT.Copy)
                last.then_inc(xt_ready, 1)

            def take_heads(i, u):
                n = 2 * i + u
                act.wait_ge(ft_ready, 4 * n + 4)
                for t in range(G):
                    act.wait_ge(qk_ready, G * n + t + 1)
                    act.wait_ge(var_ready, G * n + t + 1)
                    act.activation(sq[t % 2][:, :], m.bank[Q0 + t % 2], ACT.Square).then_inc(sq_ready, 1)
                    act.activation(qk[u][:, t, :].rearrange("p (n d h) -> p n h d", d=z.DK, h=z.HPU),
                                   m.bank[Q0 + t % 2].rearrange("p (n h d) -> p n h d", d=z.DK, h=z.HPU), ACT.Copy
                                   ).then_inc(qk_taken, 1)
                    if t % 2:
                        act.wait_ge(ones_ready, 1)
                        act.wait_ge(v_stored[u], V_STORED * i + V_STORED)
                        act.wait_ge(v_ready, 2 * n + t // 2 + 5)
                        act.activation(vx[u][:, t - 1:t + 1, :, 0:16],
                                       m.bank[VB].rearrange("p (t h d) -> p t h d", t=2, d=16), ACT.Copy
                                       ).then_inc(vx_ready, 1)

            def root_of_heads(i, u):
                n = 2 * i + u
                act.wait_ge(var_ready, G * n + G + 2)
                act.activation(hsd[u][:, :, :], var[u][:, :, :], ACT.Sqrt, bias=m.eps[:, 0:1], scale=1.0 / z.DK
                               ).then_inc(hsd_ready, 1)

            def take_features(i, u):
                n = 2 * i + u
                act.wait_ge(rest_done, n + 1)
                for j in range(4):
                    act.wait_ge(ft_ready, 4 * n + j + 9)
                    act.activation(feat[u][:, j, :], m.bank[F0 + j % 2], ACT.Identity, bias=m.beta_col[:, 0:1],
                                   scale=m.gamma_col[:, 0:1]).then_inc(feat_ready, 1)

            three_stages(act, GROUPS, lambda last, now, next: (last(take_features), now(take_heads), next(root),
                                                               now(root_of_heads), next(take_turned)))

        @block.tensor
        def _(pe):
            pe.sem_inc(turned, 2)
            pe.sem_inc(v_ready, 4)
            pe.sem_inc(ft_ready, 8)

            def turn(i, u):
                n = 2 * i + u
                pe.wait_ge(xn_ready, n + 1)
                pe.wait_ge(xt_ready, n + 1)
                turn_group(pe, z, m.bank[T0:T0 + DC], xn[u], m.ident).then_inc(turned, 1)

            def project(i, u):
                n = 2 * i + u
                pe.wait_ge(xt_ready, n + 2)
                for t in range(G):
                    pe.wait_ge(qk_taken, G * n + t + 1)
                    for c in range(DC):
                        last = pe.matmul(m.bank[Q0 + t % 2], xt[u][:, c, t * P:(t + 1) * P], m.w_qkv[:, c, 0:W],
                                         start=(c == 0), stop=(c == DC - 1))
                    last.then_inc(qk_ready, 1)
                    if t % 2:
                        pe.wait_ge(vx_ready, 2 * n + t // 2 + 1)
                        for k, tile in enumerate((t - 1, t)):
                            for c in range(DC):
                                last = pe.matmul(m.bank[VB][:, k * z.D:(k + 1) * z.D], xt[u][:, c, tile * P:(tile + 1) * P],
                                                 m.w_qkv[:, c, W:W + z.D], start=(c == 0), stop=(c == DC - 1))
                        last.then_inc(v_ready, 1)

            def turn_features(i, u):
                n = 2 * i + u
                pe.wait_ge(qn_ready, n + 1)
                for j in range(4):
                    pe.wait_ge(feat_ready, 4 * n + j + 1)
                    for t in range(G):
                        last = pe.transpose(m.bank[F0 + j % 2][:, t * P:(t + 1) * P], qk[u][:, t, j * P:(j + 1) * P],
                                            m.ident[:, :])
                    last.then_inc(ft_ready, 1)

            three_stages(pe, GROUPS, lambda last, now, next: (last(turn_features), now(project), next(turn)))



def scale_pass(nc, z, m, normed):
    G, GROUPS = z.G, z.TILES // z.G
    with ExitStack() as ctx:
        def sb(name, shape, dt=F32):
            return [ctx.enter_context(nc.sbuf_tensor(f"s_{name}{u}", shape, dt)) for u in range(2)]

        raw, mv, sd, rs = sb("raw", [P, G, 6]), sb("mv", [P, G, 2]), sb("sd", [P, G]), sb("rs", [P, G])
        (raw_done, mv_ready, sd_ready, rs_ready, inner_ready, gained, normed_ready, peaked) = sems(
            nc, *["s_" + x for x in ("raw_done", "mv_ready", "sd_ready", "rs_ready", "inner_ready", "gained",
                                     "normed_ready", "peaked")])
        block = ctx.enter_context(nc.Block())

        @block.vector
        def _(dve):
            def measure(i, u):
                n = 2 * i + u
                statistics(m, dve, of_group(z, m.x, n), raw[u], mv[u], raw_done, mv_ready, n)

            def divide(i, u):
                n = 2 * i + u
                inverse(dve, sd[u], rs[u], sd_ready, rs_ready, n)
                for t, (dst, tile) in enumerate(zip(of_group(z, normed, n), of_group(z, m.x, n))):
                    last = dve.tensor_scalar(dst, tile, mv[u][:, t, 0:1], rs[u][:, t:t + 1], ALU.subtract, ALU.mult)
                last.then_inc(inner_ready, 1)

            def largest(n):
                dve.wait_ge(normed_ready, n + 1)
                dve.tensor_reduce(m.peaks[:, bass.ds(n, 1)], normed[:, bass.ts(n, G), :], AX.XY, ALU.max,
                                  apply_absolute_value=True).then_inc(peaked, 1)

            for u in range(2):
                measure(0, u)
            for u in range(2):
                divide(0, u)
                measure(1, u)
            with dve.Fori(1, GROUPS // 2 - 1) as i:
                for u in range(2):
                    divide(i, u)
                    measure(i + 1, u)
                    largest(2 * i + u - 2)
            for u in range(2):
                divide(GROUPS // 2 - 1, u)
                largest(GROUPS - 4 + u)
            for u in range(2):
                largest(GROUPS - 2 + u)

        @block.gpsimd
        def _(pool):
            with pool.Fori(0, GROUPS // 2) as i:
                for u in range(2):
                    n = 2 * i + u
                    wait_alone(pool, inner_ready, n + 1, m.alone)
                    view = normed[:, bass.ts(n, G), :]
                    pool.tensor_tensor(view, view, m.ln_gamma[:, :].unsqueeze(1).to_broadcast([P, G, z.D]),
                                       ALU.mult).then_inc(gained, 1)
                    wait_alone(pool, gained, n + 1, m.alone)
                    pool.tensor_tensor(view, view, m.ln_beta[:, :].unsqueeze(1).to_broadcast([P, G, z.D]),
                                       ALU.add).then_inc(normed_ready, 1)

        @block.scalar
        def _(act):
            with act.Fori(0, GROUPS // 2) as i:
                for u in range(2):
                    deviation(act, mv[u], sd[u], m.eps_both, mv_ready, sd_ready, 2 * i + u, scale=1.0 + EPS_IN)



def ternary_pass(nc, z, m, normed, out):
    G, DC, GROUPS = z.G, z.DC, z.TILES // z.G
    QB, EPS = 128.0, 1e-5
    og = out.rearrange("b s d -> (b s) d").rearrange("(n p) d -> p n d", p=P)
    with ExitStack() as ctx:
        def sb(name, shape, dt=F32):
            return [ctx.enter_context(nc.sbuf_tensor(f"t_{name}{u}", shape, dt)) for u in range(2)]

        raw, mv, sd, rs = sb("raw", [P, G, 6]), sb("mv", [P, G, 2]), sb("sd", [P, G]), sb("rs", [P, G])
        grs, xt, zt = sb("grs", [P, G]), sb("xt", [P, DC, z.GT]), sb("zt", [P, G, z.D])
        cap_in = sb("cap_in", [P, G, z.D])
        one = lambda name: ctx.enter_context(nc.sbuf_tensor("t_" + name, [P, 1], F32))
        peak, gamma, inv, factor, gain, gain2 = (one(x) for x in ("peak", "gamma", "inv", "factor", "gain", "gain2"))
        stored = sems(nc, "t_stored0", "t_stored1")
        (peak_ready, gamma_ready, setup, capped, turned, xt_ready, y_ready, raw_done, mv_ready, sd_ready, rs_ready,
         grs_ready, zt_ready, added) = sems(nc, *["t_" + x for x in (
             "peak_ready", "gamma_ready", "setup", "capped", "turned", "xt_ready", "y_ready", "raw_done", "mv_ready",
             "sd_ready", "rs_ready", "grs_ready", "zt_ready", "added")])
        block = ctx.enter_context(nc.Block())
        T0 = 0
        SETUP = 6

        def banks(u):
            return [m.psum[:, 4 + 2 * u + t // 2, (t % 2) * z.D:(t % 2 + 1) * z.D] for t in range(G)]

        @block.sync
        def _(sp):
            with sp.Fori(0, GROUPS // 2) as i:
                for u in range(2):
                    n = 2 * i + u
                    sp.wait_ge(added, n + 3)
                    sp.dma_start(og[:, bass.ts(n, G), :], m.x[:, bass.ts(n, G), :]).then_inc(stored[u], 16)
            for u in range(2):
                sp.wait_ge(stored[u], 16 * (GROUPS // 2))

        @block.vector
        def _(dve):
            count = [0]

            def did(ins):
                count[0] += 1
                ins.then_inc(setup, 1)
                dve.wait_ge(setup, count[0])

            dve.tensor_reduce(peak[:, :], m.peaks[:, :], AX.X, ALU.max).then_inc(peak_ready, 1)
            dve.wait_ge(gamma_ready, 1)
            did(dve.reciprocal(inv[:, :], gamma[:, :]))
            did(dve.tensor_scalar(factor[:, :], inv[:, :], QB, None, ALU.mult))
            did(dve.tensor_scalar(gain[:, :], gamma[:, :], m.w_mean[:, 0:1], None, ALU.mult))
            did(dve.tensor_scalar(gain[:, :], gain[:, :], 1.0 / QB, None, ALU.mult))
            did(dve.tensor_tensor(gain2[:, :], gain[:, :], gain[:, :], ALU.mult))
            dve.sem_inc(setup, 1)
            dve.sem_inc(xt_ready, 2)
            dve.sem_inc(zt_ready, 2)

            def cap(i, u):
                n = 2 * i + u
                dve.wait_ge(turned, n + 1)
                dve.tensor_scalar(cap_in[u][:, :, :], normed[:, bass.ts(n, G), :], factor[:, 0:1], QB - EPS, ALU.mult,
                                  ALU.min).then_inc(capped, 1)

            def floor(i, u):
                n = 2 * i + u
                dve.wait_ge(turned, n + 3)
                dve.wait_ge(y_ready, n + 1)
                for c in range(DC):
                    last = dve.tensor_scalar(xt[u][:, c, :], m.bank[T0 + 2 * u + c], EPS - QB, None, ALU.max)
                last.then_inc(xt_ready, 1)

            def norm(i, u):
                norm_sums(m, dve, banks(u), raw[u], mv[u], sd[u], rs[u], zt[u], y_ready, raw_done, mv_ready, sd_ready,
                          rs_ready, added, zt_ready, 2 * i + u, 2, gain=(gain[:, 0:1], grs[u], grs_ready))

            three_stages(dve, GROUPS, lambda last, now, next: (last(norm), next(cap), now(floor)))

        @block.gpsimd
        def _(pool):
            pool.wait_ge(peak_ready, 1)
            pool.partition_all_reduce(gamma[:, :], peak[:, :], P, bass.bass_isa.ReduceOp.max).then_inc(gamma_ready, 1)
            add_to_x(pool, z, m, zt, zt_ready, added, GROUPS)

        @block.scalar
        def _(act):
            act.wait_ge(setup, SETUP)
            with act.Fori(0, GROUPS // 2) as i:
                for u in range(2):
                    deviation(act, mv[u], sd[u], m.eps, mv_ready, sd_ready, 2 * i + u, scale=gain2[:, 0:1])

        @block.tensor
        def _(pe):
            pe.sem_inc(y_ready, 2)
            pe.sem_inc(turned, 2)

            def turn(i, u):
                n = 2 * i + u
                pe.wait_ge(capped, n + 1)
                pe.wait_ge(xt_ready, n + 1)
                for c in range(DC):
                    for t in range(G):
                        src = cap_in[u][:, t, c * P:(c + 1) * P]
                        last = pe.transpose(m.bank[T0 + 2 * u + c][:, t * P:(t + 1) * P], src, m.ident[:, :])
                last.then_inc(turned, 1)

            def project(i, u):
                n = 2 * i + u
                pe.wait_ge(xt_ready, n + 3)
                pe.wait_ge(zt_ready, n + 1)
                for t, bank in enumerate(banks(u)):
                    for c in range(DC):
                        last = pe.matmul(bank, xt[u][:, c, t * P:(t + 1) * P], m.w_ter[:, c, :], start=(c == 0),
                                         stop=(c == DC - 1))
                last.then_inc(y_ready, 1)

            staggered(pe, GROUPS, turn, project, behind_first=True)


_INS = ['L0_attn_x', 'L0_attn_W_dq', 'L0_attn_W_uq', 'L0_attn_W_dkv', 'L0_attn_W_uk', 'L0_attn_W_uv', 'L0_attn_W_o',
        'L0_ffn_fast_b', 'L0_ffn_w_fc', 'L0_ffn_w_proj', 'L0_ffn_u', 'L0_ffn_v', 'L0_ffn_gate', 'L1_attn_Wq',
        'L1_attn_Wk', 'L1_attn_Wv', 'L1_attn_Wo', 'L1_attn_gamma', 'L1_attn_beta', 'L1_ffn_weight',
        'L1_ffn_ln_gamma', 'L1_ffn_ln_beta']


def kernel(**inputs):
    import numpy as _np
    import concourse.bacc as _bacc
    from concourse.bass_utils import run_bass_kernel_spmd as _run

    nc = _bacc.Bacc("TRN2", target_bir_lowering=False, num_devices=1)
    arrays, aps = {}, {}
    for name in _INS:
        a = _np.ascontiguousarray(inputs[name]).reshape(_np.shape(inputs[name]) or (1,))
        arrays[f"in_{name}"] = a
        aps[name] = nc.dram_tensor(f"in_{name}", a.shape, mybir.dt.from_np(a.dtype), kind="ExternalInput").ap()
    out = nc.dram_tensor("out_0", arrays["in_L0_attn_x"].shape, F32, kind="ExternalOutput").ap()
    build(nc, aps, out)
    r = _run(nc, [arrays], core_ids=[0])
    return r.results[0]["out_0"]
```

```python
from contextlib import ExitStack

import concourse.bass as bass
from concourse import mybir

F32 = mybir.dt.float32
BF16 = mybir.dt.bfloat16
ALU = mybir.AluOpType
ACT = mybir.ActivationFunctionType
AX = mybir.AxisListType

P = 128
EPS = 1e-5
EPS_IN = 1e-3
NEG = -3.0e38
PARTS = 3
Q_STACK = ((0, 0, 3), (1, 0, 2), (2, 0, 1))
K_STACK = ((0, 1, 3), (0, 1, 2), (0, 1, 1))
STACK = 16 * 6


class Sizes:
    def __init__(self, x, w_dq, w_fc):
        self.B, self.S, self.D = x.shape
        self.C = w_dq.shape[1]
        self.HID = w_fc.shape[0]
        self.DK = 16
        self.H = self.D // self.DK
        self.DC = self.D // P
        self.HC = self.HID // P
        self.TILES = self.B * self.S // P
        self.G = 4
        self.GT = self.G * P
        self.HPU = 4
        self.UPB = self.H // self.HPU
        self.UNITS = self.B * self.UPB
        self.ST = self.S // P
        assert self.S == 2 * self.GT and 2 * self.C == P and self.DC == 2 and self.H * self.DK == self.D


def build(nc, a, out):
    z = Sizes(a["L0_attn_x"], a["L0_attn_W_dq"], a["L0_ffn_w_fc"])
    with ExitStack() as ctx:
        m = Resident(nc, ctx, z)

        def run(one_pass, *args, **settings):
            with nc.cleanup_on_exit():
                one_pass(nc, z, m, *args, **settings)

        run(weights_pass, a)
        run(latent_pass)
        run(attend_pass, softmax=True)
        run(mix_pass, m.wo0, None)
        run(mlp_pass)
        run(features_pass)
        run(attend_pass, softmax=False)
        with nc.sbuf_tensor("normed", [P, z.TILES, z.D], F32) as normed:
            run(mix_pass, m.wo1, EPS, normed)
            run(ternary_pass, normed, out)


class Resident:

    def __init__(self, nc, ctx, z):
        def sb(name, shape, dt=F32):
            return ctx.enter_context(nc.sbuf_tensor(name, shape, dt))

        self.x = sb("x", [P, z.TILES, z.D])
        self.ident = sb("ident", [P, P])
        self.ident16 = sb("ident16", [P, P], BF16)
        self.eps = sb("eps", [P, 1])
        self.eps_both = sb("eps_both", [P, 1])
        self.w_down = sb("w_down", [P, z.DC, P])
        self.w_uq = sb("w_uq", [P, z.D])
        self.w_uk = sb("w_uk", [P, z.D])
        self.w_uv = sb("w_uv", [P, z.D])
        self.wo0 = sb("wo0", [P, z.DC, z.D])
        self.wo1 = sb("wo1", [P, z.DC, z.D])
        self.w_fc = sb("w_fc", [P, z.DC, z.HID])
        self.w_proj = sb("w_proj", [P, z.HC, z.D], BF16)
        self.proj_scale = sb("proj_scale", [P, z.D])
        self.w_qkv = sb("w_qkv", [P, z.DC, 3 * z.D])
        self.w_ter = sb("w_ter", [P, z.DC, z.D])
        self.gamma_col = sb("gamma_col", [P, 1])
        self.beta_col = sb("beta_col", [P, 1])
        self.ln_gamma = sb("ln_gamma", [P, z.D])
        self.ln_beta = sb("ln_beta", [P, z.D])
        self.peaks = sb("peaks", [P, z.TILES // z.G])
        self.w_mean = sb("w_mean", [P, 1])
        self.psum = ctx.enter_context(nc.psum_tensor("psum", [P, 8, 512], F32))
        self.bank = [self.psum[:, i, :] for i in range(8)]
        self.alone = ctx.enter_context(nc.semaphore("alone"))
        self.qk_dram = nc.dram_tensor("qk_parts", [PARTS, 2, z.B * z.D, z.S], BF16, kind="Internal").ap()
        self.v_dram = nc.dram_tensor("values", [z.UNITS, z.S, P], F32, kind="Internal").ap()
        self.sums_dram = nc.dram_tensor("sums", [z.B * z.H * 32, z.S], F32, kind="Internal").ap()
        self.inv_dram = nc.dram_tensor("reciprocals", [z.B * z.H, z.S], F32, kind="Internal").ap()


def sems(nc, *names):
    return [nc.alloc_semaphore(n) for n in names]



def wait_alone(eng, sem, value, alone):
    eng.wait_ge(sem, value)
    eng.sem_inc(alone, 1)


def statistics(m, dve, tiles, raw, mv, raw_done, mv_ready, n):
    for t, tile in enumerate(tiles):
        last = dve.bn_stats(raw[:, t, :], tile)
    last.then_inc(raw_done, 1)
    wait_alone(dve, raw_done, n + 1, m.alone)
    for t in range(len(tiles)):
        last = dve.bn_aggr(mv[:, t, :], raw[:, t, :])
    last.then_inc(mv_ready, 1)


def deviation(act, mv, sd, eps, mv_ready, sd_ready, n, scale=1.0):
    act.wait_ge(mv_ready, n + 1)
    act.activation(sd[:, :], mv[:, :, 1], ACT.Sqrt, bias=eps[:, 0:1], scale=scale).then_inc(sd_ready, 1)


def inverse(dve, sd, rs, sd_ready, rs_ready, n):
    dve.wait_ge(sd_ready, n + 1)
    dve.reciprocal(rs[:, :], sd[:, :]).then_inc(rs_ready, 1)
    dve.wait_ge(rs_ready, n + 1)


def normalise(dve, out, tiles, mv, rs):
    for t, tile in enumerate(tiles):
        last = dve.tensor_scalar(out[:, t, :], tile, mv[:, t, 0:1], rs[:, t:t + 1], ALU.subtract, ALU.mult)
    return last


def turn_group(pe, z, banks, src, ident):
    for c in range(z.DC):
        for t in range(z.G):
            last = pe.transpose(banks[c][:, t * P:(t + 1) * P], src[:, t, c * P:(c + 1) * P], ident[:, :])
    return last


def staggered(eng, groups, ahead, behind, behind_first=False):
    for u in range(2):
        ahead(0, u)
    with eng.Fori(0, groups // 2 - 1) as i:
        for u in range(2):
            if behind_first:
                behind(i, u)
            ahead(i + 1, u)
            if not behind_first:
                behind(i, u)
    for u in range(2):
        behind(groups // 2 - 1, u)


def lagged(eng, groups, *stages):
    rounds, most = groups // 2, max(lag for lag, _ in stages)

    def round_of(i, exists):
        for u in range(2):
            for lag, fn in stages:
                if exists(lag):
                    fn(i - lag, u)

    for i in range(most):
        round_of(i, lambda lag: lag <= i)
    with eng.Fori(most, rounds) as i:
        round_of(i, lambda lag: True)
    for i in range(rounds, rounds + most):
        round_of(i, lambda lag: i - lag < rounds)


def of_group(z, x, n):
    return [x[:, bass.ds(n * z.G + t, 1), :] for t in range(z.G)]



def weights_pass(nc, z, m, a):
    with ExitStack() as ctx:
        def sb(name, shape, dt=F32):
            return ctx.enter_context(nc.sbuf_tensor(name, shape, dt))

        rank = a["L0_ffn_u"].shape[1]
        fc = sb("fc", [P, z.HC, z.D])
        proj = sb("proj", [P, z.DC, z.HID])
        qkv = sb("qkv", [P, 3, z.DC, z.D])
        wo = sb("wo", [P, z.DC, z.D])
        ter = sb("ter", [P, z.DC, z.D])
        u = sb("u", [P, z.HC, rank])
        fast = sb("fast", [rank, rank])
        v = sb("v", [rank, z.D])
        gate = sb("gate", [rank, 1])
        uq = sb("uq", [P, z.D])
        fast_t = sb("fast_t", [rank, rank])
        fv = sb("fv", [rank, z.D])
        u_t = sb("u_t", [rank, z.HID])
        sums = sb("sums_w", [P, z.HC + z.DC + 1])
        scale = sb("scale", [P, z.HC + z.DC])
        half = sb("half", [P, z.HC + z.DC + 1])
        nhalf = sb("nhalf", [P, z.HC + z.DC + 1])
        fc_w = sb("fc_w", [P, z.HC, z.D])
        proj_w = sb("proj_w", [P, z.DC, z.HID])
        ones = sb("ones", [P, P])
        diag = sb("diag", [P, z.DC, P])
        neg = sb("neg", [P, z.HC * z.D])
        means = sb("means", [P, z.DC * 2 * z.H])
        total = sb("total", [P, 1])
        (loaded, x_loaded, ident_zero, ident_ready, zeros_ready, step, pe_step, drained, total_ready, total_in) = sems(
            nc, "w_loaded", "w_x_loaded", "w_ident_zero", "w_ident_ready", "w_zeros_ready", "w_dve_step", "w_pe_step",
            "w_drained", "w_total_ready", "w_total_in")
        block = ctx.enter_context(nc.Block())
        chunks = lambda w: w.rearrange("(c p) n -> p c n", p=P)
        loads = [
            (fc[:, :, :], chunks(a["L0_ffn_w_fc"])), (proj[:, :, :], chunks(a["L0_ffn_w_proj"])),
            (qkv[:, 0, :, :], chunks(a["L1_attn_Wq"])), (qkv[:, 1, :, :], chunks(a["L1_attn_Wk"])),
            (qkv[:, 2, :, :], chunks(a["L1_attn_Wv"])), (wo[:, :, :], chunks(a["L1_attn_Wo"])),
            (ter[:, :, :], chunks(a["L1_ffn_weight"])), (u[:, :, :], chunks(a["L0_ffn_u"])),
            (fast[:, :], a["L0_ffn_fast_b"]), (v[:, :], a["L0_ffn_v"]),
            (gate[:, :], a["L0_ffn_gate"].partition_broadcast(rank)),
            (m.w_down[:, :, 0:z.C], chunks(a["L0_attn_W_dq"])), (m.w_down[:, :, z.C:P], chunks(a["L0_attn_W_dkv"])),
            (uq[0:z.C, :], a["L0_attn_W_uq"]), (uq[z.C:P, :], a["L0_attn_W_uk"]),
            (m.w_uv[z.C:P, :], a["L0_attn_W_uv"]), (m.wo0[:, :, :], chunks(a["L0_attn_W_o"])),
            (m.ln_gamma[:, :], a["L1_ffn_ln_gamma"].partition_broadcast(P)),
            (m.ln_beta[:, :], a["L1_ffn_ln_beta"].partition_broadcast(P)),
        ]
        for row in range(0, P, z.HPU * z.DK):
            for column, name in ((m.gamma_col, "L1_attn_gamma"), (m.beta_col, "L1_attn_beta")):
                src = a[name].unsqueeze(1).unsqueeze(2).to_broadcast([z.DK, z.HPU, 1])
                loads.append((column[row:row + z.HPU * z.DK, :], src))

        @block.sync
        def _(sp):
            for dst, src in loads:
                sp.dma_start(dst, src).then_inc(loaded, 16)
            for b in range(z.B):
                sp.dma_start(m.x[:, b * z.ST:(b + 1) * z.ST, :], a["L0_attn_x"][b].rearrange("(n p) d -> p n d", p=P)
                             ).then_inc(x_loaded, 16)
            sp.wait_ge(x_loaded, 16 * z.B)

        @block.gpsimd
        def _(pool):
            pool.memset(m.ident[:, :], 0.0).then_inc(ident_zero, 1)
            pool.memset(m.ident16[:, :], 0.0).then_inc(ident_zero, 1)
            pool.wait_ge(ident_zero, 2)
            for t in (m.ident, m.ident16):
                pool.affine_select(out=t[:, :], in_=t[:, :], compare_op=ALU.not_equal, fill=1.0, base=0,
                                   pattern=[[-1, P]], channel_multiplier=1).then_inc(ident_ready, 1)
            pool.wait_ge(total_in, 1)
            pool.partition_all_reduce(total[:, :], sums[:, z.HC + z.DC:], P,
                                      bass.bass_isa.ReduceOp.add).then_inc(total_ready, 1)

        T_FC, T_PROJ = "fc", "proj"
        dve_done, pe_done = {}, {}

        @block.vector
        def _(dve):
            count = [0]

            def did(ins, name=None):
                count[0] += 1
                ins.then_inc(step, 1)
                dve.wait_ge(step, count[0])
                if name:
                    dve_done[name] = count[0]

            did(dve.memset(m.w_uq[z.C:P, :], 0.0))
            did(dve.memset(m.w_uk[0:z.C, :], 0.0))
            did(dve.memset(m.w_uv[0:z.C, :], 0.0))
            did(dve.memset(ones[:, :], 1.0))
            did(dve.memset(m.eps[:, :], EPS))
            did(dve.memset(m.eps_both[:, :], EPS * EPS_IN))
            dve.wait_ge(loaded, 16 * len(loads))
            for dst, rows in ((m.w_uq, slice(0, z.C)), (m.w_uk, slice(z.C, P))):
                did(dve.tensor_copy(dst[rows, :].rearrange("p (n d h) -> p n h d", d=z.DK, h=z.HPU),
                                    uq[rows, :].rearrange("p (n h d) -> p n h d", d=z.DK, h=z.HPU)))
            did(dve.tensor_reduce(sums[:, 0:z.HC], fc[:, :, :], AX.X, ALU.add, apply_absolute_value=True))
            did(dve.tensor_reduce(sums[:, z.HC:z.HC + z.DC], proj[:, :, :], AX.X, ALU.add, apply_absolute_value=True))
            did(dve.tensor_reduce(sums[:, z.HC + z.DC:], ter[:, :, :], AX.XY, ALU.add, apply_absolute_value=True))
            dve.sem_inc(total_in, 1)
            did(dve.tensor_scalar(scale[:, 0:z.HC], sums[:, 0:z.HC], 1.0 / z.D, 1e-5, ALU.mult, ALU.max))
            did(dve.tensor_scalar(scale[:, z.HC:], sums[:, z.HC:z.HC + z.DC], 1.0 / z.HID, 1e-5, ALU.mult, ALU.max))
            did(dve.tensor_scalar(half[:, 0:z.HC + z.DC], scale[:, :], 0.5, None, ALU.mult))
            did(dve.tensor_scalar(nhalf[:, 0:z.HC + z.DC], scale[:, :], -0.5, None, ALU.mult))
            for name, w, dst, rows, width, at in ((T_FC, fc, fc_w, z.HC, z.D, 0),
                                                  (T_PROJ, proj, proj_w, z.DC, z.HID, z.HC)):
                view = neg[:, :].rearrange("p (r w) -> p r w", r=rows)
                for r in range(rows):
                    k = at + r
                    by = scale[:, k:k + 1] if name == T_FC else 1.0
                    dve.tensor_scalar(dst[:, r, :], w[:, r, :], half[:, k:k + 1], by, ALU.is_gt, ALU.mult)
                    last = dve.tensor_scalar(view[:, r, :], w[:, r, :], nhalf[:, k:k + 1], by, ALU.is_lt, ALU.mult)
                did(last)
                did(dve.tensor_tensor(dst[:, :, :], dst[:, :, :], view, ALU.subtract), name)
            dve.wait_ge(ident_ready, 2)
            for c in range(z.DC):
                last = dve.tensor_scalar(diag[:, c, :], m.ident[:, :], scale[:, z.HC + c:z.HC + c + 1], None, ALU.mult)
            did(last, "diag")
            dve.wait_ge(total_ready, 1)
            k = z.HC + z.DC
            did(dve.tensor_scalar(m.w_mean[:, :], total[:, :], 1.0 / (z.D * z.D), None, ALU.mult))
            did(dve.tensor_scalar(half[:, k:k + 1], m.w_mean[:, :], 1e-5, 0.5, ALU.add, ALU.mult))
            did(dve.tensor_scalar(nhalf[:, k:k + 1], half[:, k:k + 1], -1.0, None, ALU.mult))
            did(dve.tensor_scalar(neg[:, 0:z.DC * z.D], ter[:, :, :].rearrange("p c n -> p (c n)"),
                                  nhalf[:, k:k + 1], None, ALU.is_lt))
            did(dve.scalar_tensor_tensor(out=m.w_ter[:, :, :].rearrange("p c n -> p (c n)"),
                                         in0=ter[:, :, :].rearrange("p c n -> p (c n)"), scalar=half[:, k:k + 1],
                                         in1=neg[:, 0:z.DC * z.D], op0=ALU.is_gt, op1=ALU.subtract))

            got = [0]

            def take(name=None, fn=None):
                got[0] += 1
                dve.wait_ge(pe_step, got[0])
                fn().then_inc(drained, 1)
                dve.wait_ge(drained, got[0])
                if name:
                    pe_done[name] = got[0]

            take("fast_t", lambda: dve.tensor_copy(fast_t[:, :], m.bank[0][0:rank, 0:rank]))
            take("fv", lambda: dve.tensor_scalar(fv[:, :], m.bank[1][0:rank, 0:z.D], gate[:, 0:1], None, ALU.mult))
            for k in range(2):
                take("u_t", lambda: dve.tensor_copy(u_t[:, k * 512:(k + 1) * 512], m.bank[2 + k][0:rank, :]))
            for n, (c, k) in enumerate((c, k) for c in range(z.DC) for k in range(z.HID // 512)):
                dst = m.w_fc[:, c, k * 512:(k + 1) * 512]
                take(None, lambda: dve.tensor_copy(dst, m.bank[4][:, :]))
                take("fc", lambda: dve.tensor_tensor(dst, dst, m.bank[5][:, :], ALU.add))
            for g in range(z.HC // 2):
                take("proj", lambda: dve.tensor_copy(m.w_proj[:, 2 * g:2 * g + 2, :],
                                                     m.bank[6 + g % 2][:, :].rearrange("p (j n) -> p j n", j=2)))
            take("proj_scale", lambda: dve.tensor_copy(m.proj_scale[:, :], m.bank[5][:, 0:z.D]))
            for w in range(4):
                dst = m.w_qkv[:, :, w * z.D:(w + 1) * z.D] if w < 3 else m.wo1[:, :, :]
                take("qkv", lambda: dve.tensor_copy(dst, m.bank[w][:, :].rearrange("p (c n) -> p c n", c=z.DC)))
            for c in range(z.DC):
                view = m.w_qkv[:, c, 0:2 * z.D].rearrange("p (h f) -> p h f", f=z.DK)
                mean = means[:, c * 2 * z.H:(c + 1) * 2 * z.H]
                did(dve.tensor_reduce(mean, view, AX.X, ALU.add))
                did(dve.tensor_scalar(mean, mean, 1.0 / z.DK, None, ALU.mult))
                did(dve.tensor_tensor(view, view, mean.unsqueeze(2).to_broadcast([P, 2 * z.H, z.DK]), ALU.subtract))

        @block.tensor
        def _(pe):
            pe.wait_ge(loaded, 16 * len(loads))
            pe.wait_ge(ident_ready, 2)
            pe.transpose(m.bank[0][0:rank, 0:rank], fast[:, :], m.ident[0:rank, 0:rank]).then_inc(pe_step, 1)
            pe.wait_ge(drained, pe_done["fast_t"])
            pe.matmul(m.bank[1][0:rank, 0:z.D], fast_t[:, :], v[:, :], start=True, stop=True).then_inc(pe_step, 1)
            for k in range(2):
                for t in range(4):
                    last = pe.transpose(m.bank[2 + k][0:rank, t * P:(t + 1) * P], u[:, 4 * k + t, :], m.ident[:, :])
                last.then_inc(pe_step, 1)
            pe.wait_ge(drained, pe_done["u_t"])
            pe.wait_ge(step, dve_done[T_PROJ])
            done = pe_done["u_t"]
            for c in range(z.DC):
                for k in range(z.HID // 512):
                    for t in range(4):
                        last = pe.transpose(m.bank[4][:, t * P:(t + 1) * P],
                                            fc_w[:, 4 * k + t, c * P:(c + 1) * P], m.ident[:, :])
                    last.then_inc(pe_step, 1)
                    pe.matmul(m.bank[5][:, :], fv[:, c * P:(c + 1) * P], u_t[:, k * 512:(k + 1) * 512],
                              start=True, stop=True).then_inc(pe_step, 1)
                    done += 2
                    pe.wait_ge(drained, done)
            for g in range(z.HC // 2):
                if g >= 2:
                    pe.wait_ge(drained, done + g - 1)
                for j in range(2):
                    for c in range(z.DC):
                        col = j * z.D + c * P
                        last = pe.transpose(m.bank[6 + g % 2][:, col:col + P],
                                            proj_w[:, c, (2 * g + j) * P:(2 * g + j + 1) * P], m.ident[:, :])
                last.then_inc(pe_step, 1)
            pe.wait_ge(step, dve_done["diag"])
            for c in range(z.DC):
                last = pe.matmul(m.bank[5][:, c * P:(c + 1) * P], ones[:, :], diag[:, c, :], start=True, stop=True)
            last.then_inc(pe_step, 1)
            for w in range(4):
                src = qkv[:, w, :, :] if w < 3 else wo[:, :, :]
                for c in range(z.DC):
                    for o in range(z.DC):
                        col = c * z.D + o * P
                        last = pe.transpose(m.bank[w][:, col:col + P], src[:, o, c * P:(c + 1) * P], m.ident[:, :])
                last.then_inc(pe_step, 1)



def latent_pass(nc, z, m):
    G, DC, GROUPS = z.G, z.DC, z.TILES // z.G
    with ExitStack() as ctx:
        def sb(name, shape, dt=F32):
            return [ctx.enter_context(nc.sbuf_tensor(f"l_{name}{u}", shape, dt)) for u in range(2)]

        raw, mv, sd, rs = sb("raw", [P, G, 6]), sb("mv", [P, G, 2]), sb("sd", [P, G]), sb("rs", [P, G])
        xn, xt, ct = sb("xn", [P, G, z.D]), sb("xt", [P, DC, z.GT]), sb("ct", [P, z.GT])
        parts, rest = sb("parts", [P, PARTS, 4, z.GT], BF16), sb("rest", [P, 4, z.GT])
        vx = sb("vx", [P, G, z.H, 32])
        stored = sems(nc, "l_stored0", "l_stored1")
        (raw_done, mv_ready, sd_ready, rs_ready, xn_ready, turned, xt_ready, c_ready, ct_ready, qk_ready,
         high_done, rest_done, mid_done, low_done, v_ready, vx_ready, ones_ready) = sems(
            nc, "l_raw_done", "l_mv_ready", "l_sd_ready", "l_rs_ready", "l_xn_ready", "l_turned", "l_xt_ready",
            "l_c_ready", "l_ct_ready", "l_qk_ready", "l_high_done", "l_rest_done", "l_mid_done", "l_low_done",
            "l_v_ready", "l_vx_ready", "l_ones_ready")
        block = ctx.enter_context(nc.Block())
        T0, CB, QK0, VB = 0, 2, 3, 7
        STORED = 16 * (PARTS * 4 + G)

        @block.sync
        def _(sp):
            for u in range(2):
                sp.sem_inc(stored[u], STORED)

            def store(i, u):
                n = 2 * i + u
                sp.wait_ge(vx_ready, 2 * n + 3)
                for t in range(G):
                    at = u * z.GT + t * P
                    sp.dma_start(m.v_dram[bass.ts(i, z.UPB), at:at + P, :].rearrange("g p k -> p g k"),
                                 vx[u][:, t, :, :].rearrange("p (g h) k -> p g (h k)", g=z.UPB)).then_inc(stored[u], 16)
                sp.wait_ge(low_done, n + 3)
                store_parts(sp, z, m, parts[u], stored[u], i, u)

            with sp.Fori(0, GROUPS // 2) as i:
                for u in range(2):
                    store(i, u)
            for u in range(2):
                sp.wait_ge(stored[u], STORED * (GROUPS // 2 + 1))

        @block.vector
        def _(dve):
            for u in range(2):
                last = dve.memset(vx[u][:, :, :, 16:32], 1.0)
            last.then_inc(ones_ready, 1)
            dve.sem_inc(rest_done, 4)

            def norm(i, u):
                n = 2 * i + u
                tiles = of_group(z, m.x, n)
                statistics(m, dve, tiles, raw[u], mv[u], raw_done, mv_ready, n)
                inverse(dve, sd[u], rs[u], sd_ready, rs_ready, n)
                dve.wait_ge(turned, n + 1)
                normalise(dve, xn[u], tiles, mv[u], rs[u]).then_inc(xn_ready, 1)

            def split(i, u):
                n = 2 * i + u
                dve.wait_ge(low_done, n + 1)
                for j in range(4):
                    dve.wait_ge(high_done, 4 * n + j + 1)
                    dve.tensor_tensor(rest[u][:, j, :], m.bank[QK0 + j][:, :], parts[u][:, 0, j, :],
                                      ALU.subtract).then_inc(rest_done, 1)
                    dve.wait_ge(rest_done, 4 * n + j + 5)
                    dve.tensor_copy(parts[u][:, 1, j, :], rest[u][:, j, :]).then_inc(mid_done, 1)

            staggered(dve, GROUPS, norm, split)

        @block.gpsimd
        def _(pool):
            pool.sem_inc(low_done, 2)
            with pool.Fori(0, GROUPS // 2) as i:
                for u in range(2):
                    n = 2 * i + u
                    for j in range(4):
                        wait_alone(pool, mid_done, 4 * n + j + 1, m.alone)
                        last = pool.tensor_tensor(parts[u][:, 2, j, :], rest[u][:, j, :], parts[u][:, 1, j, :],
                                                  ALU.subtract)
                    last.then_inc(low_done, 1)

        @block.scalar
        def _(act):
            act.sem_inc(xt_ready, 1)
            act.sem_inc(ct_ready, 1)
            act.sem_inc(vx_ready, 1)

            def root(i, u):
                deviation(act, mv[u], sd[u], m.eps, mv_ready, sd_ready, 2 * i + u)

            def take_turned(i, u):
                n = 2 * i + u
                act.wait_ge(turned, n + 3)
                act.wait_ge(c_ready, n + 1)
                for c in range(DC):
                    last = act.activation(xt[u][:, c, :], m.bank[T0 + c][:, :], ACT.Copy)
                last.then_inc(xt_ready, 1)

            def take_down(i, u):
                n = 2 * i + u
                act.wait_ge(c_ready, n + 3)
                act.wait_ge(v_ready, 2 * n + 2)
                act.activation(ct[u][:, :], m.bank[CB][:, :], ACT.Copy).then_inc(ct_ready, 1)

            def take_heads(i, u):
                n = 2 * i + u
                act.wait_ge(stored[u], STORED * i + STORED)
                for j in range(4):
                    act.wait_ge(qk_ready, 4 * n + j + 1)
                    act.activation(parts[u][:, 0, j, :], m.bank[QK0 + j][:, :], ACT.Copy).then_inc(high_done, 1)
                act.wait_ge(ones_ready, 1)
                for k in range(2):
                    act.wait_ge(v_ready, 2 * n + k + 5)
                    act.activation(vx[u][:, 2 * k:2 * k + 2, :, 0:16],
                                   m.bank[VB][:, :].rearrange("p (t h d) -> p t h d", t=2, d=16),
                                   ACT.Copy).then_inc(vx_ready, 1)

            for u in range(2):
                root(0, u)
                take_turned(0, u)
            with act.Fori(0, GROUPS // 2 - 1) as i:
                for u in range(2):
                    take_down(i, u)
                    root(i + 1, u)
                    take_heads(i, u)
                    take_turned(i + 1, u)
            for u in range(2):
                take_down(GROUPS // 2 - 1, u)
                take_heads(GROUPS // 2 - 1, u)

        @block.tensor
        def _(pe):
            pe.sem_inc(turned, 2)
            pe.sem_inc(c_ready, 2)
            pe.sem_inc(v_ready, 4)

            def turn(i, u):
                n = 2 * i + u
                pe.wait_ge(xn_ready, n + 1)
                pe.wait_ge(xt_ready, n + 1)
                turn_group(pe, z, m.bank[T0:T0 + DC], xn[u], m.ident).then_inc(turned, 1)

            def down(i, u):
                n = 2 * i + u
                pe.wait_ge(xt_ready, n + 2)
                pe.wait_ge(ct_ready, n + 1)
                for c in range(DC):
                    last = pe.matmul(m.bank[CB][:, :], m.w_down[:, c, :], xt[u][:, c, :], start=(c == 0), stop=(c == DC - 1))
                last.then_inc(c_ready, 1)

            def heads(i, u):
                n = 2 * i + u
                pe.wait_ge(ct_ready, n + 2)
                for j in range(4):
                    w = (m.w_uq, m.w_uk)[j // 2]
                    pe.wait_ge(rest_done, 4 * n + j + 1)
                    pe.matmul(m.bank[QK0 + j][:, :], w[:, (j % 2) * P:(j % 2 + 1) * P], ct[u][:, :],
                              start=True, stop=True).then_inc(qk_ready, 1)

            def values(i, u, k):
                n = 2 * i + u
                pe.wait_ge(vx_ready, 2 * n + k + 1)
                for t in range(2):
                    cols = slice((2 * k + t) * P, (2 * k + t + 1) * P)
                    last = pe.matmul(m.bank[VB][:, t * z.D:(t + 1) * z.D], ct[u][:, cols], m.w_uv[:, :],
                                     start=True, stop=True)
                last.then_inc(v_ready, 1)

            for u in range(2):
                turn(0, u)
            with pe.Fori(0, GROUPS // 2 - 1) as i:
                for u in range(2):
                    down(i, u)
                    heads(i, u)
                    values(i, u, 0)
                    turn(i + 1, u)
                    values(i, u, 1)
            for u in range(2):
                down(GROUPS // 2 - 1, u)
                heads(GROUPS // 2 - 1, u)
                for k in range(2):
                    values(GROUPS // 2 - 1, u, k)


def store_parts(eng, z, m, parts, stored, i, u):
    for part in range(PARTS):
        for j in range(4):
            eng.dma_start(m.qk_dram[part, j // 2, bass.ds(i * z.D + (j % 2) * P, P), u * z.GT:(u + 1) * z.GT],
                          parts[:, part, j, :]).then_inc(stored, 16)



def attend_pass(nc, z, m, softmax):
    tag = "a" if softmax else "b"
    RING = 3
    HPU, ST, UNITS = z.HPU, z.ST, z.UNITS
    ROUNDS = (UNITS - 2) // RING
    assert UNITS == RING * ROUNDS + 2
    ROWS = STACK + 2 if softmax else STACK
    steps = [(h, kt) for h in range(2) for kt in range(4 * (h + 1))]
    STEPS = len(steps)
    DIAG = [s for s, (h, kt) in enumerate(steps) if kt >= 4 * h]
    AHEAD = 2
    PAIRS = 2 if softmax else 3
    SLOTS = 4
    chunks = [(hd, pieces) for hd in range(HPU) for pieces in (
        ((0, 0, 0, 128), (2, 0, 128, 384)), ((3, 0, 0, 512),), ((1, 0, 0, 256), (5, 1, 256, 256)),
        ((4, 0, 0, 512),), ((4, 1, 0, 128), (6, 1, 128, 384)), ((5, 0, 0, 512),), ((6, 0, 0, 512),),
        ((7, 0, 0, 512),), ((7, 1, 0, 512),))]
    CH = len(chunks)
    assert CH == 3 * STEPS
    SRING = 3
    with ExitStack() as ctx:
        def sb(name, shape, dt=F32, n=1):
            return [ctx.enter_context(nc.sbuf_tensor(f"{tag}_{name}{u}", shape, dt)) for u in range(n)]

        def sm(*names):
            return sems(nc, *[f"{tag}_{x}" for x in names])

        qs, ks = sb("qs", [P, HPU, z.S], BF16, RING), sb("ks", [P, HPU, z.S], BF16, RING)
        vs = sb("vs", [P, ST, P], F32, RING)
        p = sb("p", [P, HPU, 512], F32, SLOTS)
        osb = sb("osb", [P, 512], F32, 2)
        loaded = sm(*[f"loaded{r}" for r in range(RING)])
        stored = sm("stored0", "stored1")
        st_ready, p_ready, masked, pv_done, o_taken = sm("st_ready", "p_ready", "masked", "pv_done", "o_taken")
        LOADED = 16 * (2 * len(Q_STACK) + 1)
        STORED = 16
        SB, OB = 4, (7 if softmax else 6, 7)
        OT = len(set(OB))
        PV, PR, STK, DR = SLOTS, PAIRS, SRING, 2
        if softmax:
            bias, = sb("bias", [P, 512])
            dump = sb("dump", [P, 512], BF16, SRING)
            peak, = sb("peak", [P, HPU * ST, 2])
            npeak, = sb("npeak", [P, HPU * ST])
            split, = sb("split", [P, 2, HPU * ST], BF16)
            rows, = sb("rows", [P, 2, HPU * ST], BF16)
            rows_loaded = sm(*[f"rows_loaded{r}" for r in range(RING)])
            (bias_zero, bias_ready, peak_set, s_ready, s_taken, npeak_ready, high_ready, split_ready,
             rows_ready, ones_ready) = sm("bias_zero", "bias_ready", "peak_set", "s_ready", "s_taken", "npeak_ready",
                                          "high_ready", "split_ready", "rows_ready", "ones_ready")
            ROWS_LOADED = 16 * 8
        else:
            twin = sb("twin", [P, 512], F32, 2)
            twin_ready, d_ready = sm("twin_ready", "d_ready")
        block = ctx.enter_context(nc.Block())

        def q0(s):
            h, kt = steps[s]
            return max(0, kt * P - h * 512)

        def score_bank(s, hd):
            return 2 * ((2 * s + hd // 2) % PAIRS) + hd % 2

        def all_units(eng, unit):
            with eng.Fori(0, ROUNDS) as i:
                for r in range(RING):
                    unit(RING * i + r, r, i, True, True)
            unit(UNITS - 2, 0, ROUNDS, True, False)
            unit(UNITS - 1, 1, ROUNDS, False, False)

        @block.sync
        def _(sp):
            for u in range(2):
                sp.sem_inc(stored[u], STORED)

            def load(n, r):
                for tile, which, stack in ((qs[r], 0, Q_STACK), (ks[r], 1, K_STACK)):
                    row = 0
                    for first, step, groups in stack:
                        last = first + step * (groups - 1) + 1
                        src = m.qk_dram[first:last, which, bass.ts(n, HPU * z.DK), :]
                        src = src.rearrange("g (d h) t -> g d (h t)", h=HPU)
                        if not step:
                            src = src.to_broadcast([groups, z.DK, HPU * z.S])
                        sp.dma_start(tile[row:row + 16 * groups, :, :].rearrange("p h t -> p (h t)"), src
                                     ).then_inc(loaded[r], 16)
                        row += 16 * groups
                sp.dma_start(vs[r][:, :, :], m.v_dram[bass.ts(n, 1), :, :].rearrange("n (k p) c -> p (n k) c", p=P)
                             ).then_inc(loaded[r], 16)

            def load_rows(n, r):
                sp.wait_ge(rows_ready, n + 1)
                for k in range(2):
                    at = qs[r][STACK + k:STACK + k + 1, :, :].rearrange("o h (q b i) -> o (h q) b i", b=4, i=32)
                    for b in range(4):
                        sp.dma_start(at[:, :, b, :], rows[32 * b:32 * b + 32, k, :]).then_inc(rows_loaded[r], 16)

            def store(n, h):
                sp.wait_ge(o_taken, 2 * n + h + 1 + OT)
                sp.dma_start(m.sums_dram[bass.ts(n, P), h * 512:(h + 1) * 512], osb[h][:, :]).then_inc(stored[h], 16)

            def unit(n, r, rnd, ahead, far):
                if far:
                    sp.wait_ge(pv_done, STEPS * n + PV)
                    load(n + 2, (r + 2) % RING)
                store(n, 0)
                if softmax and ahead:
                    load_rows(n + 1, (r + 1) % RING)
                store(n, 1)

            load(0, 0)
            load(1, 1)
            if softmax:
                load_rows(0, 0)
            all_units(sp, unit)
            for h in range(2):
                sp.wait_ge(stored[h], STORED * (UNITS + 1))

        @block.gpsimd
        def _(pool):
            if softmax:
                pool.memset(bias[:, :], 0.0).then_inc(bias_zero, 1)
                pool.wait_ge(bias_zero, 1)
                pool.affine_select(out=bias[:, 512 - P:], in_=bias[:, 512 - P:], compare_op=ALU.is_ge, fill=NEG,
                                   base=0, pattern=[[-1, P]], channel_multiplier=1).then_inc(bias_ready, 1)

            def unit(n, r, rnd, ahead, far):
                for d, s in enumerate(DIAG):
                    if not softmax:
                        pool.wait_ge(d_ready, STEPS * n + s + 1 + DR)
                    wait_alone(pool, p_ready, 2 * STEPS * n + 2 * s + 2 + PR, m.alone)
                    diag = p[s % SLOTS][:, :, q0(s):q0(s) + P]
                    pool.affine_select(out=diag, in_=diag, compare_op=ALU.is_ge, fill=0.0, base=0,
                                       pattern=[[0, HPU], [1, P]], channel_multiplier=-1).then_inc(masked, 1)

            all_units(pool, unit)

        @block.scalar
        def _(act):
            act.sem_inc(p_ready, PR)
            act.sem_inc(o_taken, OT)

            def take_sums(n, h):
                act.wait_ge(pv_done, STEPS * n + (4, STEPS)[h] + PV)
                act.wait_ge(stored[h], STORED * n + STORED)
                act.activation(osb[h][:, :], m.bank[OB[h]], ACT.Copy).then_inc(o_taken, 1)

            def weights(n, s):
                act.wait_ge(pv_done, STEPS * n + s + 1)
                for k in range(2):
                    act.wait_ge(st_ready, 2 * STEPS * n + 2 * s + k + 1)
                    heads = 2 if softmax or k == 0 else 1
                    at = score_bank(s, 2 * k)
                    act.activation(p[s % SLOTS][:, 2 * k:2 * k + heads, q0(s):512], m.psum[:, at:at + heads, q0(s):512],
                                   ACT.Exp if softmax else ACT.Square, scale=z.DK ** -0.5).then_inc(p_ready, 1)

            def unit(n, r, rnd, ahead, far):
                for s in range(STEPS):
                    if s + AHEAD < STEPS:
                        weights(n, s + AHEAD)
                    elif ahead:
                        weights(n + 1, s + AHEAD - STEPS)
                    if s == 3:
                        take_sums(n, 0)
                take_sums(n, 1)

            for s in range(AHEAD):
                weights(0, s)
            all_units(act, unit)

        @block.vector
        def _(dve):
            if not softmax:
                dve.sem_inc(d_ready, DR)

                def unit(n, r, rnd, ahead, far):
                    for s in range(STEPS):
                        dve.wait_ge(st_ready, 2 * STEPS * n + 2 * s + 2)
                        bank = m.bank[score_bank(s, 3)][:, q0(s):512]
                        dve.tensor_copy(twin[s % 2][:, q0(s):512], bank).then_inc(twin_ready, 1)
                        dve.wait_ge(pv_done, STEPS * n + s + 1)
                        dve.wait_ge(twin_ready, STEPS * n + s + 1)
                        dve.scalar_tensor_tensor(out=p[s % SLOTS][:, 3, q0(s):512], in0=bank, scalar=1.0 / z.DK,
                                                 in1=twin[s % 2][:, q0(s):512], op0=ALU.mult, op1=ALU.mult
                                                 ).then_inc(d_ready, 1)

                all_units(dve, unit)
                return
            for r in range(RING):
                last = dve.memset(ks[r][STACK:STACK + 2, :, :], 1.0)
            last.then_inc(ones_ready, 1)
            dve.memset(peak[:, :, :], NEG).then_inc(peak_set, 1)
            dve.sem_inc(s_taken, STK)
            dve.wait_ge(peak_set, 1)
            dve.wait_ge(bias_ready, 1)

            def maxima(n, a, b):
                for c in range(a, b):
                    hd, pieces = chunks[c]
                    wait_alone(dve, s_ready, CH * n + c + 1, m.alone)
                    for qt, h, at, w in pieces:
                        piece, dst = m.bank[SB + c % SRING][:, at:at + w], peak[:, hd * ST + qt, h:h + 1]
                        if h < qt // 4:
                            last = dve.tensor_reduce(dst, piece, AX.X, ALU.max)
                        else:
                            last = dve.tensor_tensor_reduce(dump[c % SRING][:, at:at + w], piece, bias[:, 512 - w:], 1.0,
                                                            NEG, ALU.add, ALU.max, dst)
                    last.then_inc(s_taken, 1)

            def largest(n, before):
                dve.wait_ge(s_taken, CH * n + CH + STK)
                dve.tensor_reduce(npeak[:, :], peak[:, :, :], AX.X, ALU.max, negate=True).then_inc(npeak_ready, 1)
                dve.wait_ge(npeak_ready, n + 1)
                dve.tensor_copy(split[:, 0, :], npeak[:, :]).then_inc(high_ready, 1)
                dve.wait_ge(high_ready, n + 1)
                dve.tensor_tensor(split[:, 1, :], npeak[:, :], split[:, 0, :], ALU.subtract).then_inc(split_ready, 1)
                if before:
                    dve.wait_ge(*before)
                dve.wait_ge(split_ready, n + 1)
                dve.transpose(rows[:, :, :].rearrange("p k c -> p (k c)"), split[:, :, :].rearrange("p k c -> p (k c)")
                              ).then_inc(rows_ready, 1)

            def unit(n, r, rnd, ahead, far):
                if ahead:
                    maxima(n + 1, CH // 2, CH)
                    largest(n + 1, (rows_loaded[r], ROWS_LOADED * rnd + ROWS_LOADED))
                if far:
                    maxima(n + 2, 0, CH // 2)

            maxima(0, 0, CH)
            largest(0, None)
            maxima(1, 0, CH // 2)
            all_units(dve, unit)

        @block.tensor
        def _(pe):
            pe.sem_inc(pv_done, PV)
            if softmax:
                pe.wait_ge(ones_ready, 1)

            def maximum_scores(n, r, a, b):
                for c in range(a, b):
                    hd, pieces = chunks[c]
                    pe.wait_ge(s_taken, CH * n + c + 1)
                    for qt, h, at, w in pieces:
                        last = pe.matmul(m.bank[SB + c % SRING][:, at:at + w], qs[r][0:STACK, hd, qt * P:(qt + 1) * P],
                                         ks[r][0:STACK, hd, h * 512:h * 512 + w], start=True, stop=True)
                    last.then_inc(s_ready, 1)

            def scores(n, r, s, k):
                h, kt = steps[s]
                pe.wait_ge(p_ready, 2 * STEPS * n + 2 * s + k + 1)
                if not softmax and k == 0:
                    pe.wait_ge(d_ready, STEPS * n + s + 1)
                for hd in (2 * k, 2 * k + 1):
                    last = pe.matmul(m.bank[score_bank(s, hd)][:, q0(s):512], ks[r][0:ROWS, hd, kt * P:(kt + 1) * P],
                                     qs[r][0:ROWS, hd, h * 512 + q0(s):(h + 1) * 512], start=True, stop=True)
                last.then_inc(st_ready, 1)

            def weigh(n, r, s):
                h, kt = steps[s]
                pe.wait_ge(p_ready, 2 * STEPS * n + 2 * s + 2 + PR)
                if not softmax:
                    pe.wait_ge(d_ready, STEPS * n + s + 1 + DR)
                if s in DIAG:
                    pe.wait_ge(masked, len(DIAG) * n + DIAG.index(s) + 1)
                if kt == 0:
                    pe.wait_ge(o_taken, 2 * n + h + 1)
                for hd in range(HPU):
                    last = pe.matmul(m.bank[OB[h]][32 * hd:32 * hd + 32, q0(s):512], vs[r][:, kt, 32 * hd:32 * hd + 32],
                                     p[s % SLOTS][:, hd, q0(s):512], start=(kt == 0), stop=(kt == 4 * h + 3),
                                     skip_group_check=True)
                last.then_inc(pv_done, 1)

            def operands(n, r, rnd):
                pe.wait_ge(loaded[r], LOADED * rnd + LOADED)
                if softmax:
                    pe.wait_ge(rows_loaded[r], ROWS_LOADED * rnd + ROWS_LOADED)

            def unit(n, r, rnd, ahead, far):
                def some_maxima(k):
                    if not softmax:
                        return
                    half = CH // 2
                    if k < half and ahead:
                        maximum_scores(n + 1, (r + 1) % RING, half + k, half + k + 1)
                    if k >= half and far:
                        if k == half:
                            pe.wait_ge(loaded[(r + 2) % RING], LOADED * (rnd + (r + 2) // RING) + LOADED)
                        maximum_scores(n + 2, (r + 2) % RING, k - half, k - half + 1)

                for s in range(STEPS):
                    t = s + AHEAD
                    there = t < STEPS or ahead
                    if t == STEPS and ahead:
                        operands(n + 1, (r + 1) % RING, rnd + (r + 1) // RING)
                    at = (n, r, t) if t < STEPS else (n + 1, (r + 1) % RING, t - STEPS)
                    if there:
                        scores(*at, 0)
                    some_maxima(3 * s)
                    if there:
                        scores(*at, 1)
                    some_maxima(3 * s + 1)
                    weigh(n, r, s)
                    some_maxima(3 * s + 2)

            if softmax:
                pe.wait_ge(loaded[0], LOADED)
                maximum_scores(0, 0, 0, CH)
                pe.wait_ge(loaded[1], LOADED)
                maximum_scores(1, 1, 0, CH // 2)
            operands(0, 0, 0)
            for s in range(AHEAD):
                for k in range(2):
                    scores(0, 0, s, k)
            all_units(pe, unit)



def mix_pass(nc, z, m, wo, den_eps, normed=None):
    tag = "m0" if den_eps is None else "m1"
    G, DC, GROUPS = z.G, z.DC, z.TILES // z.G
    with ExitStack() as ctx:
        def sb(name, shape, dt=F32):
            return [ctx.enter_context(nc.sbuf_tensor(f"{tag}_{name}{u}", shape, dt)) for u in range(2)]

        num, inv, att = sb("num", [P, DC, z.GT]), sb("inv", [P, DC, z.GT]), sb("att", [P, DC, z.GT])
        dens = ctx.enter_context(nc.sbuf_tensor(f"{tag}_dens", [P, z.S], F32))
        raw, mv, sd, rs = sb("raw", [P, G, 6]), sb("mv", [P, G, 2]), sb("sd", [P, G]), sb("rs", [P, G])
        zt, sums_offset = sb("zt", [P, G, z.D]), sb("sums_offset", [P, G])
        sums_offset_ready, = sems(nc, f"{tag}_sums_offset_ready")
        loaded = sems(nc, f"{tag}_loaded0", f"{tag}_loaded1")
        (dens_loaded, padded, inverted, inv_stored, att_ready, y_ready, raw_done, mv_ready, sd_ready, rs_ready,
         zt_ready, added) = sems(nc, *[f"{tag}_{x}" for x in (
             "dens_loaded", "padded", "inverted", "inv_stored", "att_ready", "y_ready", "raw_done", "mv_ready",
             "sd_ready", "rs_ready", "zt_ready", "added")])
        if normed is not None:
            raw2, mv2, sd2, rs2 = sb("raw2", [P, G, 6]), sb("mv2", [P, G, 2]), sb("sd2", [P, G]), sb("rs2", [P, G])
            offset = sb("offset", [P, G])
            (raw2_done, mv2_ready, sd2_ready, rs2_ready, offset_ready, inner_ready, gained, normed_ready, peaked) = sems(
                nc, *["m_" + x for x in ("raw2_done", "mv2_ready", "sd2_ready", "rs2_ready", "offset_ready",
                                         "inner_ready", "gained", "normed_ready", "peaked")])
        block = ctx.enter_context(nc.Block())
        HPC = P // z.DK
        LOADED = 16 * 2 * DC
        assert z.B * z.H == P

        def banks(u):
            return [m.psum[:, 2 * u + t // 2, (t % 2) * z.D:(t % 2 + 1) * z.D] for t in range(G)]

        @block.sync
        def _(sp):
            heads = m.sums_dram.rearrange("(h k) t -> h k t", k=32)
            sp.dma_start(dens[:, :], heads[:, z.DK, :]).then_inc(dens_loaded, 16)
            sp.wait_ge(inverted, 1)
            sp.dma_start(m.inv_dram, dens[:, :]).then_inc(inv_stored, 16)
            sp.wait_ge(inv_stored, 16)
            with sp.Fori(0, GROUPS // 2) as i:
                for u in range(2):
                    n = 2 * i + u
                    sp.wait_ge(att_ready, n + 1)
                    for c in range(DC):
                        src = heads[bass.ds(z.H * i + HPC * c, HPC), 0:z.DK, u * z.GT:(u + 1) * z.GT]
                        sp.dma_start(num[u][:, c, :], src).then_inc(loaded[u], 16)
                        rows = m.inv_dram[bass.ds(z.H * i + HPC * c, HPC), u * z.GT:(u + 1) * z.GT]
                        sp.dma_start(inv[u][:, c, :], rows.unsqueeze(1).to_broadcast([HPC, z.DK, z.GT])
                                     ).then_inc(loaded[u], 16)

        @block.vector
        def _(dve):
            dve.sem_inc(zt_ready, 2)
            dve.wait_ge(dens_loaded, 16)
            if den_eps is not None:
                dve.tensor_scalar(dens[:, :], dens[:, :], den_eps, None, ALU.add).then_inc(padded, 1)
                dve.wait_ge(padded, 1)
            dve.reciprocal(dens[:, :], dens[:, :]).then_inc(inverted, 1)

            def norm(i, u):
                measure_sums(m, dve, banks(u), raw[u], mv[u], sd[u], rs[u], sums_offset[u], y_ready, raw_done, mv_ready,
                             sd_ready, rs_ready, zt_ready, sums_offset_ready, 2 * i + u)

            def measure(i, u):
                n = 2 * i + u
                dve.wait_ge(added, n + 3)
                statistics(m, dve, of_group(z, m.x, n), raw2[u], mv2[u], raw2_done, mv2_ready, n)

            def divisor(i, u):
                n = 2 * i + u
                dve.wait_ge(inner_ready, n + 1)
                inverse(dve, sd2[u], rs2[u], sd2_ready, rs2_ready, n)
                dve.scalar_tensor_tensor(out=offset[u][:, :], in0=mv2[u][:, :, 0], scalar=-1.0, in1=rs2[u][:, :],
                                         op0=ALU.mult, op1=ALU.mult).then_inc(offset_ready, 1)

            def gain(i, u):
                n = 2 * i + u
                dve.wait_ge(inner_ready, n + 3)
                view = normed[:, bass.ts(n, G), :]
                dve.tensor_tensor(view, view, m.ln_gamma[:, :].unsqueeze(1).to_broadcast([P, G, z.D]),
                                  ALU.mult).then_inc(gained, 1)

            def largest(i, u):
                n = 2 * i + u
                dve.wait_ge(normed_ready, n + 1)
                dve.tensor_reduce(m.peaks[:, bass.ds(n, 1)], normed[:, bass.ts(n, G), :], AX.XY, ALU.max,
                                  apply_absolute_value=True).then_inc(peaked, 1)

            if normed is None:
                lagged(dve, GROUPS, (0, norm))
            else:
                lagged(dve, GROUPS, (1, measure), (0, norm), (1, divisor), (2, gain), (3, largest))

        @block.gpsimd
        def _(pool):
            pool.sem_inc(added, 2)
            pool.sem_inc(att_ready, 2)

            def divide(i, u):
                n = 2 * i + u
                pool.wait_ge(y_ready, n + 1)
                pool.wait_ge(loaded[u], LOADED * i + LOADED)
                pool.sem_inc(m.alone, 1)
                pool.tensor_tensor(att[u][:, :, :], num[u][:, :, :], inv[u][:, :, :], ALU.mult).then_inc(att_ready, 1)

            def add(i, u):
                add_group(pool, z, m, zt, zt_ready, added, i, u, 2)

            def shift(i, u):
                n = 2 * i + u
                wait_alone(pool, gained, n + 1, m.alone)
                view = normed[:, bass.ts(n, G), :]
                pool.tensor_tensor(view, view, m.ln_beta[:, :].unsqueeze(1).to_broadcast([P, G, z.D]),
                                   ALU.add).then_inc(normed_ready, 1)

            if normed is None:
                lagged(pool, GROUPS, (0, divide), (1, add))
            else:
                lagged(pool, GROUPS, (0, divide), (1, add), (3, shift))

        @block.scalar
        def _(act):
            if normed is not None:
                act.sem_inc(inner_ready, 2)

            def root(i, u):
                deviation(act, mv[u], sd[u], m.eps, mv_ready, sd_ready, 2 * i + u)

            def root2(i, u):
                deviation(act, mv2[u], sd2[u], m.eps_both, mv2_ready, sd2_ready, 2 * i + u, scale=1.0 + EPS_IN)

            def inner(i, u):
                n = 2 * i + u
                act.wait_ge(offset_ready, n + 1)
                for t, (dst, tile) in enumerate(zip(of_group(z, normed, n), of_group(z, m.x, n))):
                    last = act.activation(dst, tile, ACT.Identity, bias=offset[u][:, t:t + 1], scale=rs2[u][:, t:t + 1])
                last.then_inc(inner_ready, 1)

            def sums(i, u):
                normalise_sums(act, banks(u), rs[u], sums_offset[u], zt[u], sums_offset_ready, added, zt_ready, 2 * i + u)

            if normed is None:
                lagged(act, GROUPS, (0, root), (0, sums))
            else:
                lagged(act, GROUPS, (1, root2), (0, root), (0, sums), (1, inner))

        @block.tensor
        def _(pe):
            pe.sem_inc(y_ready, 2)
            with pe.Fori(0, GROUPS // 2) as i:
                for u in range(2):
                    n = 2 * i + u
                    pe.wait_ge(att_ready, n + 3)
                    pe.wait_ge(zt_ready, n + 1)
                    for t, bank in enumerate(banks(u)):
                        for c in range(DC):
                            last = pe.matmul(bank, att[u][:, c, t * P:(t + 1) * P], wo[:, c, :], start=(c == 0),
                                             stop=(c == DC - 1))
                    last.then_inc(y_ready, 1)


def norm_sums(m, dve, sums, raw, mv, sd, rs, zt, sums_ready, raw_done, mv_ready, sd_ready, rs_ready, added, zt_ready,
              n, credit):
    dve.wait_ge(sums_ready, n + 1 + credit)
    statistics(m, dve, sums, raw, mv, raw_done, mv_ready, n)
    inverse(dve, sd, rs, sd_ready, rs_ready, n)
    dve.wait_ge(added, n + 1)
    normalise(dve, zt, sums, mv, rs).then_inc(zt_ready, 1)


def measure_sums(m, dve, banks, raw, mv, sd, rs, offset, y_ready, raw_done, mv_ready, sd_ready, rs_ready, zt_ready,
                 offset_ready, n, gain=None):
    dve.wait_ge(y_ready, n + 3)
    statistics(m, dve, banks, raw, mv, raw_done, mv_ready, n)
    dve.wait_ge(zt_ready, n + 1)
    inverse(dve, sd, rs, sd_ready, rs_ready, n)
    if gain:
        factor, gained, ready = gain
        dve.tensor_scalar(gained[:, :], rs[:, :], factor, None, ALU.mult).then_inc(ready, 1)
        dve.wait_ge(ready, n + 1)
        rs = gained
    dve.scalar_tensor_tensor(out=offset[:, :], in0=mv[:, :, 0], scalar=-1.0, in1=rs[:, :], op0=ALU.mult,
                             op1=ALU.mult).then_inc(offset_ready, 1)


def normalise_sums(act, banks, rs, offset, zt, offset_ready, added, zt_ready, n):
    act.wait_ge(offset_ready, n + 1)
    act.wait_ge(added, n + 1)
    for t, bank in enumerate(banks):
        last = act.activation(zt[:, t, :], bank, ACT.Identity, bias=offset[:, t:t + 1], scale=rs[:, t:t + 1])
    last.then_inc(zt_ready, 1)


def add_group(pool, z, m, zt, zt_ready, added, i, u, credit):
    n = 2 * i + u
    wait_alone(pool, zt_ready, n + 1 + credit, m.alone)
    x = m.x[:, bass.ts(n, z.G), :]
    pool.tensor_tensor(x, x, zt[u][:, :, :], ALU.add).then_inc(added, 1)


def add_to_x(pool, z, m, zt, zt_ready, added, groups):
    pool.sem_inc(added, 2)
    with pool.Fori(0, groups // 2) as i:
        for u in range(2):
            add_group(pool, z, m, zt, zt_ready, added, i, u, 2)



def mlp_pass(nc, z, m):
    G, DC, HC, GROUPS = z.G, z.DC, z.HC, z.TILES // z.G
    with ExitStack() as ctx:
        def sb(name, shape, dt=F32, n=2):
            return [ctx.enter_context(nc.sbuf_tensor(f"f_{name}{u}", shape, dt)) for u in range(n)]

        raw, mv, sd, rs = sb("raw", [P, G, 6]), sb("mv", [P, G, 2]), sb("sd", [P, G]), sb("rs", [P, G])
        raw2, mv2, sd2, rs2 = sb("raw2", [P, G, 6]), sb("mv2", [P, G, 2]), sb("sd2", [P, G]), sb("rs2", [P, G])
        xn, xt, zt = sb("xn", [P, G, z.D]), sb("xt", [P, DC, z.GT]), sb("zt", [P, G, z.D])
        hid, rest = sb("hid", [P, z.GT], n=4), sb("rest", [P, z.GT], n=4)
        parts = sb("parts", [P, PARTS, HC, z.GT], BF16)
        scaled = ctx.enter_context(nc.sbuf_tensor("f_scaled", [P, G, z.D], F32))
        (raw_done, mv_ready, sd_ready, rs_ready, xn_ready, turned, xt_ready, fc_ready, relu_ready, squared, high_ready,
         rest_ready, mid_ready, low_ready, y_ready, scaled_ready,
         raw2_done, mv2_ready, sd2_ready, rs2_ready, zt_ready, added) = sems(nc, *["f_" + x for x in (
             "raw_done", "mv_ready", "sd_ready", "rs_ready", "xn_ready", "turned", "xt_ready", "fc_ready", "relu_ready",
             "squared", "high_ready", "rest_ready", "mid_ready", "low_ready", "y_ready", "scaled_ready", "raw2_done", "mv2_ready", "sd2_ready", "rs2_ready", "zt_ready", "added")])
        block = ctx.enter_context(nc.Block())
        T0, F0, Y0 = 0, 2, 6
        banks = [m.psum[:, Y0 + t // 2, (t % 2) * z.D:(t % 2 + 1) * z.D] for t in range(G)]

        @block.vector
        def _(dve):
            dve.sem_inc(rest_ready, 4)
            dve.sem_inc(scaled_ready, 1)
            dve.sem_inc(zt_ready, 1)

            def norm(i, u):
                n = 2 * i + u
                tiles = of_group(z, m.x, n)
                statistics(m, dve, tiles, raw[u], mv[u], raw_done, mv_ready, n)
                inverse(dve, sd[u], rs[u], sd_ready, rs_ready, n)
                dve.wait_ge(turned, n + 1)
                normalise(dve, xn[u], tiles, mv[u], rs[u]).then_inc(xn_ready, 1)

            def square(i, u):
                n = 2 * i + u
                for j in range(HC + 1):
                    if j < HC:
                        dve.wait_ge(relu_ready, HC * n + j + 5)
                        dve.tensor_tensor(hid[j % 4][:, :], hid[j % 4][:, :], hid[j % 4][:, :], ALU.mult
                                          ).then_inc(squared, 1)
                    if j:
                        c = j - 1
                        dve.wait_ge(low_ready, HC * n + c + 1)
                        dve.wait_ge(high_ready, HC * n + c + 1)
                        dve.tensor_tensor(rest[c % 4][:, :], hid[c % 4][:, :], parts[u][:, 0, c, :], ALU.subtract
                                          ).then_inc(rest_ready, 1)
                        dve.wait_ge(rest_ready, HC * n + c + 5)
                        dve.tensor_copy(parts[u][:, 1, c, :], rest[c % 4][:, :]).then_inc(mid_ready, 1)

            def out(i, u):
                n = 2 * i + u
                dve.wait_ge(zt_ready, n + 1)
                dve.wait_ge(y_ready, n + 3)
                dve.tensor_tensor(scaled[:, :, :], m.psum[:, Y0:Y0 + 2, :].rearrange("p b (t d) -> p (b t) d", d=z.D),
                                  m.proj_scale[:, :].unsqueeze(1).to_broadcast([P, G, z.D]), ALU.mult
                                  ).then_inc(scaled_ready, 1)
                norm_sums(m, dve, [scaled[:, t, :] for t in range(G)], raw2[u], mv2[u], sd2[u], rs2[u], zt[u],
                          scaled_ready, raw2_done, mv2_ready, sd2_ready, rs2_ready, added, zt_ready, n, 1)

            def two_groups(i, first=False):
                norm(i + 1, 0)
                if not first:
                    out(i - 1, 1)
                square(i, 1)
                norm(i + 1, 1)
                out(i, 0)
                square(i + 1, 0)

            for u in range(2):
                norm(0, u)
            square(0, 0)
            two_groups(0, first=True)
            with dve.Fori(1, GROUPS // 2 - 1) as i:
                two_groups(i)
            out(GROUPS // 2 - 2, 1)
            square(GROUPS // 2 - 1, 1)
            for u in range(2):
                out(GROUPS // 2 - 1, u)

        @block.gpsimd
        def _(pool):
            pool.sem_inc(low_ready, 4)
            pool.sem_inc(added, 2)

            def low(i, u):
                n = 2 * i + u
                for j in range(HC):
                    wait_alone(pool, mid_ready, HC * n + j + 1, m.alone)
                    pool.tensor_tensor(parts[u][:, 2, j, :], rest[j % 4][:, :], parts[u][:, 1, j, :], ALU.subtract
                                       ).then_inc(low_ready, 1)

            def add(i, u):
                add_group(pool, z, m, zt, zt_ready, added, i, u, 1)

            low(0, 0)
            with pool.Fori(0, GROUPS // 2 - 1) as i:
                low(i, 1)
                add(i, 0)
                low(i + 1, 0)
                add(i, 1)
            low(GROUPS // 2 - 1, 1)
            for u in range(2):
                add(GROUPS // 2 - 1, u)

        @block.scalar
        def _(act):
            act.sem_inc(xt_ready, 1)
            act.sem_inc(relu_ready, 4)

            def root(i, u):
                deviation(act, mv[u], sd[u], m.eps, mv_ready, sd_ready, 2 * i + u)

            def take_turned(i, u):
                n = 2 * i + u
                act.wait_ge(turned, n + 3)
                act.wait_ge(fc_ready, HC * n + HC)
                for c in range(DC):
                    last = act.activation(xt[u][:, c, :], m.bank[T0 + c], ACT.Copy)
                last.then_inc(xt_ready, 1)

            def rectify(i, u):
                n = 2 * i + u
                for j in range(HC + 1):
                    if j < HC:
                        act.wait_ge(fc_ready, HC * n + j + 1 + 2 * HC)
                        act.wait_ge(rest_ready, HC * n + j + 1)
                        act.activation(hid[j % 4][:, :], m.bank[F0 + j % 4], ACT.Relu).then_inc(relu_ready, 1)
                    if j == 1:
                        act.wait_ge(y_ready, n + 1)
                    if j:
                        act.wait_ge(squared, HC * n + j)
                        act.activation(parts[u][:, 0, j - 1, :], hid[(j - 1) % 4][:, :], ACT.Copy).then_inc(high_ready, 1)

            def root2(i, u):
                deviation(act, mv2[u], sd2[u], m.eps, mv2_ready, sd2_ready, 2 * i + u)

            def two_groups(i, first=False):
                root(i + 1, 0)
                if not first:
                    take_turned(i, 1)
                    root2(i - 1, 1)
                rectify(i, 1)
                root(i + 1, 1)
                take_turned(i + 1, 0)
                root2(i, 0)
                rectify(i + 1, 0)

            for u in range(2):
                root(0, u)
                take_turned(0, u)
            rectify(0, 0)
            two_groups(0, first=True)
            with act.Fori(1, GROUPS // 2 - 1) as i:
                two_groups(i)
            take_turned(GROUPS // 2 - 1, 1)
            root2(GROUPS // 2 - 2, 1)
            rectify(GROUPS // 2 - 1, 1)
            for u in range(2):
                root2(GROUPS // 2 - 1, u)

        @block.tensor
        def _(pe):
            pe.sem_inc(turned, 2)
            pe.sem_inc(fc_ready, 2 * HC)
            pe.sem_inc(y_ready, 2)

            def turn(i, u):
                n = 2 * i + u
                pe.wait_ge(xn_ready, n + 1)
                pe.wait_ge(xt_ready, n + 1)
                turn_group(pe, z, m.bank[T0:T0 + DC], xn[u], m.ident).then_inc(turned, 1)

            def hidden(i, u):
                n = 2 * i + u
                pe.wait_ge(xt_ready, n + 2)
                for j in range(HC):
                    pe.wait_ge(relu_ready, HC * n + j + 1)
                    for c in range(DC):
                        last = pe.matmul(m.bank[F0 + j % 4], m.w_fc[:, c, j * P:(j + 1) * P], xt[u][:, c, :],
                                         start=(c == 0), stop=(c == DC - 1))
                    last.then_inc(fc_ready, 1)

            def project(i, u):
                n = 2 * i + u
                pe.wait_ge(scaled_ready, n + 1)
                pe.wait_ge(low_ready, HC * n + HC + 4)
                for t, bank in enumerate(banks):
                    for part in range(PARTS):
                        for j in range(HC):
                            last = pe.matmul(bank, parts[u][:, part, j, t * P:(t + 1) * P], m.w_proj[:, j, :],
                                             start=(part == j == 0), stop=(part == PARTS - 1 and j == HC - 1))
                last.then_inc(y_ready, 1)

            for u in range(2):
                turn(0, u)
            hidden(0, 0)
            with pe.Fori(0, GROUPS // 2 - 1) as i:
                hidden(i, 1)
                turn(i + 1, 0)
                project(i, 0)
                hidden(i + 1, 0)
                turn(i + 1, 1)
                project(i, 1)
            hidden(GROUPS // 2 - 1, 1)
            for u in range(2):
                project(GROUPS // 2 - 1, u)



def features_pass(nc, z, m):
    G, DC, GROUPS, H2 = z.G, z.DC, z.TILES // z.G, 2 * z.H
    W = 2 * z.D
    with ExitStack() as ctx:
        def sb(name, shape, dt=F32):
            return [ctx.enter_context(nc.sbuf_tensor(f"g_{name}{u}", shape, dt)) for u in range(2)]

        raw, mv, sd, rs = sb("raw", [P, G, 6]), sb("mv", [P, G, 2]), sb("sd", [P, G]), sb("rs", [P, G])
        xn, xt = sb("xn", [P, G, z.D]), sb("xt", [P, DC, z.GT])
        qk, sq = sb("qk", [P, G, W]), sb("sq", [P, W])
        var, hsd, hrs = sb("var", [P, G, H2]), sb("hsd", [P, G, H2]), sb("hrs", [P, G, H2])
        feat = sb("feat", [P, 4, z.GT])
        parts = sb("parts", [P, PARTS, 4, z.GT], BF16)
        rest = ctx.enter_context(nc.sbuf_tensor("g_rest", [P, 4, z.GT], F32))
        vx = sb("vx", [P, G, z.H, 32])
        v_stored, stored = sems(nc, "g_v_stored0", "g_v_stored1"), sems(nc, "g_stored0", "g_stored1")
        (raw_done, mv_ready, sd_ready, rs_ready, xn_ready, turned, xt_ready, qk_ready, qk_taken, sq_ready, var_ready,
         hsd_ready, hrs_ready, qn_ready, ft_ready, feat_ready, high_done, rest_done, mid_done, low_done, v_ready,
         vx_ready, ones_ready) = sems(nc, *["g_" + x for x in (
             "raw_done", "mv_ready", "sd_ready", "rs_ready", "xn_ready", "turned", "xt_ready", "qk_ready", "qk_taken",
             "sq_ready", "var_ready", "hsd_ready", "hrs_ready", "qn_ready", "ft_ready", "feat_ready", "high_done",
             "rest_done", "mid_done", "low_done", "v_ready", "vx_ready", "ones_ready")])
        block = ctx.enter_context(nc.Block())
        T0, Q0, VB, F0 = 0, 2, 4, 5
        V_STORED, STORED = 16 * G, 16 * PARTS * 4

        @block.sync
        def _(sp):
            for u in range(2):
                sp.sem_inc(v_stored[u], V_STORED)
                sp.sem_inc(stored[u], STORED)

            def store_values(i, u):
                sp.wait_ge(vx_ready, 2 * (2 * i + u) + 3)
                for t in range(G):
                    at = u * z.GT + t * P
                    sp.dma_start(m.v_dram[bass.ts(i, z.UPB), at:at + P, :].rearrange("g p k -> p g k"),
                                 vx[u][:, t, :, :].rearrange("p (g h) k -> p g (h k)", g=z.UPB)).then_inc(v_stored[u], 16)

            def store_features(i, u):
                sp.wait_ge(low_done, 2 * i + u + 2)
                store_parts(sp, z, m, parts[u], stored[u], i, u)

            staggered(sp, GROUPS, store_values, store_features)
            for u in range(2):
                sp.wait_ge(v_stored[u], V_STORED * (GROUPS // 2 + 1))
                sp.wait_ge(stored[u], STORED * (GROUPS // 2 + 1))

        @block.vector
        def _(dve):
            for u in range(2):
                last = dve.memset(vx[u][:, :, :, 16:32], 1.0)
            last.then_inc(ones_ready, 1)
            dve.sem_inc(var_ready, 2)
            dve.sem_inc(rest_done, 2)

            def measure(i, u):
                n = 2 * i + u
                statistics(m, dve, of_group(z, m.x, n), raw[u], mv[u], raw_done, mv_ready, n)

            def norm(i, u):
                n = 2 * i + u
                inverse(dve, sd[u], rs[u], sd_ready, rs_ready, n)
                dve.wait_ge(turned, n + 1)
                normalise(dve, xn[u], of_group(z, m.x, n), mv[u], rs[u]).then_inc(xn_ready, 1)

            def sum_squares(i, u, pair):
                n = 2 * i + u
                for t in (2 * pair, 2 * pair + 1):
                    dve.wait_ge(sq_ready, G * n + t + 1)
                    dve.tensor_reduce(var[u][:, t, :], sq[t % 2][:, :].rearrange("p (h f) -> p h f", f=z.DK), AX.X,
                                      ALU.add).then_inc(var_ready, 1)

            def scale_heads(i, u):
                n = 2 * i + u
                dve.wait_ge(hsd_ready, n + 1)
                dve.reciprocal(hrs[u][:, :, :], hsd[u][:, :, :]).then_inc(hrs_ready, 1)
                dve.wait_ge(hrs_ready, n + 1)
                for t in range(G):
                    view = qk[u][:, t, :].rearrange("p (n d h) -> p n d h", d=z.DK, h=z.HPU)
                    inverses = hrs[u][:, t, :].rearrange("p (n h) -> p n h", h=z.HPU).unsqueeze(2)
                    last = dve.tensor_tensor(view, view, inverses.to_broadcast([P, H2 // z.HPU, z.DK, z.HPU]), ALU.mult)
                last.then_inc(qn_ready, 1)

            def split(i, u):
                n = 2 * i + u
                dve.wait_ge(feat_ready, 4 * n + 6)
                dve.wait_ge(stored[u], STORED * i + STORED)
                dve.tensor_copy(parts[u][:, 0, :, :], feat[u][:, :, :]).then_inc(high_done, 1)
                dve.wait_ge(high_done, n + 1)
                dve.wait_ge(low_done, n + 1)
                dve.tensor_tensor(rest[:, :, :], feat[u][:, :, :], parts[u][:, 0, :, :], ALU.subtract).then_inc(rest_done, 1)
                dve.wait_ge(rest_done, n + 3)
                dve.tensor_copy(parts[u][:, 1, :, :], rest[:, :, :]).then_inc(mid_done, 1)

            lagged(dve, GROUPS, (0, measure), (1, lambda i, u: sum_squares(i, u, 0)), (0, norm),
                   (1, lambda i, u: sum_squares(i, u, 1)), (2, split), (1, scale_heads))

        @block.gpsimd
        def _(pool):
            pool.sem_inc(low_done, 1)
            with pool.Fori(0, GROUPS // 2) as i:
                for u in range(2):
                    n = 2 * i + u
                    wait_alone(pool, mid_done, n + 1, m.alone)
                    pool.tensor_tensor(parts[u][:, 2, :, :], rest[:, :, :], parts[u][:, 1, :, :], ALU.subtract
                                       ).then_inc(low_done, 1)

        @block.scalar
        def _(act):
            act.sem_inc(xt_ready, 1)
            act.sem_inc(qk_taken, 2)
            act.sem_inc(feat_ready, 2)
            act.sem_inc(vx_ready, 1)

            def root(i, u):
                deviation(act, mv[u], sd[u], m.eps, mv_ready, sd_ready, 2 * i + u)

            def take_turned(i, u):
                n = 2 * i + u
                act.wait_ge(turned, n + 3)
                act.wait_ge(v_ready, 2 * n + 2)
                for c in range(DC):
                    last = act.activation(xt[u][:, c, :], m.bank[T0 + c], ACT.Copy)
                last.then_inc(xt_ready, 1)

            def take_heads(i, u, pair):
                n = 2 * i + u
                act.wait_ge(ft_ready, 4 * n + 4)
                for t in (2 * pair, 2 * pair + 1):
                    act.wait_ge(qk_ready, G * n + t + 1)
                    act.wait_ge(var_ready, G * n + t + 1)
                    act.activation(sq[t % 2][:, :], m.bank[Q0 + t % 2], ACT.Square).then_inc(sq_ready, 1)
                    act.activation(qk[u][:, t, :].rearrange("p (n d h) -> p n h d", d=z.DK, h=z.HPU),
                                   m.bank[Q0 + t % 2].rearrange("p (n h d) -> p n h d", d=z.DK, h=z.HPU), ACT.Copy
                                   ).then_inc(qk_taken, 1)
                    if t % 2:
                        act.wait_ge(ones_ready, 1)
                        act.wait_ge(v_stored[u], V_STORED * i + V_STORED)
                        act.wait_ge(v_ready, 2 * n + t // 2 + 5)
                        act.activation(vx[u][:, t - 1:t + 1, :, 0:16],
                                       m.bank[VB].rearrange("p (t h d) -> p t h d", t=2, d=16), ACT.Copy
                                       ).then_inc(vx_ready, 1)

            def root_of_heads(i, u):
                n = 2 * i + u
                act.wait_ge(var_ready, G * n + G + 2)
                act.activation(hsd[u][:, :, :], var[u][:, :, :], ACT.Sqrt, bias=m.eps[:, 0:1], scale=1.0 / z.DK
                               ).then_inc(hsd_ready, 1)

            def take_features(i, u):
                n = 2 * i + u
                act.wait_ge(rest_done, n + 1)
                for j in range(4):
                    act.wait_ge(ft_ready, 4 * n + j + 9)
                    act.activation(feat[u][:, j, :], m.bank[F0 + j % 2], ACT.Identity, bias=m.beta_col[:, 0:1],
                                   scale=m.gamma_col[:, 0:1]).then_inc(feat_ready, 1)

            lagged(act, GROUPS, (2, take_features), (1, lambda i, u: take_heads(i, u, 0)), (0, root),
                   (1, lambda i, u: take_heads(i, u, 1)), (1, root_of_heads), (0, take_turned))

        @block.tensor
        def _(pe):
            pe.sem_inc(turned, 2)
            pe.sem_inc(v_ready, 4)
            pe.sem_inc(ft_ready, 8)

            def turn(i, u):
                n = 2 * i + u
                pe.wait_ge(xn_ready, n + 1)
                pe.wait_ge(xt_ready, n + 1)
                turn_group(pe, z, m.bank[T0:T0 + DC], xn[u], m.ident).then_inc(turned, 1)

            def project(i, u):
                n = 2 * i + u
                pe.wait_ge(xt_ready, n + 2)
                for t in range(G):
                    pe.wait_ge(qk_taken, G * n + t + 1)
                    for c in range(DC):
                        last = pe.matmul(m.bank[Q0 + t % 2], xt[u][:, c, t * P:(t + 1) * P], m.w_qkv[:, c, 0:W],
                                         start=(c == 0), stop=(c == DC - 1))
                    last.then_inc(qk_ready, 1)
                    if t % 2:
                        pe.wait_ge(vx_ready, 2 * n + t // 2 + 1)
                        for k, tile in enumerate((t - 1, t)):
                            for c in range(DC):
                                last = pe.matmul(m.bank[VB][:, k * z.D:(k + 1) * z.D], xt[u][:, c, tile * P:(tile + 1) * P],
                                                 m.w_qkv[:, c, W:W + z.D], start=(c == 0), stop=(c == DC - 1))
                        last.then_inc(v_ready, 1)

            def turn_features(i, u):
                n = 2 * i + u
                pe.wait_ge(qn_ready, n + 1)
                for j in range(4):
                    pe.wait_ge(feat_ready, 4 * n + j + 1)
                    for t in range(G):
                        last = pe.transpose(m.bank[F0 + j % 2][:, t * P:(t + 1) * P], qk[u][:, t, j * P:(j + 1) * P],
                                            m.ident[:, :])
                    last.then_inc(ft_ready, 1)

            lagged(pe, GROUPS, (2, turn_features), (1, project), (0, turn))



def ternary_pass(nc, z, m, normed, out):
    G, DC, GROUPS = z.G, z.DC, z.TILES // z.G
    QB, EPS = 128.0, 1e-5
    og = out.rearrange("b s d -> (b s) d").rearrange("(n p) d -> p n d", p=P)
    with ExitStack() as ctx:
        def sb(name, shape, dt=F32):
            return [ctx.enter_context(nc.sbuf_tensor(f"t_{name}{u}", shape, dt)) for u in range(2)]

        raw, mv, sd, rs = sb("raw", [P, G, 6]), sb("mv", [P, G, 2]), sb("sd", [P, G]), sb("rs", [P, G])
        offset_ready, = sems(nc, "t_offset_ready")
        offset, grs, xt, zt = sb("offset", [P, G]), sb("grs", [P, G]), sb("xt", [P, DC, z.GT]), sb("zt", [P, G, z.D])
        large = sb("large", [P, G, z.D])
        one = lambda name: ctx.enter_context(nc.sbuf_tensor("t_" + name, [P, 1], F32))
        peak, gamma, inv, factor, gain, gain2 = (one(x) for x in ("peak", "gamma", "inv", "factor", "gain", "gain2"))
        stored = sems(nc, "t_stored0", "t_stored1")
        (peak_ready, gamma_ready, setup, enlarged, turned, xt_ready, y_ready, raw_done, mv_ready, sd_ready, rs_ready,
         grs_ready, zt_ready, added) = sems(nc, *["t_" + x for x in (
             "peak_ready", "gamma_ready", "setup", "enlarged", "turned", "xt_ready", "y_ready", "raw_done", "mv_ready",
             "sd_ready", "rs_ready", "grs_ready", "zt_ready", "added")])
        block = ctx.enter_context(nc.Block())
        T0 = 0
        SETUP = 6

        def banks(u):
            return [m.psum[:, 4 + 2 * u + t // 2, (t % 2) * z.D:(t % 2 + 1) * z.D] for t in range(G)]

        @block.sync
        def _(sp):
            with sp.Fori(0, GROUPS // 2) as i:
                for u in range(2):
                    n = 2 * i + u
                    sp.wait_ge(added, n + 3)
                    sp.dma_start(og[:, bass.ts(n, G), :], m.x[:, bass.ts(n, G), :]).then_inc(stored[u], 16)
            for u in range(2):
                sp.wait_ge(stored[u], 16 * (GROUPS // 2))

        @block.vector
        def _(dve):
            count = [0]

            def did(ins):
                count[0] += 1
                ins.then_inc(setup, 1)
                dve.wait_ge(setup, count[0])

            dve.tensor_reduce(peak[:, :], m.peaks[:, :], AX.X, ALU.max).then_inc(peak_ready, 1)
            dve.wait_ge(gamma_ready, 1)
            did(dve.reciprocal(inv[:, :], gamma[:, :]))
            did(dve.tensor_scalar(factor[:, :], inv[:, :], QB, None, ALU.mult))
            did(dve.tensor_scalar(gain[:, :], gamma[:, :], m.w_mean[:, 0:1], None, ALU.mult))
            did(dve.tensor_scalar(gain[:, :], gain[:, :], 1.0 / QB, None, ALU.mult))
            did(dve.tensor_tensor(gain2[:, :], gain[:, :], gain[:, :], ALU.mult))
            dve.sem_inc(setup, 1)
            dve.sem_inc(xt_ready, 2)
            dve.sem_inc(zt_ready, 2)

            def clip(i, u):
                n = 2 * i + u
                dve.wait_ge(turned, n + 3)
                dve.wait_ge(y_ready, n + 1)
                for c in range(DC):
                    last = dve.tensor_scalar(xt[u][:, c, :], m.bank[T0 + 2 * u + c], EPS - QB, QB - EPS, ALU.max, ALU.min)
                last.then_inc(xt_ready, 1)

            def norm(i, u):
                measure_sums(m, dve, banks(u), raw[u], mv[u], sd[u], rs[u], offset[u], y_ready, raw_done, mv_ready,
                             sd_ready, rs_ready, zt_ready, offset_ready, 2 * i + u,
                             gain=(gain[:, 0:1], grs[u], grs_ready))

            staggered(dve, GROUPS, clip, norm)

        @block.gpsimd
        def _(pool):
            pool.wait_ge(peak_ready, 1)
            pool.partition_all_reduce(gamma[:, :], peak[:, :], P, bass.bass_isa.ReduceOp.max).then_inc(gamma_ready, 1)
            add_to_x(pool, z, m, zt, zt_ready, added, GROUPS)

        @block.scalar
        def _(act):
            act.wait_ge(setup, SETUP)

            def root(i, u):
                deviation(act, mv[u], sd[u], m.eps, mv_ready, sd_ready, 2 * i + u, scale=gain2[:, 0:1])

            def enlarge(i, u):
                n = 2 * i + u
                act.wait_ge(turned, n + 1)
                act.activation(large[u][:, :, :], normed[:, bass.ts(n, G), :], ACT.Copy, scale=factor[:, 0:1]
                               ).then_inc(enlarged, 1)

            def sums(i, u):
                normalise_sums(act, banks(u), grs[u], offset[u], zt[u], offset_ready, added, zt_ready, 2 * i + u)

            lagged(act, GROUPS, (2, root), (0, enlarge), (2, sums))

        @block.tensor
        def _(pe):
            pe.sem_inc(y_ready, 2)
            pe.sem_inc(turned, 2)

            def turn(i, u):
                n = 2 * i + u
                pe.wait_ge(enlarged, n + 1)
                pe.wait_ge(xt_ready, n + 1)
                for c in range(DC):
                    for t in range(G):
                        src = large[u][:, t, c * P:(c + 1) * P]
                        last = pe.transpose(m.bank[T0 + 2 * u + c][:, t * P:(t + 1) * P], src, m.ident[:, :])
                last.then_inc(turned, 1)

            def project(i, u):
                n = 2 * i + u
                pe.wait_ge(xt_ready, n + 3)
                pe.wait_ge(zt_ready, n + 1)
                for t, bank in enumerate(banks(u)):
                    for c in range(DC):
                        last = pe.matmul(bank, xt[u][:, c, t * P:(t + 1) * P], m.w_ter[:, c, :], start=(c == 0),
                                         stop=(c == DC - 1))
                last.then_inc(y_ready, 1)

            staggered(pe, GROUPS, turn, project, behind_first=True)


_INS = ['L0_attn_x', 'L0_attn_W_dq', 'L0_attn_W_uq', 'L0_attn_W_dkv', 'L0_attn_W_uk', 'L0_attn_W_uv', 'L0_attn_W_o',
        'L0_ffn_fast_b', 'L0_ffn_w_fc', 'L0_ffn_w_proj', 'L0_ffn_u', 'L0_ffn_v', 'L0_ffn_gate', 'L1_attn_Wq',
        'L1_attn_Wk', 'L1_attn_Wv', 'L1_attn_Wo', 'L1_attn_gamma', 'L1_attn_beta', 'L1_ffn_weight',
        'L1_ffn_ln_gamma', 'L1_ffn_ln_beta']


def kernel(**inputs):
    import numpy as _np
    import concourse.bacc as _bacc
    from concourse.bass_utils import run_bass_kernel_spmd as _run

    nc = _bacc.Bacc("TRN2", target_bir_lowering=False, num_devices=1)
    arrays, aps = {}, {}
    for name in _INS:
        a = _np.ascontiguousarray(inputs[name]).reshape(_np.shape(inputs[name]) or (1,))
        arrays[f"in_{name}"] = a
        aps[name] = nc.dram_tensor(f"in_{name}", a.shape, mybir.dt.from_np(a.dtype), kind="ExternalInput").ap()
    out = nc.dram_tensor("out_0", arrays["in_L0_attn_x"].shape, F32, kind="ExternalOutput").ap()
    build(nc, aps, out)
    r = _run(nc, [arrays], core_ids=[0])
    return r.results[0]["out_0"]
```
